# Optimizing a Trainium2 kernel written in Bass

```python
import numpy as np
import jax
import jax.numpy as jnp

def _softmax(x, axis=-1):
    return jax.nn.softmax(x, axis=axis)

def _gelu(x):
    return jax.nn.gelu(x, approximate=True)

def _silu(x):
    return jax.nn.silu(x)

def _sigmoid(x):
    return jax.nn.sigmoid(x)

def _layernorm(x, axis=-1, eps=1e-05):
    m = jnp.mean(x, axis=axis, keepdims=True)
    v = jnp.var(x, axis=axis, keepdims=True)
    return (x - m) / jnp.sqrt(v + eps)

def _scatter_add(tgt, idx, src, axis=0):
    return tgt.at[idx].add(src)

def _segment_sum(src, seg, n):
    return jax.ops.segment_sum(src, seg, n)
kernel_name = 'mk_seq_postln_d2_jaxref_r8_eac718'

def setup_inputs(seed: int=0):
    np.random.seed(seed)
    _w = jnp.asarray

    def _L0_attn_setup():
        import jax, jax.numpy as jnp
        import numpy as np
        HIDDEN = 512
        NUM_HEADS = 32
        HEAD_DIM = HIDDEN // NUM_HEADS

        def _fp8_roundtrip(x):
            return x.astype(jnp.float8_e4m3fn).astype(jnp.float32)
        key = jax.random.key(seed)
        ks = jax.random.split(key, 10)
        B, S = (2, 512)
        hidden_states = jax.random.normal(ks[0], (B, S, HIDDEN), dtype=jnp.float32)
        scale = 0.02

        def lin(kw, kb):
            w = jax.random.normal(kw, (HIDDEN, HIDDEN), dtype=jnp.float32) * scale
            b = jax.random.normal(kb, (HIDDEN,), dtype=jnp.float32) * scale
            return (w, b)
        wq, bq = lin(ks[1], ks[2])
        wk, bk = lin(ks[3], ks[4])
        wv, bv = lin(ks[5], ks[6])
        wl, bl = lin(ks[7], ks[8])
        wq, bq = (_fp8_roundtrip(wq), _fp8_roundtrip(bq))
        wk, bk = (_fp8_roundtrip(wk), _fp8_roundtrip(bk))
        wv, bv = (_fp8_roundtrip(wv), _fp8_roundtrip(bv))
        return {'hidden_states': hidden_states, 'wq': wq, 'bq': bq, 'wk': wk, 'bk': bk, 'wv': wv, 'bv': bv, 'wl': wl, 'bl': bl}
    _L0_attn_in = _L0_attn_setup()

    def _L0_ffn_setup():
        import jax, jax.numpy as jnp
        import numpy as np
        import math
        D = 512
        TOKENS = (4, 256)
        P = 0.8

        def conn_dense(kernel, x):
            w = jnp.where(kernel, jnp.asarray(1.0, x.dtype), jnp.asarray(-1.0, x.dtype))
            return x @ w

        def ei_dense(x, kernel, scale, p):
            in_dim = x.shape[-1]
            ne = round(in_dim * p)
            x_exc = x[..., :ne]
            x_inh = x[..., ne:]
            xx = jnp.concatenate([x_exc, -p / (1.0 - p) * x_inh], axis=-1)
            return scale * conn_dense(kernel, xx)
        key = jax.random.key(seed)
        ks = jax.random.split(key, 4)
        x = jax.random.normal(ks[0], (*TOKENS, D), dtype=jnp.float32)
        k0 = jax.random.bernoulli(ks[1], 0.5, (D, D))
        k1 = jax.random.bernoulli(ks[2], 0.5, (D, D))
        k2 = jax.random.bernoulli(ks[3], 0.5, (D, D))
        s = jnp.asarray(1.0 / math.sqrt(D), dtype=jnp.float32)
        return {'x': x, 'k0': k0, 's0': s, 'k1': k1, 's1': s, 'k2': k2, 's2': s}
    _L0_ffn_in = _L0_ffn_setup()

    def _L1_attn_setup():
        import jax, jax.numpy as jnp
        import numpy as np
        D_MODEL = 512
        NUM_HEADS = 32
        NUM_KV_HEADS = 8
        HEAD_DIM = D_MODEL // NUM_HEADS
        GROUP = NUM_HEADS // NUM_KV_HEADS
        WINDOW = 128
        BATCH, SEQ = (1, 256)

        def rotate_half(x):
            x1, x2 = jnp.split(x, 2, axis=-1)
            return jnp.concatenate((-x2, x1), axis=-1)

        def build_rotary(seq_len, dim):
            inv_freq = 1.0 / 10000.0 ** (jnp.arange(0, dim, 2, dtype=jnp.float32) / dim)
            t = jnp.arange(seq_len, dtype=jnp.float32)
            freqs = jnp.einsum('i,j->ij', t, inv_freq)
            emb = jnp.concatenate((freqs, freqs), axis=-1)
            return (jnp.cos(emb)[None, None], jnp.sin(emb)[None, None])

        def _split_kv(t, B, S):
            t = t.reshape(B, S, NUM_KV_HEADS, GROUP * HEAD_DIM).transpose(0, 2, 1, 3)
            t = t.reshape(B, NUM_KV_HEADS, S, GROUP, HEAD_DIM).transpose(0, 1, 3, 2, 4)
            return t.reshape(B, NUM_HEADS, S, HEAD_DIM)
        key = jax.random.key(seed)
        ks = jax.random.split(key, 5)
        s = 1.0 / np.sqrt(D_MODEL)
        return {'x': jax.random.normal(ks[0], (BATCH, SEQ, D_MODEL), dtype=jnp.float32), 'Wq': jax.random.normal(ks[1], (D_MODEL, D_MODEL), dtype=jnp.float32) * s, 'Wk': jax.random.normal(ks[2], (D_MODEL, D_MODEL), dtype=jnp.float32) * s, 'Wv': jax.random.normal(ks[3], (D_MODEL, D_MODEL), dtype=jnp.float32) * s, 'Wo': jax.random.normal(ks[4], (D_MODEL, D_MODEL), dtype=jnp.float32) * s}
    _L1_attn_in = _L1_attn_setup()

    def _L1_ffn_setup():
        import jax, jax.numpy as jnp
        import numpy as np
        HIDDEN = 512
        MOE_INTER = 128
        SHARED_INTER = 512
        NUM_EXPERTS = 16
        TOP_K = 2

        def _moe_forward(x, gate_w, w_gate_up, w_down, shared_w_gate_up, shared_w_down):
            orig_shape = x.shape
            x2 = x.reshape(-1, orig_shape[-1])
            gu_s = x2 @ shared_w_gate_up.T
            g_s, u_s = jnp.split(gu_s, 2, axis=-1)
            shared_out = jax.nn.silu(g_s) * u_s @ shared_w_down.T
            logits = x2 @ gate_w.T
            probs = jax.nn.softmax(logits, axis=-1)
            topk_vals, topk_idx = jax.lax.top_k(probs, TOP_K)
            topk_vals = topk_vals / jnp.sum(topk_vals, axis=-1, keepdims=True)
            combine = jnp.sum(jax.nn.one_hot(topk_idx, NUM_EXPERTS, dtype=x2.dtype) * topk_vals[..., None], axis=1)
            gu = jnp.einsum('th,eih->eti', x2, w_gate_up)
            g, u = jnp.split(gu, 2, axis=-1)
            act = jax.nn.silu(g) * u
            out_e = jnp.einsum('eti,ehi->eth', act, w_down)
            moe_out = jnp.einsum('eth,te->th', out_e, combine)
            return (moe_out + shared_out).reshape(orig_shape)
        key = jax.random.key(seed)
        ks = jax.random.split(key, 6)
        s = 0.02
        hidden_states = jax.random.normal(ks[0], (2, 256, HIDDEN), dtype=jnp.float32)
        gate_w = jax.random.normal(ks[1], (NUM_EXPERTS, HIDDEN), dtype=jnp.float32) * s
        w_gate_up = jax.random.normal(ks[2], (NUM_EXPERTS, 2 * MOE_INTER, HIDDEN), dtype=jnp.float32) * s
        w_down = jax.random.normal(ks[3], (NUM_EXPERTS, HIDDEN, MOE_INTER), dtype=jnp.float32) * s
        shared_w_gate_up = jax.random.normal(ks[4], (2 * SHARED_INTER, HIDDEN), dtype=jnp.float32) * s
        shared_w_down = jax.random.normal(ks[5], (HIDDEN, SHARED_INTER), dtype=jnp.float32) * s
        return {'hidden_states': hidden_states, 'gate_w': gate_w, 'w_gate_up': w_gate_up, 'w_down': w_down, 'shared_w_gate_up': shared_w_gate_up, 'shared_w_down': shared_w_down}
    _L1_ffn_in = _L1_ffn_setup()
    _d = {'L0_attn_hidden_states': _L0_attn_in['hidden_states'], 'L0_attn_wq': _L0_attn_in['wq'], 'L0_attn_bq': _L0_attn_in['bq'], 'L0_attn_wk': _L0_attn_in['wk'], 'L0_attn_bk': _L0_attn_in['bk'], 'L0_attn_wv': _L0_attn_in['wv'], 'L0_attn_bv': _L0_attn_in['bv'], 'L0_attn_wl': _L0_attn_in['wl'], 'L0_attn_bl': _L0_attn_in['bl'], 'L0_ffn_k0': _L0_ffn_in['k0'], 'L0_ffn_s0': _L0_ffn_in['s0'], 'L0_ffn_k1': _L0_ffn_in['k1'], 'L0_ffn_s1': _L0_ffn_in['s1'], 'L0_ffn_k2': _L0_ffn_in['k2'], 'L0_ffn_s2': _L0_ffn_in['s2'], 'L1_attn_Wq': _L1_attn_in['Wq'], 'L1_attn_Wk': _L1_attn_in['Wk'], 'L1_attn_Wv': _L1_attn_in['Wv'], 'L1_attn_Wo': _L1_attn_in['Wo'], 'L1_ffn_gate_w': _L1_ffn_in['gate_w'], 'L1_ffn_w_gate_up': _L1_ffn_in['w_gate_up'], 'L1_ffn_w_down': _L1_ffn_in['w_down'], 'L1_ffn_shared_w_gate_up': _L1_ffn_in['shared_w_gate_up'], 'L1_ffn_shared_w_down': _L1_ffn_in['shared_w_down']}
    _x0 = _d['L0_attn_hidden_states']
    _d['L0_attn_hidden_states'] = jax.random.normal(jax.random.fold_in(jax.random.key(seed), 1), (1, 1024, 512), dtype=_x0.dtype)
    del _x0
    return _d

def reference(L0_attn_hidden_states, L0_attn_wq, L0_attn_bq, L0_attn_wk, L0_attn_bk, L0_attn_wv, L0_attn_bv, L0_attn_wl, L0_attn_bl, L0_ffn_k0, L0_ffn_s0, L0_ffn_k1, L0_ffn_s1, L0_ffn_k2, L0_ffn_s2, L1_attn_Wq, L1_attn_Wk, L1_attn_Wv, L1_attn_Wo, L1_ffn_gate_w, L1_ffn_w_gate_up, L1_ffn_w_down, L1_ffn_shared_w_gate_up, L1_ffn_shared_w_down):

    def _L0_attn_ref(hidden_states, wq, bq, wk, bk, wv, bv, wl, bl):
        import jax, jax.numpy as jnp
        import numpy as np
        HIDDEN = 512
        NUM_HEADS = 32
        HEAD_DIM = HIDDEN // NUM_HEADS

        def _fp8_roundtrip(x):
            return x.astype(jnp.float8_e4m3fn).astype(jnp.float32)
        B, S, E = hidden_states.shape
        H, D = (NUM_HEADS, HEAD_DIM)
        q = (hidden_states @ wq.T + bq).reshape(B, S, H, D)
        k = (hidden_states @ wk.T + bk).reshape(B, S, H, D)
        v = (hidden_states @ wv.T + bv).reshape(B, S, H, D)
        latent = hidden_states @ wl.T + bl
        scores = jnp.einsum('bshd,bstd->bsht', q, k) / np.sqrt(D).astype(np.float32)
        probs = jax.nn.softmax(scores, axis=-1)
        context = jnp.einsum('bsht,bstd->bshd', probs, v).reshape(B, S, E)
        return context

    def _L0_ffn_ref(x, k0, s0, k1, s1, k2, s2):
        import jax, jax.numpy as jnp
        import numpy as np
        import math
        D = 512
        TOKENS = (4, 256)
        P = 0.8

        def conn_dense(kernel, x):
            w = jnp.where(kernel, jnp.asarray(1.0, x.dtype), jnp.asarray(-1.0, x.dtype))
            return x @ w

        def ei_dense(x, kernel, scale, p):
            in_dim = x.shape[-1]
            ne = round(in_dim * p)
            x_exc = x[..., :ne]
            x_inh = x[..., ne:]
            xx = jnp.concatenate([x_exc, -p / (1.0 - p) * x_inh], axis=-1)
            return scale * conn_dense(kernel, xx)
        h = s0 * conn_dense(k0, x)
        h = jax.nn.relu(h) * 2.0
        h = ei_dense(h, k1, s1, P)
        h = jax.nn.relu(h) * 2.0
        return ei_dense(h, k2, s2, P)

    def _L1_attn_ref(x, Wq, Wk, Wv, Wo):
        import jax, jax.numpy as jnp
        import numpy as np
        D_MODEL = 512
        NUM_HEADS = 32
        NUM_KV_HEADS = 8
        HEAD_DIM = D_MODEL // NUM_HEADS
        GROUP = NUM_HEADS // NUM_KV_HEADS
        WINDOW = 128
        BATCH, SEQ = (1, 256)

        def rotate_half(x):
            x1, x2 = jnp.split(x, 2, axis=-1)
            return jnp.concatenate((-x2, x1), axis=-1)

        def build_rotary(seq_len, dim):
            inv_freq = 1.0 / 10000.0 ** (jnp.arange(0, dim, 2, dtype=jnp.float32) / dim)
            t = jnp.arange(seq_len, dtype=jnp.float32)
            freqs = jnp.einsum('i,j->ij', t, inv_freq)
            emb = jnp.concatenate((freqs, freqs), axis=-1)
            return (jnp.cos(emb)[None, None], jnp.sin(emb)[None, None])

        def _split_kv(t, B, S):
            t = t.reshape(B, S, NUM_KV_HEADS, GROUP * HEAD_DIM).transpose(0, 2, 1, 3)
            t = t.reshape(B, NUM_KV_HEADS, S, GROUP, HEAD_DIM).transpose(0, 1, 3, 2, 4)
            return t.reshape(B, NUM_HEADS, S, HEAD_DIM)
        B, S, _ = x.shape
        q = (x @ Wq.T).reshape(B, S, NUM_HEADS, HEAD_DIM).transpose(0, 2, 1, 3)
        k = _split_kv(x @ Wk.T, B, S)
        v = _split_kv(x @ Wv.T, B, S)
        cos, sin = build_rotary(S, HEAD_DIM)
        q = q * cos + rotate_half(q) * sin
        k = k * cos + rotate_half(k) * sin
        scores = jnp.einsum('bhqd,bhkd->bhqk', q, k) / jnp.sqrt(jnp.float32(HEAD_DIM))
        i = jnp.arange(S)[:, None]
        j = jnp.arange(S)[None, :]
        allowed = (j <= i) & (j > i - WINDOW)
        scores = jnp.where(allowed[None, None], scores, -jnp.inf)
        attn = jax.nn.softmax(scores, axis=-1)
        out = jnp.einsum('bhqk,bhkd->bhqd', attn, v)
        out = out.transpose(0, 2, 1, 3).reshape(B, S, D_MODEL)
        return out @ Wo.T

    def _L1_ffn_ref(hidden_states, gate_w, w_gate_up, w_down, shared_w_gate_up, shared_w_down):
        import jax, jax.numpy as jnp
        import numpy as np
        HIDDEN = 512
        MOE_INTER = 128
        SHARED_INTER = 512
        NUM_EXPERTS = 16
        TOP_K = 2

        def _moe_forward(x, gate_w, w_gate_up, w_down, shared_w_gate_up, shared_w_down):
            orig_shape = x.shape
            x2 = x.reshape(-1, orig_shape[-1])
            gu_s = x2 @ shared_w_gate_up.T
            g_s, u_s = jnp.split(gu_s, 2, axis=-1)
            shared_out = jax.nn.silu(g_s) * u_s @ shared_w_down.T
            logits = x2 @ gate_w.T
            probs = jax.nn.softmax(logits, axis=-1)
            topk_vals, topk_idx = jax.lax.top_k(probs, TOP_K)
            topk_vals = topk_vals / jnp.sum(topk_vals, axis=-1, keepdims=True)
            combine = jnp.sum(jax.nn.one_hot(topk_idx, NUM_EXPERTS, dtype=x2.dtype) * topk_vals[..., None], axis=1)
            gu = jnp.einsum('th,eih->eti', x2, w_gate_up)
            g, u = jnp.split(gu, 2, axis=-1)
            act = jax.nn.silu(g) * u
            out_e = jnp.einsum('eti,ehi->eth', act, w_down)
            moe_out = jnp.einsum('eth,te->th', out_e, combine)
            return (moe_out + shared_out).reshape(orig_shape)
        return _moe_forward(hidden_states, gate_w, w_gate_up, w_down, shared_w_gate_up, shared_w_down)
    x = L0_attn_hidden_states
    x = _layernorm(x + _L0_attn_ref(x, L0_attn_wq, L0_attn_bq, L0_attn_wk, L0_attn_bk, L0_attn_wv, L0_attn_bv, L0_attn_wl, L0_attn_bl), axis=-1)
    x = _layernorm(x + _L0_ffn_ref(x, L0_ffn_k0, L0_ffn_s0, L0_ffn_k1, L0_ffn_s1, L0_ffn_k2, L0_ffn_s2), axis=-1)
    x = _layernorm(x + _L1_attn_ref(x, L1_attn_Wq, L1_attn_Wk, L1_attn_Wv, L1_attn_Wo), axis=-1)
    x = _layernorm(x + _L1_ffn_ref(x, L1_ffn_gate_w, L1_ffn_w_gate_up, L1_ffn_w_down, L1_ffn_shared_w_gate_up, L1_ffn_shared_w_down), axis=-1)
    return x

_drawn_inputs = setup_inputs


def setup_inputs(seed=0):
    import zlib

    import numpy as np

    out = dict(_drawn_inputs(seed))
    spreads = {}
    factors = {'L0_attn_wq': 3.804,
     'L0_attn_bq': 8.0,
     'L0_attn_wk': 3.43,
     'L0_attn_bk': 8.0,
     'L0_attn_bv': 8.0,
     'L1_ffn_gate_w': 3.512,
     'L1_ffn_w_gate_up': 3.294,
     'L1_ffn_w_down': 3.28}
    for name, (base, spread) in spreads.items():
        noise = np.random.default_rng([zlib.crc32(name.encode()), seed]).standard_normal(out[name].shape)
        drawn = base * np.exp(spread * noise) if base else spread * noise
        out[name] = jnp.asarray(drawn.astype(out[name].dtype))
    for name, factor in factors.items():
        out[name] = (out[name] * factor).astype(out[name].dtype)
    return out
```

```python
from contextlib import ExitStack

import concourse.bass as bass
from concourse import mybir

F32 = mybir.dt.float32
F32R = mybir.dt.float32r
BF16 = mybir.dt.bfloat16
U8 = mybir.dt.uint8
ALU = mybir.AluOpType
ACT = mybir.ActivationFunctionType
AX = mybir.AxisListType.X

P = 128
D = 512
DC = D // P
T = 1024 // P
G = 4
H = 32
HD = D // H
KS = 64
E = 16
SE = 4
NE = SE + E
EPS = 1e-5
SCALE = HD ** -0.5
CONSTS = 5 * 16
BIG = 1e30
CH = 16
NCH = P // CH
WCOLS = DC * 2 * P + D


class Ring:

    def __init__(self, banks, full, free):
        self.banks, self.full, self.free = banks, full, free
        self.number, self.taken = {}, 0

    def fill(self, pe, name):
        n = len(self.number)
        assert name not in self.number
        self.number[name] = n
        if n >= 2:
            pe.wait_ge(self.free, n - 1)
        return self.banks[n % 2]

    def take(self, engine, name):
        n = self.number[name]
        assert n == self.taken, (name, n, self.taken)
        self.taken += 1
        engine.wait_ge(self.full, n + 1)
        return self.banks[n % 2]

    def drained(self, engine, name):
        engine.wait_ge(self.free, self.number[name] + 1)


def build(nc, x, wq, wk, wv, bias, k0, k1, k2, s0, s1, s2, aq, ak, av, ao, gate, wgu, wd, sgu, sd,
          rope_c, factor_c, select_c, rank_c, out):
    with ExitStack() as ctx:
        def sb(name, shape, dt):
            return ctx.enter_context(nc.sbuf_tensor(name, shape, dt))

        def sem(name):
            return ctx.enter_context(nc.semaphore(name))

        banks = [ctx.enter_context(nc.psum_tensor(f"bank{i}", [P, 512], F32)) for i in range(8)]

        X = sb("X", [P, T, D], F32)
        W = sb("W", [P, 8, DC * D], F32R)
        XR = sb("XR", [P, 2 * DC * G * P], F32R)
        XT = XR[:, :].rearrange("p (a c n) -> p a c n", a=2, c=DC)
        RP = sb("RP", [P, 8192], F32R)
        FP = sb("FP", [P, 18432], F32)
        ident = sb("ident", [P, P], F32)
        identb = sb("identb", [P, P], BF16)
        maskb = sb("maskb", [P, 3 * P], BF16)
        rope = sb("rope", [P, T, 2, HD], F32)
        factor = sb("factor", [P, 2, DC], F32)
        scales = sb("scales", [P, 3], F32)
        ones = sb("ones", [1, P], F32R)
        kraw = sb("kraw", [P, DC, D], U8)
        epst = sb("epst", [P, 1], F32)
        st6 = sb("st6", [P, T, 6], F32)
        mv = sb("mv", [P, T, 2], F32)
        std = sb("std", [P, T], F32)
        rstd = sb("rstd", [P, T], F32)
        small = sb("small", [P, 4, CH], F32)
        hmax = sb("hmax", [P, H], F32)
        hsum = sb("hsum", [P, 2, G * G], F32)

        biasf = FP[0:1, 16384:17920].rearrange("p (n d) -> p n d", n=3)
        biasr = RP[0:1, 0:3072].rearrange("p (a n d) -> p a n d", a=2, n=3)
        qkrow = FP[:, 0:4096].rearrange("p (h t r) -> p h t r", h=H, t=G)
        vrow = FP[:, 4096:6144].rearrange("p (d t h) -> p d t h", d=HD, t=G)
        cx = FP[:, 4096:6144].rearrange("p (s d) -> p s d", d=HD)
        qT = FP[:, 6144:10240].rearrange("p (s h) -> p s h", h=H)
        kT = FP[:, 10240:14336].rearrange("p (s h) -> p s h", h=H)
        vT = FP[:, 14336:16384].rearrange("p (s d) -> p s d", d=HD)
        sc = FP[:, 16384:17408].rearrange("p (b s t) -> p b s t", b=2, t=H)
        pT = FP[:, 17408:18432].rearrange("p (b s t) -> p b s t", b=2, t=H)
        raw_a = [FP[:, 6144:8192], FP[:, 10240:12288], FP[:, 14336:16384]]
        h1 = RP[:, 0:4096].rearrange("p (a c n) -> p a c n", a=2, c=DC)
        h2 = XT
        K = [W[:, 6, :].rearrange("p (c n) -> p c n", c=DC), W[:, 7, :].rearrange("p (c n) -> p c n", c=DC),
             RP[:, 4096:6144].rearrange("p (c n) -> p c n", c=DC)]
        hf = FP[:, 16384:17408].rearrange("p (b n) -> p b n", b=2)
        raw_c = [FP[:, 0:2048], FP[:, 2048:4096], FP[:, 4096:6144], FP[:, 14336:16384]]
        qsp = FP[:, 0:4096].rearrange("p (b h r) -> p b h r", b=2, r=KS)
        ksp = FP[:, 4096:6144].rearrange("p (h r) -> p h r", r=KS)
        qf = FP[:, 6144:6656]
        kf = FP[:, 6656:7168]
        rt = FP[:, 7168:7680]
        vaug = FP[:, 7680:10752].rearrange("p (s h r) -> p s h r", s=3, r=32)
        PT = FP[:, 10752:12800].rearrange("p (b w h q) -> p b w h q", b=2, w=2, h=G)
        cT = FP[:, 12800:13824]
        co = FP[:, 13824:14336]
        XT2 = XR[:, 0:2048].rearrange("p (b a c n) -> p b a c n", b=2, a=2, c=DC)
        qS = XR[:, 2048:4096].rearrange("p (a q) -> p a q", q=P)
        qM = RP[:, 0:2048].rearrange("p (a q) -> p a q", q=P)
        kS = RP[:, 2048:8192].rearrange("p (a s k) -> p a s k", s=3, k=P)
        raw_e = [FP[:, b * WCOLS:(b + 1) * WCOLS] for b in range(3)]
        selr = FP[0:2 * E, 4608:4608 + E * P]
        sg = FP[:, 6656:7680].rearrange("p (b n) -> p b n", b=2)
        ac = FP[:, 7680:8192]
        gates = FP[:, 9216:9216 + DC * E]
        lg, l2, ex, oh1, oh2, tmp, cw = (FP[:, 9344 + 64 * n:9344 + 64 * (n + 1)].rearrange("p (t e) -> p t e", e=E)
                                         for n in range(7))
        cst = FP[:, 9856:9984].rearrange("p (t a e) -> p t a e", t=G, a=2)
        rank = FP[:, 10048:10048 + E]
        tiny = FP[:, 10112:10176].rearrange("p (a t) -> p a t", t=G)
        ah = RP[:, 0:2048].rearrange("p (b a n) -> p b a n", b=2, a=2)
        cTr = RP[0:2 * E, 2048:2560]
        selx = RP[0:2 * E, 2560:2560 + E * P].rearrange("p (e n) -> p e n", e=E)
        gr = RP[:, 4608:4608 + 2 * DC * E].rearrange("p (a c e) -> p a c e", a=2, c=DC)

        V = Ring(banks[0:2], sem("vbank_full"), sem("vbank_free"))
        A = Ring(banks[2:4], sem("abank_full"), sem("abank_free"))
        C = Ring(banks[4:6], sem("cbank_full"), sem("cbank_free"))
        S = Ring(banks[6:8], sem("sbank_full"), sem("sbank_free"))
        x_in = [sem(f"x_in{g}") for g in range(2)]
        wa_in = [sem(f"wa_in{n}") for n in range(3)]
        k_in = [sem(f"k_in{n}") for n in range(3)]
        wc_in = [sem(f"wc_in{n}") for n in range(4)]
        we_in = [sem(f"we_in{n}") for n in range(3)]
        consts_in = sem("consts_in")
        bias_in = sem("bias_in")
        gate_in = sem("gate_in")
        out_done = sem("out_done")
        w_high = sem("w_high")
        w_split = sem("w_split")
        k_ready = sem("k_ready")
        dve = sem("dve_step")
        act_step = sem("act_step")
        pool = sem("pool_step")
        small_ready = sem("small_ready")
        bias_ready = sem("bias_ready")
        ident_ready = sem("ident_ready")
        masks_ready = sem("masks_ready")
        pads_ready = sem("pads_ready")
        x_ready = sem("x_ready")
        stats_ready = sem("stats_ready")
        std_ready = sem("std_ready")
        expd = sem("expd")
        pt_ready = sem("pt_ready")
        h_ready = sem("h_ready")
        k_turned = sem("k_turned")
        q_turned = sem("q_turned")
        k_high = sem("k_high")
        q_high = sem("q_high")
        ksp_ready = sem("ksp_ready")
        qsp_ready = sem("qsp_ready")
        max_ready = sem("max_ready")
        pt_masked = sem("pt_masked")
        weighed = sem("weighed")
        ctx_ready = sem("ctx_ready")
        we_high = sem("we_high")
        we_split = sem("we_split")
        gate_ready = sem("gate_ready")
        logits_shifted = sem("logits_shifted")
        logits_exp = sem("logits_exp")
        cst_ready = sem("cst_ready")
        act_ready = sem("act_ready")
        down_done = sem("down_done")
        acc_done = sem("acc_done")

        def wsplit(n):
            return (W[:, 2 * n, :].rearrange("p (c n) -> p c n", c=DC), W[:, 2 * n + 1, :].rearrange("p (c n) -> p c n", c=DC))

        def window(i):
            cur, prev = i % 3, (i - 1) % 3
            if i == 0:
                return cur, 0
            if prev < cur:
                return slice(prev, cur + 1, cur - prev), P
            return slice(cur, prev + 1, prev - cur), 0

        def expert(n):
            k = 2 * (n % 3)
            return [(W[:, k + a, 0:DC * 2 * P].rearrange("p (c g n) -> p c g n", c=DC, g=2),
                     W[:, k + a, DC * 2 * P:WCOLS]) for a in range(2)]

        block = ctx.enter_context(nc.Block())

        @block.sync
        def _(sp):
            xin = x.rearrange("(g t p) n -> g p t n", g=2, p=P)
            sp.dma_start(X[:, 0:G, :], xin[0]).then_inc(x_in[0], 16)
            for n, w in enumerate((wq, wk, wv)):
                sp.dma_start(raw_a[n].rearrange("p (c n) -> p c n", c=DC), w.rearrange("(c p) n -> p c n", p=P)).then_inc(wa_in[n], 16)
            sp.dma_start(biasf, bias.rearrange("(a b) n -> a b n", a=1)).then_inc(bias_in, 16)
            sp.dma_start(rope[:, :, :, :], rope_c.rearrange("(t p) a d -> p t a d", p=P)).then_inc(consts_in, 16)
            sp.dma_start(factor[:, :, :], factor_c).then_inc(consts_in, 16)
            for n, s in enumerate((s0, s1, s2)):
                sp.dma_start(scales[:, n:n + 1], s.broadcast_to([P, 1])).then_inc(consts_in, 16)
            sp.dma_start(X[:, G:T, :], xin[1]).then_inc(x_in[1], 16)
            for n, k in enumerate((k0, k1, k2)):
                if n >= 1:
                    sp.wait_ge(k_ready, 1 + (n - 1) * DC)
                sp.dma_start(kraw[:, :, :], k.rearrange("(c p) n -> p c n", p=P)).then_inc(k_in[n], 16)
            sp.wait_ge(x_ready, T)
            for n, w in enumerate((aq, ak, av, ao)):
                sp.dma_start(raw_c[n].rearrange("p (c n) -> p c n", c=DC), w.rearrange("(c p) n -> p c n", p=P)).then_inc(wc_in[n], 16)
            sp.wait_ge(stats_ready, 5)
            sp.dma_start(gates.rearrange("p (c e) -> p c e", c=DC), gate.rearrange("(c p) e -> p c e", p=P)).then_inc(gate_in, 16)
            sp.dma_start(selr, select_c).then_inc(gate_in, 16)
            sp.dma_start(rank, rank_c).then_inc(gate_in, 16)
            for n in range(2 * NE):
                e = n % NE
                b = n % 3
                if n >= 3:
                    sp.wait_ge(we_split, n - 2)
                gu = raw_e[b][:, 0:DC * 2 * P].rearrange("p (c a n) -> p c a n", c=DC, a=2)
                dn = raw_e[b][:, DC * 2 * P:WCOLS]
                if e < SE:
                    src = sgu.rearrange("(c p) (a s n) -> p c a s n", p=P, a=2, s=SE)[:, :, :, e, :]
                    for a in range(2):
                        sp.dma_start(gu[:, :, a, :], src[:, :, a, :]).then_inc(we_in[b], 16)
                    sp.dma_start(dn, sd[e * P:(e + 1) * P, :]).then_inc(we_in[b], 16)
                else:
                    src = wgu[e - SE].rearrange("(c p) (a n) -> p c a n", p=P, a=2)
                    for a in range(2):
                        sp.dma_start(gu[:, :, a, :], src[:, :, a, :]).then_inc(we_in[b], 16)
                    sp.dma_start(dn, wd[e - SE]).then_inc(we_in[b], 16)
            for t in range(T):
                sp.wait_ge(x_ready, 3 * T + t + 1)
                sp.dma_start(out[t * P:(t + 1) * P, :], X[:, t, :]).then_inc(out_done, 16)
            sp.wait_ge(out_done, 16 * T)

        @block.tensor
        def _(pe):
            def product(bank, terms):
                for n, (lhs, rhs) in enumerate(terms):
                    mm = nc.tensor.matmul(bank, lhs, rhs, start=(n == 0), stop=(n == len(terms) - 1))
                return mm

            def split_terms(lhs, rhs):
                return [t for lh, ll, rh, rl in zip(*lhs, *rhs) for t in ((lh, rh), (lh, rl), (ll, rh))]

            def transpose_row(name, src):
                b = V.fill(pe, name)
                for c in range(DC):
                    mm = nc.tensor.transpose(b[:, c * P:(c + 1) * P], src[:, c * P:(c + 1) * P], ident[:, :])
                mm.then_inc(V.full, 1)

            def tokens(j):
                return [[XT[:, a, c, j * P:(j + 1) * P] for c in range(DC)] for a in range(2)]

            def tokens2(b):
                return [[XT2[:, b, a, c, :] for c in range(DC)] for a in range(2)]

            def chunks(w):
                return [[m[:, c, :] for c in range(DC)] for m in w]

            pe.wait_ge(ident_ready, 2)
            for g in range(2):
                pe.wait_ge(x_in[g], 16)
                for j in range(G):
                    transpose_row(("x", g * G + j), X[:, g * G + j, :])
                pe.wait_ge(bias_ready, 3)

                def project(n):
                    pe.wait_ge(w_split, n + 1)
                    for j in range(G):
                        V.drained(pe, ("x", g * G + j))
                        b = A.fill(pe, ("rows", g, n, j))
                        terms = [(ones[:, :], biasr[:, a, n, :]) for a in range(2)]
                        product(b[:, :], terms + split_terms(tokens(j), chunks(wsplit(n)))).then_inc(A.full, 1)

                def to_heads(ring, n, src, count):
                    A.drained(pe, ("rows", g, n, G - 1))
                    for a in range(count // 4):
                        b = ring.fill(pe, ("heads", g, n, a))
                        for m in range(4):
                            mm = nc.tensor.transpose(b[:, m * P:(m + 1) * P], src[:, 4 * a + m, :, :], ident[:, :])
                        mm.then_inc(ring.full, 1)

                project(0)
                project(2)
                to_heads(A, 0, qkrow, H)
                project(1)
                to_heads(V, 2, vrow, HD)
                to_heads(V, 1, qkrow, H)

                def scores(c):
                    b = C.fill(pe, ("scores", g, c))
                    for s in range(CH):
                        for j in range(G):
                            q = slice(32 * j, 32 * j + HD)
                            mm = nc.tensor.matmul(b[32 * j:32 * j + 32, s * H:(s + 1) * H], qT[q, c * CH + s, :],
                                                  kT[q, c * CH + s, :], start=True, stop=True)
                    mm.then_inc(C.full, 1)

                def values(c):
                    pe.wait_ge(pt_ready, g * NCH + c + 1)
                    b = S.fill(pe, ("values", g, c))
                    for s in range(CH):
                        for j in range(G):
                            q = slice(32 * j, 32 * j + 32)
                            mm = nc.tensor.matmul(b[q, s * HD:(s + 1) * HD], pT[q, c % 2, s, :],
                                                  vT[q, c * CH + s, :], start=True, stop=True)
                    mm.then_inc(S.full, 1)

                A.drained(pe, ("heads", g, 0, H // 4 - 1))
                V.drained(pe, ("heads", g, 1, H // 4 - 1))
                scores(0)
                for c in range(NCH):
                    if c + 1 < NCH:
                        scores(c + 1)
                    values(c)
                S.drained(pe, ("values", g, NCH - 1))
                for a in range(HD // 4):
                    b = V.fill(pe, ("context", g, a))
                    for m in range(4):
                        mm = nc.tensor.transpose(b[:, m * P:(m + 1) * P], cx[:, :, 4 * a + m], ident[:, :])
                    mm.then_inc(V.full, 1)

            for g in range(2):
                for j in range(G):
                    pe.wait_ge(x_ready, g * G + j + 1)
                    transpose_row(("x1", g * G + j), X[:, g * G + j, :])
                for layer, src in ((0, XT), (1, h1)):
                    pe.wait_ge(k_ready, 1 if layer == 0 else 1 + DC)
                    if layer == 0:
                        V.drained(pe, ("x1", g * G + G - 1))
                    else:
                        pe.wait_ge(h_ready, (2 * g + 1) * DC)
                    for o in range(DC):
                        b = A.fill(pe, ("hidden", g, layer, o))
                        product(b[:, :], [(K[layer][:, c, o * P:(o + 1) * P], src[:, a, c, :]) for c in range(DC) for a in range(2)])\
                            .then_inc(A.full, 1)
                pe.wait_ge(h_ready, (2 * g + 2) * DC)
                pe.wait_ge(k_ready, 1 + 2 * DC)
                for j in range(G):
                    b = V.fill(pe, ("ffn", g * G + j))
                    product(b[:, :], [(h2[:, a, c, j * P:(j + 1) * P], K[2][:, c, :]) for c in range(DC) for a in range(2)])\
                        .then_inc(V.full, 1)

            def stack(name, src):
                for a in range(4):
                    b = A.fill(pe, name + (a,))
                    for m in range(4):
                        pr = 2 * (4 * a + m)
                        mm = nc.tensor.transpose(b[:, m * P:(m + 1) * P], src[:, pr:pr + 2, :], ident[:, :])
                    mm.then_inc(A.full, 1)

            def half(hh):
                return slice(KS * hh, KS * hh + KS)

            def front(i):
                pe.wait_ge(x_ready, T + i + 1)
                transpose_row(("x2", i), X[:, i, :])
                V.drained(pe, ("x2", i))
                for n, ring in ((1, V), (0, V), (2, A)):
                    pe.wait_ge(w_split, 4 + n)
                    b = ring.fill(pe, ("qkv", i, n))
                    product(b[:, :], split_terms(tokens2(0), chunks(wsplit(n)))).then_inc(ring.full, 1)
                pe.wait_ge(ksp_ready, i + 1)
                stack(("kstack", i), ksp)
                pe.wait_ge(qsp_ready, i + 1)
                stack(("qstack", i), qsp[:, i % 2])

            def row_scores(i, f):
                slots, m0 = window(i)
                n = P if i == 0 else 2 * P
                r = half(f % 2)
                b = V.fill(pe, ("rowscores", i, f))[:, :].rearrange("p (a k) -> p a k", a=2)[:, :, 0:n]
                nc.tensor.matmul(b, identb[:, :], maskb[:, m0:m0 + n].rearrange("p (a k) -> p a k", a=1).broadcast_to([P, 2, n]),
                                 start=True, stop=False)
                for m in range(2):
                    pr = 2 * (f // 2) + m
                    mm = nc.tensor.matmul(b[:, m, :], qS[r, pr, :], kS[r, pr, slots, :], start=False, stop=(m == 1))
                mm.then_inc(V.full, 1)

            def key_scores(i, hg):
                r = half(hg % 2)
                for w in range(1 if i == 0 else 2):
                    b = S.fill(pe, ("keyscores", i, hg, w))
                    for m in range(4):
                        pr = 4 * (hg // 2) + m
                        mm = nc.tensor.matmul(b[:, m * P:(m + 1) * P], kS[r, pr, (i - w) % 3, :], qM[r, pr, :],
                                              start=True, stop=True)
                    mm.then_inc(S.full, 1)

            def weigh(i, hg):
                pe.wait_ge(pt_masked, 8 * i + hg + 1)
                if hg == 0 and i >= 1:
                    pe.wait_ge(ctx_ready, 2 * i)
                nw = 1 if i == 0 else 2
                for m in range(4):
                    h = 8 * (hg // 2) + 2 * m + hg % 2
                    for w in range(nw):
                        mm = nc.tensor.matmul(C.banks[h // 16][32 * (h % 4):32 * (h % 4) + 32, (h // 4 % 4) * P:(h // 4 % 4 + 1) * P],
                                              vaug[:, (i - w) % 3, h, :], PT[:, hg % 2, w, m, :],
                                              start=(w == 0), stop=(w == nw - 1))
                mm.then_inc(weighed, 1)

            pe.wait_ge(pads_ready, 5)
            pe.wait_ge(masks_ready, 6)
            front(0)
            A.drained(pe, ("qstack", 0, 3))
            for f in range(H // 2):
                row_scores(0, f)
            for i in range(T):
                if i + 1 < T:
                    front(i + 1)
                pe.wait_ge(max_ready, i + 1)
                stack(("qmstack", i), qsp[:, i % 2])
                A.drained(pe, ("qmstack", i, 3))
                for hg in range(8):
                    key_scores(i, hg)
                    if i + 1 < T:
                        row_scores(i + 1, 2 * hg)
                        row_scores(i + 1, 2 * hg + 1)
                    if hg >= 1:
                        weigh(i, hg - 1)
                weigh(i, 7)
                for a in range(2):
                    pe.wait_ge(ctx_ready, 2 * i + a + 1)
                    b = V.fill(pe, ("context2", i, a))
                    for m in range(4):
                        mm = nc.tensor.transpose(b[:, m * P:(m + 1) * P], cT[:, (4 * a + m) * P:(4 * a + m + 1) * P], ident[:, :])
                    mm.then_inc(V.full, 1)
                V.drained(pe, ("context2", i, 1))
                transpose_row(("co", i), co)
                V.drained(pe, ("co", i))
                pe.wait_ge(w_split, 7)
                b = V.fill(pe, ("wo", i))
                product(b[:, :], split_terms(tokens2(1), chunks(wsplit(3)))).then_inc(V.full, 1)

            acc = banks[4:8]

            def up(n, part, ring, name):
                b = ring.fill(pe, name)
                w = [[m[:, c, part, :] for c in range(DC)] for m, _ in expert(n)]
                product(b[:, :], split_terms(w, [[XT[:, a, c, :] for c in range(DC)] for a in range(2)])).then_inc(ring.full, 1)

            def down(n):
                e = n % NE
                pe.wait_ge(act_ready, n + 1)
                (_, dh), (_, dl) = expert(n)
                hi, lo = (ah[:, n % 2, a, :] for a in range(2))
                for j in range(G):
                    for k, (l, r) in enumerate(((hi, dh), (hi, dl), (lo, dh))):
                        mm = nc.tensor.matmul(acc[j][:, :], l[:, j * P:(j + 1) * P], r,
                                              start=(e == 0 and k == 0), stop=(e == NE - 1 and k == 2))
                mm.then_inc(down_done, 1)

            for g in range(2):
                for j in range(G):
                    pe.wait_ge(x_ready, 2 * T + g * G + j + 1)
                    transpose_row(("x3", g * G + j), X[:, g * G + j, :])
                V.drained(pe, ("x3", g * G + G - 1))
                pe.wait_ge(gate_ready, 3)
                b = V.fill(pe, ("logits", g))
                for j in range(G):
                    mm = product(b[:, j * E:(j + 1) * E], split_terms(tokens(j), [[gr[:, a, c, :] for c in range(DC)] for a in range(2)]))
                mm.then_inc(V.full, 1)
                for e in range(NE):
                    n = g * NE + e
                    if e == SE:
                        pe.wait_ge(cst_ready, g + 1)
                        b = V.fill(pe, ("combine", g))
                        for j in range(G):
                            mm = nc.tensor.transpose(b[0:2 * E, j * P:(j + 1) * P], cst[:, j, :, :], ident[:, :])
                        mm.then_inc(V.full, 1)
                    pe.wait_ge(we_split, n + 1)
                    up(n, 0, A, ("gate", n))
                    up(n, 1, V, ("up", n))
                    if e >= SE:
                        V.drained(pe, ("combine", g))
                        b = V.fill(pe, ("share", n))
                        nc.tensor.matmul(b[:, :], selx[:, e - SE, :], cTr, start=True, stop=True).then_inc(V.full, 1)
                    if e >= 1:
                        if e == 1 and g == 1:
                            pe.wait_ge(acc_done, G)
                        down(n - 1)
                down(n)

        @block.vector
        def _(v):
            steps = [0]

            def own(ins):
                ins.then_inc(dve, 1)
                steps[0] += 1
                v.wait_ge(dve, steps[0])

            def tt(o, a, b, op):
                return nc.vector.tensor_tensor(o, a, b, op)

            def tile_parts(j):
                return [XT[:, a, :, j * P:(j + 1) * P] for a in range(2)]

            def split_xt(name, parts):
                b = V.take(v, name)[:, :].rearrange("p (c n) -> p c n", c=DC)
                hi, lo = parts
                own(nc.vector.tensor_copy(hi, b))
                tt(lo, b, hi.bitcast(F32), ALU.subtract).then_inc(V.free, 1)

            def stats(t):
                own(nc.vector.bn_stats(st6[:, t, :], X[:, t, :]))
                return nc.vector.bn_aggr(mv[:, t, :], st6[:, t, :])

            def normalise(tiles, batch):
                v.wait_ge(std_ready, batch + 1)
                own(nc.vector.reciprocal(rstd[:, tiles], std[:, tiles]))
                for t in range(tiles.start, tiles.stop):
                    nc.vector.tensor_scalar(X[:, t, :], X[:, t, :], mv[:, t, 0:1], rstd[:, t:t + 1],
                                            ALU.subtract, ALU.mult).then_inc(x_ready, 1)

            def low_part(n, slot, raw):
                v.wait_ge(w_high, n + 1)
                tt(W[:, 2 * slot + 1, :], raw, W[:, 2 * slot, :].bitcast(F32), ALU.subtract).then_inc(w_split, 1)

            nc.vector.memset(epst[:, :], EPS).then_inc(small_ready, 1)
            v.wait_ge(bias_in, 16)
            nc.vector.tensor_copy(biasr[:, 0, :, :], biasf).then_inc(bias_ready, 1)
            v.wait_ge(bias_ready, 1)
            tt(biasr[:, 1, :, :], biasf, biasr[:, 0, :, :].bitcast(F32), ALU.subtract).then_inc(bias_ready, 1)
            nc.vector.memset(ones[:, :].bitcast(F32), 1.0).then_inc(bias_ready, 1)

            for g in range(2):
                for j in range(G):
                    split_xt(("x", g * G + j), tile_parts(j))
                if g == 0:
                    for n in range(3):
                        low_part(n, n, raw_a[n])
                    v.wait_ge(k_in[0], 16)
                    nc.vector.tensor_scalar(K[0][:, :, :], kraw[:, :, :], 2.0, -1.0, ALU.mult, ALU.add).then_inc(k_ready, 1)
                    v.wait_ge(consts_in, CONSTS)
                    for n in (1, 2):
                        v.wait_ge(k_in[n], 16)
                        for c in range(DC):
                            nc.vector.tensor_scalar(K[n][:, c, :], kraw[:, c, :], factor[:, 0, c:c + 1], factor[:, 1, c:c + 1],
                                                    ALU.mult, ALU.subtract).then_inc(k_ready, 1)
                for n, dst, count in ((2, vT, HD), (1, kT, H)):
                    for a in range(count // 4):
                        b = V.take(v, ("heads", g, n, a))
                        nc.vector.tensor_copy(dst[:, :, 4 * a:4 * a + 4].rearrange("p s h -> p h s"),
                                              b[:, :].rearrange("p (h s) -> p h s", h=4)).then_inc(V.free, 1)

                def shift(c):
                    if c >= 1:
                        C.drained(v, ("scores", g, c - 1))
                    b = C.take(v, ("scores", g, c))[:, :].rearrange("p (s t) -> p s t", t=H)
                    own(nc.vector.tensor_reduce(small[:, 0, :], b, AX, ALU.max))
                    tt(sc[:, c % 2], b, small[:, 0, :].rearrange("p (s a) -> p s a", a=1).broadcast_to([P, CH, H]), ALU.subtract)\
                        .then_inc(C.free, 1)

                def weights(c):
                    v.wait_ge(expd, g * NCH + c + 1)
                    own(nc.vector.tensor_reduce(small[:, 1, :], sc[:, c % 2], AX, ALU.add))
                    if c >= 2:
                        S.drained(v, ("values", g, c - 2))
                    own(nc.vector.reciprocal(small[:, 2 + c % 2, :], small[:, 1, :]))
                    nc.vector.transpose(pT[:, c % 2], sc[:, c % 2]).then_inc(pt_ready, 1)

                def contexts(c):
                    b = S.take(v, ("values", g, c))[:, 0:CH * HD].rearrange("p (s d) -> p s d", d=HD)
                    tt(cx[:, c * CH:(c + 1) * CH, :], b,
                       small[:, 2 + c % 2, :].rearrange("p (s a) -> p s a", a=1).broadcast_to([P, CH, HD]), ALU.mult).then_inc(S.free, 1)

                shift(0)
                for c in range(NCH):
                    if c + 1 < NCH:
                        shift(c + 1)
                    weights(c)
                    if c >= 1:
                        contexts(c - 1)
                contexts(NCH - 1)
                tiles = slice(g * G, g * G + G)
                for a in range(HD // 4):
                    b = V.take(v, ("context", g, a))[:, :].rearrange("p (m j h) -> p j h m", m=4, j=G)
                    for j in range(G):
                        xv = X[:, g * G + j, :].rearrange("p (h d) -> p h d", d=HD)[:, :, 4 * a:4 * a + 4]
                        ins = tt(xv, xv, b[:, j], ALU.add)
                        if j < G - 1:
                            ins.then_inc(dve, 1)
                            steps[0] += 1
                    ins.then_inc(V.free, 1)
                V.drained(v, ("context", g, HD // 4 - 1))
                for t in range(tiles.start, tiles.stop):
                    ins = stats(t)
                    if t < tiles.stop - 1:
                        ins.then_inc(dve, 1)
                        steps[0] += 1
                ins.then_inc(stats_ready, 1)
                normalise(tiles, g)

            for g in range(2):
                for j in range(G):
                    split_xt(("x1", g * G + j), tile_parts(j))
                for layer, dst in ((0, h1), (1, h2)):
                    for o in range(DC):
                        n = (2 * g + layer) * DC + o
                        A.drained(v, ("hidden", g, layer, o))
                        tt(dst[:, 1, o, :], hf[:, o % 2, :], dst[:, 0, o, :].bitcast(F32), ALU.subtract).then_inc(h_ready, 1)
                for j in range(G):
                    t = g * G + j
                    b = V.take(v, ("ffn", t))
                    nc.vector.scalar_tensor_tensor(X[:, t, :], b[:, :], scales[:, 2:3], X[:, t, :], ALU.mult, ALU.add)\
                        .then_inc(V.free, 1)
                    V.drained(v, ("ffn", t))
                    ins = stats(t)
                    if j < G - 1:
                        ins.then_inc(dve, 1)
                        steps[0] += 1
                ins.then_inc(stats_ready, 1)
                normalise(slice(g * G, g * G + G), 2 + g)
                if g == 0:
                    for n in range(3):
                        low_part(3 + n, n, raw_c[n])
            low_part(6, 3, raw_c[3])

            def rotate(i, n, dst, done):
                name = ("qkv", i, n)
                b = V.take(v, name)[:, :].rearrange("p (h d) -> p h d", d=HD)
                o = dst.rearrange("p (h d) -> p h d", d=HD)
                r = rt.rearrange("p (h d) -> p h d", d=HD)
                cos, sin = (rope[:, i, a:a + 1, :].broadcast_to([P, H, HD]) for a in range(2))
                k = HD // 2
                if n == 0:
                    v.wait_ge(k_turned, i + 1)
                elif i >= 1:
                    v.wait_ge(q_turned, i)
                tt(r, b, cos, ALU.mult).then_inc(dve, 1)
                tt(o[:, :, 0:k], b[:, :, k:HD], sin[:, :, 0:k], ALU.mult).then_inc(dve, 1)
                steps[0] += 2
                tt(o[:, :, k:HD], b[:, :, 0:k], sin[:, :, k:HD], ALU.mult).then_inc(V.free, 1)
                V.drained(v, name)
                tt(dst, dst, rt, ALU.add).then_inc(done, 1)

            def front(i):
                split_xt(("x2", i), [XT2[:, 0, a] for a in range(2)])
                rotate(i, 1, kf, k_turned)
                rotate(i, 0, qf, q_turned)
                q = qsp[:, i % 2]
                v.wait_ge(k_high, i + 1)
                tt(ksp[:, :, HD:2 * HD], kf.rearrange("p (h d) -> p h d", d=HD), ksp[:, :, 0:HD], ALU.subtract).then_inc(ksp_ready, 1)
                nc.vector.memset(q[:, :, 3 * HD:3 * HD + 2], 0.0).then_inc(dve, 1)
                steps[0] += 1
                v.wait_ge(q_high, i + 1)
                tt(q[:, :, 2 * HD:3 * HD].bitcast(F32R), qf.rearrange("p (h d) -> p h d", d=HD), q[:, :, 0:HD], ALU.subtract)\
                    .then_inc(qsp_ready, 1)

            def row_maxima(i):
                n = P if i == 0 else 2 * P
                for f in range(H // 2):
                    b = V.take(v, ("rowscores", i, f))[:, :].rearrange("p (a k) -> p a k", a=2)[:, :, 0:n]
                    h = 4 * (f // 2) + f % 2
                    nc.vector.tensor_reduce(hmax[:, h:h + 3:2], b, AX, ALU.max).then_inc(V.free, 1)
                V.drained(v, ("rowscores", i, H // 2 - 1))
                m = hmax[:, :].rearrange("p (h a) -> p h a", a=1)
                q = qsp[:, i % 2]
                own(nc.vector.tensor_copy(q[:, :, 3 * HD:3 * HD + 1].bitcast(F32R), m))
                tt(q[:, :, 3 * HD + 1:3 * HD + 2], m, q[:, :, 3 * HD:3 * HD + 1], ALU.subtract).then_inc(max_ready, 1)

            front(0)
            row_maxima(0)
            for i in range(T):
                if i + 1 < T:
                    front(i + 1)
                    row_maxima(i + 1)
                v.wait_ge(weighed, 8 * (i + 1))
                for a in range(2):
                    nc.vector.tensor_copy(cT[:, a * 512:(a + 1) * 512], C.banks[a][:, :]).then_inc(ctx_ready, 1)
                for a in range(2):
                    b = V.take(v, ("context2", i, a))[:, :].rearrange("p (h r) -> p h r", r=32)
                    s = hsum[:, a, :].rearrange("p (h r) -> p h r", r=1)
                    own(nc.vector.reciprocal(s, b[:, :, HD:HD + 1]))
                    tt(co[:, a * 256:(a + 1) * 256].rearrange("p (h d) -> p h d", d=HD), b[:, :, 0:HD], s.broadcast_to([P, 16, HD]),
                       ALU.mult).then_inc(V.free, 1)
                split_xt(("co", i), [XT2[:, 1, a] for a in range(2)])
                b = V.take(v, ("wo", i))
                tt(X[:, i, :], X[:, i, :], b[:, :], ALU.add).then_inc(V.free, 1)
                V.drained(v, ("wo", i))
                ins = stats(i)
                if i < T - 1:
                    ins.then_inc(dve, 1)
                    steps[0] += 1
            ins.then_inc(stats_ready, 1)
            normalise(slice(0, T), 4)

            v.wait_ge(gate_in, 48)
            gv = gates.rearrange("p (c e) -> p c e", c=DC)
            nc.vector.tensor_copy(gr[:, 0], gv).then_inc(gate_ready, 1)
            v.wait_ge(gate_ready, 1)
            tt(gr[:, 1], gv, gr[:, 0].bitcast(F32), ALU.subtract).then_inc(gate_ready, 1)
            nc.vector.tensor_copy(RP[0:2 * E, 2560:2560 + E * P], selr).then_inc(gate_ready, 1)
            for g in range(2):
                for j in range(G):
                    split_xt(("x3", g * G + j), tile_parts(j))
                rk = rank.rearrange("p (a e) -> p a e", a=1).broadcast_to([P, G, E])
                b = V.take(v, ("logits", g))
                nc.vector.tensor_copy(lg, b[:, 0:G * E].rearrange("p (t e) -> p t e", e=E)).then_inc(V.free, 1)
                V.drained(v, ("logits", g))

                def best(src, one, mx):
                    m = tiny[:, mx, :].rearrange("p (t a) -> p t a", a=1)
                    r = tiny[:, 2, :].rearrange("p (t a) -> p t a", a=1)
                    own(nc.vector.tensor_reduce(tiny[:, mx, :], src, AX, ALU.max))
                    own(tt(tmp, src, m.broadcast_to([P, G, E]), ALU.is_equal))
                    own(tt(tmp, tmp, rk, ALU.mult))
                    own(nc.vector.tensor_reduce(tiny[:, 2, :], tmp, AX, ALU.max))
                    own(tt(one, tmp, r.broadcast_to([P, G, E]), ALU.is_equal))

                best(lg, oh1, 0)
                tt(ex, lg, tiny[:, 0, :].rearrange("p (t a) -> p t a", a=1).broadcast_to([P, G, E]), ALU.subtract).then_inc(logits_shifted, 1)
                own(nc.vector.scalar_tensor_tensor(l2, oh1, -BIG, lg, ALU.mult, ALU.add))
                best(l2, oh2, 1)
                own(tt(oh1, oh1, oh2, ALU.add))
                v.wait_ge(logits_exp, g + 1)
                own(tt(cw, ex, oh1, ALU.mult))
                own(nc.vector.tensor_reduce(tiny[:, 2, :], cw, AX, ALU.add))
                own(nc.vector.reciprocal(tiny[:, 3, :], tiny[:, 2, :]))
                own(tt(cw, cw, tiny[:, 3, :].rearrange("p (t a) -> p t a", a=1).broadcast_to([P, G, E]), ALU.mult))
                own(nc.vector.tensor_copy(cst[:, :, 0, :].bitcast(F32R), cw))
                tt(cst[:, :, 1, :], cw, cst[:, :, 0, :], ALU.subtract).then_inc(cst_ready, 1)
                for e in range(NE):
                    n = g * NE + e
                    if e == SE:
                        b = V.take(v, ("combine", g))
                        nc.vector.tensor_copy(cTr, b[0:2 * E, :]).then_inc(V.free, 1)
                    b = V.take(v, ("up", n))
                    A.drained(v, ("gate", n))
                    if n >= 1:
                        v.wait_ge(act_ready, n)
                    tt(ac, sg[:, n % 2, :], b[:, :], ALU.mult).then_inc(V.free, 1)
                    V.drained(v, ("up", n))
                    if e >= SE:
                        b = V.take(v, ("share", n))
                        tt(ac, ac, b[:, :], ALU.mult).then_inc(V.free, 1)
                        V.drained(v, ("share", n))
                    if n >= 2:
                        v.wait_ge(down_done, n - 1)
                    own(nc.vector.tensor_copy(ah[:, n % 2, 0, :], ac))
                    tt(ah[:, n % 2, 1, :], ac, ah[:, n % 2, 0, :].bitcast(F32), ALU.subtract).then_inc(act_ready, 1)
                v.wait_ge(down_done, (g + 1) * NE)
                for j in range(G):
                    t = g * G + j
                    tt(X[:, t, :], X[:, t, :], banks[4 + j][:, :], ALU.add).then_inc(acc_done, 1)
                    v.wait_ge(acc_done, t + 1)
                    ins = stats(t)
                    if j < G - 1:
                        ins.then_inc(dve, 1)
                        steps[0] += 1
                ins.then_inc(stats_ready, 1)
                normalise(slice(g * G, g * G + G), 5 + g)

        @block.scalar
        def _(s):
            steps = [0]

            def act(o, i, func, **kw):
                return nc.scalar.activation(o, i, func, **kw)

            def high_part(n, slot, raw, arrived):
                s.wait_ge(arrived, 16)
                act(W[:, 2 * slot, :], raw, ACT.Copy).then_inc(w_high, 1)

            def roots(tiles, batch):
                s.wait_ge(stats_ready, batch + 1)
                act(std[:, tiles], mv[:, tiles, 1], ACT.Sqrt, bias=epst[:, 0:1]).then_inc(std_ready, 1)

            for n in range(3):
                high_part(n, n, raw_a[n], wa_in[n])
            s.wait_ge(small_ready, 1)
            for g in range(2):
                def rows_out(n):
                    for j in range(G):
                        b = A.take(s, ("rows", g, n, j))
                        if n == 2:
                            act(vrow[:, :, j, :], b[:, :].rearrange("p (h d) -> p d h", d=HD), ACT.Copy).then_inc(A.free, 1)
                        else:
                            act(qkrow[:, :, j, 0:HD], b[:, :].rearrange("p (h d) -> p h d", d=HD), ACT.Copy).then_inc(A.free, 1)

                if g == 0:
                    s.wait_ge(pads_ready, 1)
                rows_out(0)
                if g == 1:
                    V.drained(s, ("context", 0, HD // 4 - 1))
                rows_out(2)
                s.wait_ge(w_split, 3)
                for a in range(H // 4):
                    b = A.take(s, ("heads", g, 0, a))
                    act(qT[:, :, 4 * a:4 * a + 4].rearrange("p s h -> p h s"), b[:, :].rearrange("p (h s) -> p h s", h=4),
                        ACT.Copy).then_inc(A.free, 1)
                rows_out(1)
                for c in range(NCH):
                    C.drained(s, ("scores", g, c))
                    act(sc[:, c % 2], sc[:, c % 2], ACT.Exp, scale=SCALE).then_inc(expd, 1)
                roots(slice(g * G, g * G + G), g)

            for g in range(2):
                if g == 1:
                    for n in range(3):
                        high_part(3 + n, n, raw_c[n], wc_in[n])
                for layer, dst in ((0, h1), (1, h2)):
                    for o in range(DC):
                        n = (2 * g + layer) * DC + o
                        b = A.take(s, ("hidden", g, layer, o))
                        if n >= 2:
                            s.wait_ge(h_ready, n - 1)
                        act(dst[:, 0, o, :], b[:, :], ACT.Relu, scale=scales[:, layer:layer + 1]).then_inc(act_step, 1)
                        act(hf[:, o % 2, :], b[:, :], ACT.Relu, scale=scales[:, layer:layer + 1]).then_inc(A.free, 1)
                roots(slice(g * G, g * G + G), 2 + g)
            high_part(6, 3, raw_c[3], wc_in[3])

            def front(i):
                q = qsp[:, i % 2].rearrange("p h (a r) -> p h a r", r=HD)
                k = ksp.rearrange("p h (a r) -> p h a r", r=HD)
                s.wait_ge(k_turned, i + 1)
                act(k[:, :, 0:3:2, :].bitcast(F32R), kf.rearrange("p (h a r) -> p h a r", a=1, r=HD).broadcast_to([P, H, 2, HD]), ACT.Copy)\
                    .then_inc(k_high, 1)
                s.wait_ge(q_turned, i + 1)
                act(q[:, :, 0:2, :].bitcast(F32R), qf.rearrange("p (h a r) -> p h a r", a=1, r=HD).broadcast_to([P, H, 2, HD]), ACT.Copy)\
                    .then_inc(q_high, 1)
                b = A.take(s, ("qkv", i, 2))
                act(vaug[:, i % 3, :, 0:HD], b[:, :].rearrange("p (h d) -> p h d", d=HD), ACT.Copy).then_inc(A.free, 1)
                for a in range(4):
                    b = A.take(s, ("kstack", i, a))
                    act(kS[:, 4 * a:4 * a + 4, i % 3, :], b[:, :].rearrange("p (m k) -> p m k", m=4), ACT.Copy).then_inc(A.free, 1)
                for a in range(4):
                    b = A.take(s, ("qstack", i, a))
                    act(qS[:, 4 * a:4 * a + 4, :], b[:, :].rearrange("p (m k) -> p m k", m=4), ACT.Copy).then_inc(A.free, 1)

            s.wait_ge(pads_ready, 5)
            front(0)
            for i in range(T):
                if i + 1 < T:
                    front(i + 1)
                for a in range(4):
                    b = A.take(s, ("qmstack", i, a))
                    act(qM[:, 4 * a:4 * a + 4, :], b[:, :].rearrange("p (m k) -> p m k", m=4), ACT.Copy).then_inc(A.free, 1)
                for hg in range(8):
                    n = 8 * i + hg
                    if n >= 2:
                        s.wait_ge(weighed, n - 1)
                    for w in range(1 if i == 0 else 2):
                        b = S.take(s, ("keyscores", i, hg, w))
                        act(PT[:, hg % 2, w], b[:, :].rearrange("p (m q) -> p m q", m=4), ACT.Exp, scale=SCALE).then_inc(S.free, 1)
            roots(slice(0, T), 4)

            def expert_high(n):
                s.wait_ge(we_in[n % 3], 48 * (n // 3 + 1))
                if n >= 3:
                    s.wait_ge(down_done, n - 2)
                act(W[:, 2 * (n % 3), 0:WCOLS], raw_e[n % 3], ACT.Copy).then_inc(we_high, 1)

            expert_high(0)
            for g in range(2):
                s.wait_ge(logits_shifted, g + 1)
                act(ex, ex, ACT.Exp).then_inc(logits_exp, 1)
                for e in range(NE):
                    n = g * NE + e
                    if n + 1 < 2 * NE:
                        expert_high(n + 1)
                    b = A.take(s, ("gate", n))
                    if n >= 2:
                        s.wait_ge(act_ready, n - 1)
                    act(sg[:, n % 2, :], b[:, :], ACT.Silu).then_inc(A.free, 1)
                roots(slice(g * G, g * G + G), 5 + g)

        @block.gpsimd
        def _(p):
            nc.gpsimd.memset(ident[:, :], 0.0).then_inc(ident_ready, 1)
            p.wait_ge(ident_ready, 1)
            nc.gpsimd.affine_select(out=ident[:, :], in_=ident[:, :], compare_op=ALU.not_equal, fill=1.0, base=0,
                                    pattern=[[-1, P]], channel_multiplier=1).then_inc(ident_ready, 1)
            nc.gpsimd.memset(qkrow[:, :, :, HD:2 * HD], 0.0).then_inc(pads_ready, 1)
            nc.gpsimd.memset(maskb[:, :], 0.0).then_inc(masks_ready, 1)
            nc.gpsimd.memset(identb[:, :], 0.0).then_inc(masks_ready, 1)
            p.wait_ge(masks_ready, 2)
            nc.gpsimd.affine_select(out=identb[:, :], in_=identb[:, :], compare_op=ALU.not_equal, fill=1.0, base=0,
                                    pattern=[[-1, P]], channel_multiplier=1).then_inc(masks_ready, 1)
            for k, (base, step) in enumerate(((0, -1), (-1, 1), (0, -1))):
                m = maskb[:, k * P:(k + 1) * P]
                nc.gpsimd.affine_select(out=m, in_=m, compare_op=ALU.is_ge, fill=-BIG, base=base,
                                        pattern=[[step, P]], channel_multiplier=-step).then_inc(masks_ready, 1)
            p.wait_ge(w_split, 6)
            nc.gpsimd.memset(qsp[:, :, :, 3 * HD:KS], 0.0).then_inc(pads_ready, 1)
            nc.gpsimd.memset(ksp[:, :, 3 * HD:3 * HD + 2], -1.0).then_inc(pads_ready, 1)
            nc.gpsimd.memset(ksp[:, :, 3 * HD + 2:KS], 0.0).then_inc(pads_ready, 1)
            nc.gpsimd.memset(vaug[:, :, :, HD + 1:32], 0.0).then_inc(pool, 1)
            nc.gpsimd.memset(vaug[:, :, :, HD:HD + 1], 1.0).then_inc(pads_ready, 1)
            for i in range(T):
                for hg in range(8):
                    nw = 1 if i == 0 else 2
                    for w in range(nw):
                        S.drained(p, ("keyscores", i, hg, w))
                        pt = PT[:, hg % 2, w]
                        if w == 0:
                            ins = nc.gpsimd.affine_select(out=pt, in_=pt, compare_op=ALU.is_ge, fill=0.0, base=0,
                                                          pattern=[[0, 4], [1, P]], channel_multiplier=-1)
                        else:
                            ins = nc.gpsimd.affine_select(out=pt, in_=pt, compare_op=ALU.is_ge, fill=0.0, base=-1,
                                                          pattern=[[0, 4], [-1, P]], channel_multiplier=1)
                        ins.then_inc(pt_masked if w == nw - 1 else pool, 1)
            for n in range(2 * NE):
                p.wait_ge(we_high, n + 1)
                k = 2 * (n % 3)
                nc.gpsimd.tensor_tensor(W[:, k + 1, 0:WCOLS], raw_e[n % 3], W[:, k, 0:WCOLS].bitcast(F32), ALU.subtract)\
                    .then_inc(we_split, 1)


def _constants(np):
    inv = (1.0 / np.power(np.float32(10000.0), np.arange(0, HD, 2, dtype=np.float32) / np.float32(HD))).astype(np.float32)
    freqs = np.arange(T * P, dtype=np.float32)[:, None] * inv[None, :]
    cos, sin = np.cos(freqs), np.sin(freqs)
    f = np.where(np.arange(D) < round(D * 0.8), 2.0, 2.0 * -0.8 / (1.0 - 0.8)).astype(np.float32).reshape(DC, P).T
    select = np.zeros((2 * E, E, P))
    for e in range(E):
        select[e, e] = select[E + e, e] = 1.0
    tables = {
        "rope": np.stack([np.concatenate([cos, cos], 1), np.concatenate([-sin, sin], 1)], 1),
        "factor": np.stack([2 * f, f], 1), "select": select.reshape(2 * E, E * P),
        "rank": np.broadcast_to(np.arange(E, 0, -1), (P, E)),
    }
    return {k: np.ascontiguousarray(t, dtype=np.float32) for k, t in tables.items()}


def kernel(**inputs):
    import numpy as np
    import concourse.bacc as _bacc
    from concourse import mybir as _mybir
    from concourse.bass_utils import run_bass_kernel_spmd as _run

    a = {k: np.asarray(v) for k, v in inputs.items()}
    lay = {
        "x": a["L0_attn_hidden_states"][0],
        "wq": a["L0_attn_wq"].T, "wk": a["L0_attn_wk"].T, "wv": a["L0_attn_wv"].T,
        "bias": np.stack([a["L0_attn_bq"], a["L0_attn_bk"], a["L0_attn_bv"]]),
        "k0": a["L0_ffn_k0"], "k1": a["L0_ffn_k1"], "k2": a["L0_ffn_k2"],
        "s0": a["L0_ffn_s0"].reshape(1, 1), "s1": a["L0_ffn_s1"].reshape(1, 1), "s2": a["L0_ffn_s2"].reshape(1, 1),
        "aq": a["L1_attn_Wq"].T, "ak": a["L1_attn_Wk"].T, "av": a["L1_attn_Wv"].T, "ao": a["L1_attn_Wo"].T,
        "gate": a["L1_ffn_gate_w"].T,
        "wgu": a["L1_ffn_w_gate_up"].transpose(0, 2, 1), "wd": a["L1_ffn_w_down"].transpose(0, 2, 1),
        "sgu": a["L1_ffn_shared_w_gate_up"].T, "sd": a["L1_ffn_shared_w_down"].T,
    }
    nc = _bacc.Bacc("TRN2", target_bir_lowering=False, num_devices=1)
    arrays, args = {}, []
    for name, array in [*lay.items(), *_constants(np).items()]:
        array = np.ascontiguousarray(array)
        arrays[f"in_{name}_dram"] = array
        args.append(nc.dram_tensor(f"in_{name}_dram", array.shape, _mybir.dt.from_np(array.dtype), kind="ExternalInput").ap())
    args.append(nc.dram_tensor("out_0_dram", (T * P, D), _mybir.dt.from_np(np.dtype("float32")), kind="ExternalOutput").ap())
    build(nc, *args)
    r = _run(nc, [arrays], core_ids=[0])
    return r.results[0]["out_0_dram"].reshape(1, T * P, D)
```

```python
from contextlib import ExitStack

import concourse.bass as bass
from concourse import mybir

F32 = mybir.dt.float32
F32R = mybir.dt.float32r
BF16 = mybir.dt.bfloat16
U8 = mybir.dt.uint8
U32 = mybir.dt.uint32
I32 = mybir.dt.int32
ALU = mybir.AluOpType
ACT = mybir.ActivationFunctionType
AX = mybir.AxisListType.X

P = 128
D = 512
DC = D // P
T = 1024 // P
G = 4
H = 32
HD = D // H
KS = 64
E = 16
SE = 4
TOP = 2
NB = T * TOP + E - 1
WB, XB_, YB_ = 4, 3, 3
YG = 12
EPS = 1e-5
SCALE = HD ** -0.5
CONSTS = 5 * 16
BIG = 1e30
CH = 16
NCH = P // CH
WCOLS = DC * 2 * P + D
TABLE = E + E * E + T + NB

ITEMS = ([("shared", 0, e) for e in range(SE)] + [("block", b) for b in range(12)] + [("shared", 1, 0)]
         + [("block", b) for b in range(12, 22)] + [("shared", 1, 1)] + [("block", b) for b in range(22, NB)]
         + [("shared", 1, e) for e in range(2, SE)])


class Ring:

    def __init__(self, banks, full, free):
        self.banks, self.full, self.free = banks, full, free
        self.number, self.taken = {}, 0

    def fill(self, pe, name):
        n, size = len(self.number), len(self.banks)
        assert name not in self.number
        self.number[name] = n
        if n >= size:
            pe.wait_ge(self.free, n - size + 1)
        return self.banks[n % size]

    def filled(self, engine, name):
        n = self.number[name]
        engine.wait_ge(self.full, n + 1)
        return self.banks[n % len(self.banks)]

    def take(self, engine, name):
        n = self.number[name]
        assert n == self.taken, (name, n, self.taken)
        self.taken += 1
        return self.filled(engine, name)

    def drained(self, engine, name):
        engine.wait_ge(self.free, self.number[name] + 1)


def build(nc, x, wq, wk, wv, bias, k0, k1, k2, s0, s1, s2, aq, ak, av, ao, gate, experts, shared,
          rope_c, factor_c, table_c, out, xs, ys):
    with ExitStack() as ctx:
        def sb(name, shape, dt):
            return ctx.enter_context(nc.sbuf_tensor(name, shape, dt))

        def sem(name):
            return ctx.enter_context(nc.semaphore(name))

        banks = [ctx.enter_context(nc.psum_tensor(f"bank{i}", [P, 512], F32)) for i in range(8)]

        X = sb("X", [P, T, D], F32)
        W = sb("W", [P, 8, DC * D], F32R)
        XR = sb("XR", [P, 2 * DC * G * P], F32R)
        XT = XR[:, :].rearrange("p (a c n) -> p a c n", a=2, c=DC)
        RP = sb("RP", [P, 8192], F32R)
        FP = sb("FP", [P, 18432], F32)
        ident = sb("ident", [P, P], F32)
        identb = sb("identb", [P, P], BF16)
        maskb = sb("maskb", [P, 3 * P], BF16)
        rope = sb("rope", [P, T, 2, HD], F32)
        factor = sb("factor", [P, 2, DC], F32)
        scales = sb("scales", [P, 3], F32)
        ones = sb("ones", [1, P], F32R)
        kraw = sb("kraw", [P, DC, D], U8)
        epst = sb("epst", [P, 1], F32)
        st6 = sb("st6", [P, T, 6], F32)
        mv = sb("mv", [P, T, 2], F32)
        std = sb("std", [P, T], F32)
        rstd = sb("rstd", [P, T], F32)
        small = sb("small", [P, 4, CH], F32)
        hmax = sb("hmax", [P, H], F32)
        before = sb("before", [P, P], BF16)
        onesb = sb("onesb", [P, P], BF16)
        picked = sb("picked", [P, T + 1, E], BF16)
        slots = sb("slots", [P, TOP, T], U32)
        owner = sb("owner", [1, NB + 1], I32)
        share = sb("share", [P, TOP, T], F32)
        hsum = sb("hsum", [P, 2, G * G], F32)

        biasf = FP[0:1, 16384:17920].rearrange("p (n d) -> p n d", n=3)
        biasr = RP[0:1, 0:3072].rearrange("p (a n d) -> p a n d", a=2, n=3)
        qkrow = FP[:, 0:4096].rearrange("p (h t r) -> p h t r", h=H, t=G)
        vrow = FP[:, 4096:6144].rearrange("p (d t h) -> p d t h", d=HD, t=G)
        cx = FP[:, 4096:6144].rearrange("p (s d) -> p s d", d=HD)
        qT = FP[:, 6144:10240].rearrange("p (s h) -> p s h", h=H)
        kT = FP[:, 10240:14336].rearrange("p (s h) -> p s h", h=H)
        vT = FP[:, 14336:16384].rearrange("p (s d) -> p s d", d=HD)
        sc = FP[:, 16384:17408].rearrange("p (b s t) -> p b s t", b=2, t=H)
        pT = FP[:, 17408:18432].rearrange("p (b s t) -> p b s t", b=2, t=H)
        raw_a = [FP[:, 6144:8192], FP[:, 10240:12288], FP[:, 14336:16384]]
        h1 = RP[:, 0:4096].rearrange("p (a c n) -> p a c n", a=2, c=DC)
        h2 = XT
        K = [W[:, 6, :].rearrange("p (c n) -> p c n", c=DC), W[:, 7, :].rearrange("p (c n) -> p c n", c=DC),
             RP[:, 4096:6144].rearrange("p (c n) -> p c n", c=DC)]
        hf = FP[:, 16384:17408].rearrange("p (b n) -> p b n", b=2)
        raw_c = [FP[:, 0:2048], FP[:, 2048:4096], FP[:, 4096:6144], FP[:, 14336:16384]]
        qsp = FP[:, 0:4096].rearrange("p (b h r) -> p b h r", b=2, r=KS)
        ksp = FP[:, 4096:6144].rearrange("p (h r) -> p h r", r=KS)
        qf = FP[:, 6144:6656]
        kf = FP[:, 6656:7168]
        rt = FP[:, 7168:7680]
        vaug = FP[:, 7680:10752].rearrange("p (s h r) -> p s h r", s=3, r=32)
        PT = FP[:, 10752:12800].rearrange("p (b w h q) -> p b w h q", b=2, w=2, h=G)
        cT = FP[:, 12800:13824]
        co = FP[:, 13824:14336]
        XT2 = XR[:, 0:2048].rearrange("p (b a c n) -> p b a c n", b=2, a=2, c=DC)
        qS = XR[:, 2048:4096].rearrange("p (a q) -> p a q", q=P)
        qM = RP[:, 0:2048].rearrange("p (a q) -> p a q", q=P)
        kS = RP[:, 2048:8192].rearrange("p (a s k) -> p a s k", s=3, k=P)
        wblock = [FP[:, c:c + WCOLS] for c in (14336, 14336 + WCOLS, 0, WCOLS)]
        xblock = FP[:, 3072:4608].rearrange("p (b n) -> p b n", b=XB_)
        xbT = FP[:, 4608:5632].rearrange("p (b c n) -> p b c n", b=2, c=DC)
        yblock = FP[:, 5632:7168].rearrange("p (b n) -> p b n", b=YB_)
        sg = FP[:, 7168:8192].rearrange("p (b n) -> p b n", b=2)
        gathered = FP[:, 8192:14336].rearrange("p (b n) -> p b n", b=YG)
        ac = FP[:, 17408:17920]
        ab = FP[:, 17920:18176].rearrange("p (b n) -> p b n", b=2)
        gates = FP[:, 17408:17472]
        table = FP[:, 17920:17920 + TABLE]
        rank, first, full, block_no = (table[:, a:b] for a, b in ((0, E), (E, E + E * E), (E + E * E, E + E * E + T),
                                                                 (E + E * E + T, TABLE)))
        lg, l2, tmp = (FP[:, 8192 + 128 * n:8320 + 128 * n].rearrange("p (t e) -> p t e", e=E) for n in range(3))
        oh, oslot = (FP[:, a:a + 256].rearrange("p (k t e) -> p k t e", k=TOP, e=E) for a in (8576, 8832))
        ranks = FP[:, 9088:9088 + (T + 1) * E].rearrange("p (t e) -> p t e", e=E)
        nblocks, base, ends = (FP[:, 9232 + E * n:9232 + E * (n + 1)] for n in range(3))
        over = FP[:, 9280:9408].rearrange("p (e k) -> p e k", k=T)
        firsts = FP[:, 9408:9664].rearrange("p (e f) -> p e f", f=E)
        passed = FP[0:1, 9664:9664 + NB * E].rearrange("p (b e) -> p b e", e=E)
        ownf = FP[0:1, 10176:10176 + NB]
        slotf = FP[:, 10240:10256].rearrange("p (k t) -> p k t", k=TOP)
        tiny = FP[:, 10256:10296].rearrange("p (a t) -> p a t", t=T)
        XT3 = [XT, RP[:, 0:4096].rearrange("p (a c n) -> p a c n", a=2, c=DC)]
        ah = RP[:, 4096:6144].rearrange("p (b a n) -> p b a n", b=2, a=2)
        gr = RP[:, 6144:6144 + 2 * DC * E].rearrange("p (a c e) -> p a c e", a=2, c=DC)
        zeros = RP[:, 6144:8192].bitcast(F32)

        V = Ring(banks[0:2], sem("vbank_full"), sem("vbank_free"))
        A = Ring(banks[2:4], sem("abank_full"), sem("abank_free"))
        C = Ring(banks[4:6], sem("cbank_full"), sem("cbank_free"))
        S = Ring(banks[6:8], sem("sbank_full"), sem("sbank_free"))
        x_in = [sem(f"x_in{g}") for g in range(2)]
        wa_in = [sem(f"wa_in{n}") for n in range(3)]
        k_in = [sem(f"k_in{n}") for n in range(3)]
        wc_in = [sem(f"wc_in{n}") for n in range(4)]
        shared_in = [sem(f"shared_in{n}") for n in range(2)]
        wblock_in = [sem(f"wblock_in{n}") for n in range(WB)]
        xblock_in = [sem(f"xblock_in{n}") for n in range(XB_)]
        yblock_out = [sem(f"yblock_out{n}") for n in range(YB_)]
        tile_gathered = [sem(f"tile_gathered{t}") for t in range(T)]
        zeros_ready = sem("zeros_ready")
        zeroed = sem("zeroed")
        picked_ready = sem("picked_ready")
        slots_ready = sem("slots_ready")
        owner_ready = sem("owner_ready")
        scattered = sem("scattered")
        silu_done = sem("silu_done")
        combined = sem("combined")
        XBank = Ring(banks[0:1], sem("xtbank_full"), sem("xtbank_free"))
        YBank = Ring(banks[1:2], sem("ybank_full"), sem("ybank_free"))
        consts_in = sem("consts_in")
        bias_in = sem("bias_in")
        gate_in = sem("gate_in")
        out_done = sem("out_done")
        w_high = sem("w_high")
        w_split = sem("w_split")
        k_ready = sem("k_ready")
        dve = sem("dve_step")
        act_step = sem("act_step")
        pool = sem("pool_step")
        small_ready = sem("small_ready")
        bias_ready = sem("bias_ready")
        ident_ready = sem("ident_ready")
        masks_ready = sem("masks_ready")
        pads_ready = sem("pads_ready")
        x_ready = sem("x_ready")
        stats_ready = sem("stats_ready")
        std_ready = sem("std_ready")
        expd = sem("expd")
        pt_ready = sem("pt_ready")
        h_ready = sem("h_ready")
        k_turned = sem("k_turned")
        q_turned = sem("q_turned")
        k_high = sem("k_high")
        q_high = sem("q_high")
        ksp_ready = sem("ksp_ready")
        qsp_ready = sem("qsp_ready")
        max_ready = sem("max_ready")
        pt_masked = sem("pt_masked")
        weighed = sem("weighed")
        ctx_ready = sem("ctx_ready")
        we_high = sem("we_high")
        we_split = sem("we_split")
        gate_ready = sem("gate_ready")
        logits_shifted = sem("logits_shifted")
        logits_exp = sem("logits_exp")
        act_ready = sem("act_ready")
        down_done = sem("down_done")
        acc_done = sem("acc_done")

        def wsplit(n):
            return (W[:, 2 * n, :].rearrange("p (c n) -> p c n", c=DC), W[:, 2 * n + 1, :].rearrange("p (c n) -> p c n", c=DC))

        def window(i):
            cur, prev = i % 3, (i - 1) % 3
            if i == 0:
                return cur, 0
            if prev < cur:
                return slice(prev, cur + 1, cur - prev), P
            return slice(cur, prev + 1, prev - cur), 0

        def halves(e):
            return [(W[:, 2 * e + a, 0:DC * 2 * P].rearrange("p (c g n) -> p c g n", c=DC, g=2),
                     W[:, 2 * e + a, DC * 2 * P:WCOLS]) for a in range(2)]

        def last_fill(k):
            return ("up", k, 1 if ITEMS[k][0] == "shared" else 0)

        item_of = {item[1]: k for k, item in enumerate(ITEMS) if item[0] == "block"}

        block = ctx.enter_context(nc.Block())

        @block.sync
        def _(sp):
            xin = x.rearrange("(g t p) n -> g p t n", g=2, p=P)
            sp.dma_start(X[:, 0:G, :], xin[0]).then_inc(x_in[0], 16)
            for n, w in enumerate((wq, wk, wv)):
                sp.dma_start(raw_a[n].rearrange("p (c n) -> p c n", c=DC), w.rearrange("(c p) n -> p c n", p=P)).then_inc(wa_in[n], 16)
            sp.dma_start(biasf, bias.rearrange("(a b) n -> a b n", a=1)).then_inc(bias_in, 16)
            sp.dma_start(rope[:, :, :, :], rope_c.rearrange("(t p) a d -> p t a d", p=P)).then_inc(consts_in, 16)
            sp.dma_start(factor[:, :, :], factor_c).then_inc(consts_in, 16)
            for n, s in enumerate((s0, s1, s2)):
                sp.dma_start(scales[:, n:n + 1], s.broadcast_to([P, 1])).then_inc(consts_in, 16)
            sp.dma_start(X[:, G:T, :], xin[1]).then_inc(x_in[1], 16)
            for n, k in enumerate((k0, k1, k2)):
                if n >= 1:
                    sp.wait_ge(k_ready, 1 + (n - 1) * DC)
                sp.dma_start(kraw[:, :, :], k.rearrange("(c p) n -> p c n", p=P)).then_inc(k_in[n], 16)
            sp.wait_ge(zeros_ready, 1)
            for b in range(0, NB, 4):
                n = min(4, NB - b)
                sp.dma_start(xs[b * P:(b + n) * P, :].rearrange("(b p) n -> p b n", p=P),
                             zeros.rearrange("p (b n) -> p b n", b=4)[:, 0:n, :]).then_inc(zeroed, 16)
            sp.wait_ge(x_ready, T)
            for n, w in enumerate((aq, ak, av, ao)):
                sp.dma_start(raw_c[n].rearrange("p (c n) -> p c n", c=DC), w.rearrange("(c p) n -> p c n", p=P)).then_inc(wc_in[n], 16)
            sp.wait_ge(w_split, 7)
            for e in range(SE):
                if e >= 2:
                    sp.wait_ge(we_split, e - 1)
                sp.dma_start(wblock[e % 2], shared[e]).then_inc(shared_in[e % 2], 16)
                if e == 1:
                    sp.dma_start(gates.rearrange("p (c e) -> p c e", c=DC), gate.rearrange("(c p) e -> p c e", p=P)).then_inc(gate_in, 16)
                    sp.dma_start(table, table_c).then_inc(gate_in, 16)

            def load_weights(b):
                if b < 2:
                    sp.wait_ge(we_split, b + 3)
                if b >= WB:
                    sp.wait_ge(down_done, item_of[b - WB] + 1)
                e = nc.sync.value_load(owner[0:1, b:b + 1], min_val=0, max_val=E - 1)
                sp.dma_start(wblock[b % WB], experts[bass.ds(e, 1), :, :].rearrange("a p n -> (a p) n")).then_inc(wblock_in[b % WB], 16)

            def load_tokens(b):
                if b >= XB_:
                    sp.wait_ge(XBank.full, b - XB_ + 1)
                sp.dma_start(xblock[:, b % XB_, :], xs[b * P:(b + 1) * P, :]).then_inc(xblock_in[b % XB_], 16)

            sp.wait_ge(owner_ready, 1)
            for b in range(WB - 1):
                load_weights(b)
            sp.wait_ge(scattered, 16 * TOP * T)
            load_tokens(0)
            load_tokens(1)
            for b in range(NB):
                if b + 2 < NB:
                    load_tokens(b + 2)
                if b + 3 < NB:
                    load_weights(b + 3)
            for t in range(T):
                sp.wait_ge(x_ready, 3 * T + t + 1)
                sp.dma_start(out[t * P:(t + 1) * P, :], X[:, t, :]).then_inc(out_done, 16)
            sp.wait_ge(out_done, 16 * T)

        @block.tensor
        def _(pe):
            def product(bank, terms):
                for n, (lhs, rhs) in enumerate(terms):
                    mm = nc.tensor.matmul(bank, lhs, rhs, start=(n == 0), stop=(n == len(terms) - 1))
                return mm

            def split_terms(lhs, rhs):
                return [t for lh, ll, rh, rl in zip(*lhs, *rhs) for t in ((lh, rh), (lh, rl), (ll, rh))]

            def transpose_row(name, src):
                b = V.fill(pe, name)
                for c in range(DC):
                    mm = nc.tensor.transpose(b[:, c * P:(c + 1) * P], src[:, c * P:(c + 1) * P], ident[:, :])
                mm.then_inc(V.full, 1)

            def tokens(j):
                return [[XT[:, a, c, j * P:(j + 1) * P] for c in range(DC)] for a in range(2)]

            def tokens2(b):
                return [[XT2[:, b, a, c, :] for c in range(DC)] for a in range(2)]

            def chunks(w):
                return [[m[:, c, :] for c in range(DC)] for m in w]

            pe.wait_ge(ident_ready, 2)
            for g in range(2):
                pe.wait_ge(x_in[g], 16)
                for j in range(G):
                    transpose_row(("x", g * G + j), X[:, g * G + j, :])
                pe.wait_ge(bias_ready, 3)

                def project(n):
                    pe.wait_ge(w_split, n + 1)
                    for j in range(G):
                        V.drained(pe, ("x", g * G + j))
                        b = A.fill(pe, ("rows", g, n, j))
                        terms = [(ones[:, :], biasr[:, a, n, :]) for a in range(2)]
                        product(b[:, :], terms + split_terms(tokens(j), chunks(wsplit(n)))).then_inc(A.full, 1)

                def to_heads(ring, n, src, count):
                    A.drained(pe, ("rows", g, n, G - 1))
                    for a in range(count // 4):
                        b = ring.fill(pe, ("heads", g, n, a))
                        for m in range(4):
                            mm = nc.tensor.transpose(b[:, m * P:(m + 1) * P], src[:, 4 * a + m, :, :], ident[:, :])
                        mm.then_inc(ring.full, 1)

                project(0)
                project(2)
                to_heads(A, 0, qkrow, H)
                project(1)
                to_heads(V, 2, vrow, HD)
                to_heads(V, 1, qkrow, H)

                def scores(c):
                    b = C.fill(pe, ("scores", g, c))
                    for s in range(CH):
                        for j in range(G):
                            q = slice(32 * j, 32 * j + HD)
                            mm = nc.tensor.matmul(b[32 * j:32 * j + 32, s * H:(s + 1) * H], qT[q, c * CH + s, :],
                                                  kT[q, c * CH + s, :], start=True, stop=True)
                    mm.then_inc(C.full, 1)

                def values(c):
                    pe.wait_ge(pt_ready, g * NCH + c + 1)
                    b = S.fill(pe, ("values", g, c))
                    for s in range(CH):
                        for j in range(G):
                            q = slice(32 * j, 32 * j + 32)
                            mm = nc.tensor.matmul(b[q, s * HD:(s + 1) * HD], pT[q, c % 2, s, :],
                                                  vT[q, c * CH + s, :], start=True, stop=True)
                    mm.then_inc(S.full, 1)

                A.drained(pe, ("heads", g, 0, H // 4 - 1))
                V.drained(pe, ("heads", g, 1, H // 4 - 1))
                scores(0)
                scores(1)
                for c in range(NCH):
                    if c + 2 < NCH:
                        scores(c + 2)
                    values(c)
                S.drained(pe, ("values", g, NCH - 1))
                for a in range(HD // 4):
                    b = V.fill(pe, ("context", g, a))
                    for m in range(4):
                        mm = nc.tensor.transpose(b[:, m * P:(m + 1) * P], cx[:, :, 4 * a + m], ident[:, :])
                    mm.then_inc(V.full, 1)

            for g in range(2):
                for j in range(G):
                    pe.wait_ge(x_ready, g * G + j + 1)
                    transpose_row(("x1", g * G + j), X[:, g * G + j, :])
                for layer, src in ((0, XT), (1, h1)):
                    pe.wait_ge(k_ready, 1 if layer == 0 else 1 + DC)
                    if layer == 0:
                        V.drained(pe, ("x1", g * G + G - 1))
                    else:
                        pe.wait_ge(h_ready, (2 * g + 1) * DC)
                    for o in range(DC):
                        b = A.fill(pe, ("hidden", g, layer, o))
                        product(b[:, :], [(K[layer][:, c, o * P:(o + 1) * P], src[:, a, c, :]) for c in range(DC) for a in range(2)])\
                            .then_inc(A.full, 1)
                pe.wait_ge(h_ready, (2 * g + 2) * DC)
                pe.wait_ge(k_ready, 1 + 2 * DC)
                for j in range(G):
                    b = V.fill(pe, ("ffn", g * G + j))
                    product(b[:, :], [(h2[:, a, c, j * P:(j + 1) * P], K[2][:, c, :]) for c in range(DC) for a in range(2)])\
                        .then_inc(V.full, 1)

            def stack(name, src):
                for a in range(4):
                    b = A.fill(pe, name + (a,))
                    for m in range(4):
                        pr = 2 * (4 * a + m)
                        mm = nc.tensor.transpose(b[:, m * P:(m + 1) * P], src[:, pr:pr + 2, :], ident[:, :])
                    mm.then_inc(A.full, 1)

            def half(hh):
                return slice(KS * hh, KS * hh + KS)

            def front(i):
                pe.wait_ge(x_ready, T + i + 1)
                transpose_row(("x2", i), X[:, i, :])
                V.drained(pe, ("x2", i))
                for n, ring in ((1, V), (0, V), (2, A)):
                    pe.wait_ge(w_split, 4 + n)
                    b = ring.fill(pe, ("qkv", i, n))
                    product(b[:, :], split_terms(tokens2(0), chunks(wsplit(n)))).then_inc(ring.full, 1)
                pe.wait_ge(ksp_ready, i + 1)
                stack(("kstack", i), ksp)
                pe.wait_ge(qsp_ready, i + 1)
                stack(("qstack", i), qsp[:, i % 2])

            def row_scores(i, f):
                slots, m0 = window(i)
                n = P if i == 0 else 2 * P
                r = half(f % 2)
                b = V.fill(pe, ("rowscores", i, f))[:, :].rearrange("p (a k) -> p a k", a=2)[:, :, 0:n]
                nc.tensor.matmul(b, identb[:, :], maskb[:, m0:m0 + n].rearrange("p (a k) -> p a k", a=1).broadcast_to([P, 2, n]),
                                 start=True, stop=False)
                for m in range(2):
                    pr = 2 * (f // 2) + m
                    mm = nc.tensor.matmul(b[:, m, :], qS[r, pr, :], kS[r, pr, slots, :], start=False, stop=(m == 1))
                mm.then_inc(V.full, 1)

            def key_scores(i, hg):
                r = half(hg % 2)
                for w in range(1 if i == 0 else 2):
                    b = S.fill(pe, ("keyscores", i, hg, w))
                    for m in range(4):
                        pr = 4 * (hg // 2) + m
                        mm = nc.tensor.matmul(b[:, m * P:(m + 1) * P], kS[r, pr, (i - w) % 3, :], qM[r, pr, :],
                                              start=True, stop=True)
                    mm.then_inc(S.full, 1)

            def weigh(i, hg):
                pe.wait_ge(pt_masked, 8 * i + hg + 1)
                if hg == 0 and i >= 1:
                    pe.wait_ge(ctx_ready, 2 * i)
                nw = 1 if i == 0 else 2
                for m in range(4):
                    h = 8 * (hg // 2) + 2 * m + hg % 2
                    for w in range(nw):
                        mm = nc.tensor.matmul(C.banks[h // 16][32 * (h % 4):32 * (h % 4) + 32, (h // 4 % 4) * P:(h // 4 % 4 + 1) * P],
                                              vaug[:, (i - w) % 3, h, :], PT[:, hg % 2, w, m, :],
                                              start=(w == 0), stop=(w == nw - 1))
                mm.then_inc(weighed, 1)

            pe.wait_ge(pads_ready, 5)
            pe.wait_ge(masks_ready, 6)
            front(0)
            A.drained(pe, ("qstack", 0, 3))
            for f in range(H // 2):
                row_scores(0, f)
            for i in range(T):
                if i + 1 < T:
                    front(i + 1)
                pe.wait_ge(max_ready, i + 1)
                stack(("qmstack", i), qsp[:, i % 2])
                A.drained(pe, ("qmstack", i, 3))
                for hg in range(8):
                    key_scores(i, hg)
                    if i + 1 < T:
                        row_scores(i + 1, 2 * hg)
                        row_scores(i + 1, 2 * hg + 1)
                    if hg >= 1:
                        weigh(i, hg - 1)
                weigh(i, 7)
                for a in range(2):
                    pe.wait_ge(ctx_ready, 2 * i + a + 1)
                    b = V.fill(pe, ("context2", i, a))
                    for m in range(4):
                        mm = nc.tensor.transpose(b[:, m * P:(m + 1) * P], cT[:, (4 * a + m) * P:(4 * a + m + 1) * P], ident[:, :])
                    mm.then_inc(V.full, 1)
                V.drained(pe, ("context2", i, 1))
                transpose_row(("co", i), co)
                V.drained(pe, ("co", i))
                pe.wait_ge(w_split, 7)
                b = V.fill(pe, ("wo", i))
                product(b[:, :], split_terms(tokens2(1), chunks(wsplit(3)))).then_inc(V.full, 1)

            acc = banks[4:8]

            for g in range(2):
                for j in range(G):
                    pe.wait_ge(x_ready, 2 * T + g * G + j + 1)
                    transpose_row(("x3", g * G + j), X[:, g * G + j, :])
            pe.wait_ge(gate_ready, 2)
            V.drained(pe, ("x3", T - 1))
            b = V.fill(pe, "logits")
            for t in range(T):
                x3 = [[XT3[t // G][:, a, c, t % G * P:(t % G + 1) * P] for c in range(DC)] for a in range(2)]
                mm = product(b[:, t * E:(t + 1) * E], split_terms(x3, [[gr[:, a, c, :] for c in range(DC)] for a in range(2)]))
            mm.then_inc(V.full, 1)

            def turn(b):
                pe.wait_ge(xblock_in[b % XB_], 16 * (b // XB_ + 1))
                if b == 0:
                    V.drained(pe, "ranks")
                bank = XBank.fill(pe, ("xblock", b))
                for c in range(DC):
                    mm = nc.tensor.transpose(bank[:, c * P:(c + 1) * P], xblock[:, b % XB_, c * P:(c + 1) * P], ident[:, :])
                mm.then_inc(XBank.full, 1)

            def up(k):
                if ITEMS[k][0] == "shared":
                    _, g, e = ITEMS[k]
                    if g == 0:
                        pe.wait_ge(we_split, e + 1)
                    x3 = [[XT3[g][:, a, c, :] for c in range(DC)] for a in range(2)]
                    for part in range(2):
                        bank = A.fill(pe, ("up", k, part))
                        w = [[m[:, c, part, :] for c in range(DC)] for m, _ in halves(e)]
                        product(bank[:, :], split_terms(w, x3)).then_inc(A.full, 1)
                else:
                    b = ITEMS[k][1]
                    pe.wait_ge(wblock_in[b % WB], 16 * (b // WB + 1))
                    XBank.drained(pe, ("xblock", b))
                    bank = A.fill(pe, ("up", k, 0))
                    w = wblock[b % WB][:, 0:DC * 2 * P].rearrange("p (c g n) -> p c g n", c=DC, g=2)
                    for part in range(2):
                        mm = product(bank[:, part * P:(part + 1) * P], [(w[:, c, part, :], xbT[:, b % 2, c, :]) for c in range(DC)])
                    mm.then_inc(A.full, 1)

            def down(k):
                if ITEMS[k][0] == "shared":
                    _, g, e = ITEMS[k]
                    pe.wait_ge(act_ready, g * SE + e + 1)
                    if g == 1 and e == 0:
                        pe.wait_ge(acc_done, G)
                    (_, dh), (_, dl) = halves(e)
                    hi, lo = (ah[:, k % 2, a, :] for a in range(2))
                    for j in range(G):
                        for n, (l, r) in enumerate(((hi, dh), (hi, dl), (lo, dh))):
                            mm = nc.tensor.matmul(acc[j][:, :], l[:, j * P:(j + 1) * P], r,
                                                  start=(e == 0 and n == 0), stop=(e == SE - 1 and n == 2))
                    mm.then_inc(down_done, 1)
                else:
                    b = ITEMS[k][1]
                    A.drained(pe, ("up", k, 0))
                    bank = YBank.fill(pe, ("yblock", b))
                    product(bank[:, :], [(ab[:, k % 2, :], wblock[b % WB][:, DC * 2 * P:WCOLS])]).then_inc(down_done, 1)

            for k in range(len(ITEMS)):
                if k + 1 < len(ITEMS) and ITEMS[k + 1][0] == "block":
                    turn(ITEMS[k + 1][1])
                up(k)
                if k == 0:
                    pe.wait_ge(picked_ready, 2)
                    b = V.fill(pe, "ranks")[:, 0:(T + 1) * E]
                    nc.tensor.matmul(b, before[:, :], picked[:, :, :], start=True, stop=False)
                    for t in range(T):
                        nc.tensor.matmul(b[:, (t + 1) * E:(T + 1) * E], onesb[:, :], picked[:, t:t + 1, :].broadcast_to([P, T - t, E]),
                                         start=False, stop=False)
                    nc.tensor.matmul(b, onesb[:, :], picked[:, T:T + 1, :].broadcast_to([P, T + 1, E]), start=False, stop=True)\
                        .then_inc(V.full, 1)
                if k >= 1:
                    down(k - 1)
            down(len(ITEMS) - 1)

        @block.vector
        def _(v):
            steps = [0]

            def own(ins):
                ins.then_inc(dve, 1)
                steps[0] += 1
                v.wait_ge(dve, steps[0])

            def tt(o, a, b, op):
                return nc.vector.tensor_tensor(o, a, b, op)

            def tile_parts(j):
                return [XT[:, a, :, j * P:(j + 1) * P] for a in range(2)]

            def split_xt(name, parts):
                b = V.take(v, name)[:, :].rearrange("p (c n) -> p c n", c=DC)
                hi, lo = parts
                own(nc.vector.tensor_copy(hi, b))
                tt(lo, b, hi.bitcast(F32), ALU.subtract).then_inc(V.free, 1)

            def stats(t):
                own(nc.vector.bn_stats(st6[:, t, :], X[:, t, :]))
                return nc.vector.bn_aggr(mv[:, t, :], st6[:, t, :])

            def normalise(tiles, batch):
                v.wait_ge(std_ready, batch + 1)
                own(nc.vector.reciprocal(rstd[:, tiles], std[:, tiles]))
                for t in range(tiles.start, tiles.stop):
                    nc.vector.tensor_scalar(X[:, t, :], X[:, t, :], mv[:, t, 0:1], rstd[:, t:t + 1],
                                            ALU.subtract, ALU.mult).then_inc(x_ready, 1)

            def low_part(n, slot, raw):
                v.wait_ge(w_high, n + 1)
                tt(W[:, 2 * slot + 1, :], raw, W[:, 2 * slot, :].bitcast(F32), ALU.subtract).then_inc(w_split, 1)

            nc.vector.memset(epst[:, :], EPS).then_inc(small_ready, 1)
            v.wait_ge(bias_in, 16)
            nc.vector.tensor_copy(biasr[:, 0, :, :], biasf).then_inc(bias_ready, 1)
            v.wait_ge(bias_ready, 1)
            tt(biasr[:, 1, :, :], biasf, biasr[:, 0, :, :].bitcast(F32), ALU.subtract).then_inc(bias_ready, 1)
            nc.vector.memset(ones[:, :].bitcast(F32), 1.0).then_inc(bias_ready, 1)

            for g in range(2):
                for j in range(G):
                    split_xt(("x", g * G + j), tile_parts(j))
                if g == 0:
                    for n in range(3):
                        low_part(n, n, raw_a[n])
                    v.wait_ge(k_in[0], 16)
                    nc.vector.tensor_scalar(K[0][:, :, :], kraw[:, :, :], 2.0, -1.0, ALU.mult, ALU.add).then_inc(k_ready, 1)
                    v.wait_ge(consts_in, CONSTS)
                    for n in (1, 2):
                        v.wait_ge(k_in[n], 16)
                        for c in range(DC):
                            nc.vector.tensor_scalar(K[n][:, c, :], kraw[:, c, :], factor[:, 0, c:c + 1], factor[:, 1, c:c + 1],
                                                    ALU.mult, ALU.subtract).then_inc(k_ready, 1)
                for n, dst, count in ((2, vT, HD), (1, kT, H)):
                    for a in range(count // 4):
                        b = V.take(v, ("heads", g, n, a))
                        nc.vector.tensor_copy(dst[:, :, 4 * a:4 * a + 4].rearrange("p s h -> p h s"),
                                              b[:, :].rearrange("p (h s) -> p h s", h=4)).then_inc(V.free, 1)

                def shift(c):
                    if c >= 1:
                        C.drained(v, ("scores", g, c - 1))
                    b = C.take(v, ("scores", g, c))[:, :].rearrange("p (s t) -> p s t", t=H)
                    own(nc.vector.tensor_reduce(small[:, 0, :], b, AX, ALU.max))
                    tt(sc[:, c % 2], b, small[:, 0, :].rearrange("p (s a) -> p s a", a=1).broadcast_to([P, CH, H]), ALU.subtract)\
                        .then_inc(C.free, 1)

                def weights(c):
                    v.wait_ge(expd, g * NCH + c + 1)
                    own(nc.vector.tensor_reduce(small[:, 1, :], sc[:, c % 2], AX, ALU.add))
                    if c >= 2:
                        S.drained(v, ("values", g, c - 2))
                    own(nc.vector.reciprocal(small[:, 2 + c % 2, :], small[:, 1, :]))
                    nc.vector.transpose(pT[:, c % 2], sc[:, c % 2]).then_inc(pt_ready, 1)

                def contexts(c):
                    b = S.take(v, ("values", g, c))[:, 0:CH * HD].rearrange("p (s d) -> p s d", d=HD)
                    tt(cx[:, c * CH:(c + 1) * CH, :], b,
                       small[:, 2 + c % 2, :].rearrange("p (s a) -> p s a", a=1).broadcast_to([P, CH, HD]), ALU.mult).then_inc(S.free, 1)

                shift(0)
                for c in range(NCH):
                    if c + 1 < NCH:
                        shift(c + 1)
                    weights(c)
                    if c >= 1:
                        contexts(c - 1)
                contexts(NCH - 1)
                tiles = slice(g * G, g * G + G)
                for a in range(HD // 4):
                    b = V.take(v, ("context", g, a))[:, :].rearrange("p (m j h) -> p j h m", m=4, j=G)
                    for j in range(G):
                        xv = X[:, g * G + j, :].rearrange("p (h d) -> p h d", d=HD)[:, :, 4 * a:4 * a + 4]
                        ins = tt(xv, xv, b[:, j], ALU.add)
                        if j < G - 1:
                            ins.then_inc(dve, 1)
                            steps[0] += 1
                    ins.then_inc(V.free, 1)
                V.drained(v, ("context", g, HD // 4 - 1))
                for t in range(tiles.start, tiles.stop):
                    ins = stats(t)
                    if t < tiles.stop - 1:
                        ins.then_inc(dve, 1)
                        steps[0] += 1
                ins.then_inc(stats_ready, 1)
                normalise(tiles, g)

            for g in range(2):
                for j in range(G):
                    split_xt(("x1", g * G + j), tile_parts(j))
                for layer, dst in ((0, h1), (1, h2)):
                    for o in range(DC):
                        n = (2 * g + layer) * DC + o
                        A.drained(v, ("hidden", g, layer, o))
                        tt(dst[:, 1, o, :], hf[:, o % 2, :], dst[:, 0, o, :].bitcast(F32), ALU.subtract).then_inc(h_ready, 1)
                for j in range(G):
                    t = g * G + j
                    b = V.take(v, ("ffn", t))
                    nc.vector.scalar_tensor_tensor(X[:, t, :], b[:, :], scales[:, 2:3], X[:, t, :], ALU.mult, ALU.add)\
                        .then_inc(V.free, 1)
                    V.drained(v, ("ffn", t))
                    ins = stats(t)
                    if j < G - 1:
                        ins.then_inc(dve, 1)
                        steps[0] += 1
                ins.then_inc(stats_ready, 1)
                normalise(slice(g * G, g * G + G), 2 + g)
                if g == 0:
                    for n in range(3):
                        low_part(3 + n, n, raw_c[n])
            low_part(6, 3, raw_c[3])

            def rotate(i, n, dst, done):
                name = ("qkv", i, n)
                b = V.take(v, name)[:, :].rearrange("p (h d) -> p h d", d=HD)
                o = dst.rearrange("p (h d) -> p h d", d=HD)
                r = rt.rearrange("p (h d) -> p h d", d=HD)
                cos, sin = (rope[:, i, a:a + 1, :].broadcast_to([P, H, HD]) for a in range(2))
                k = HD // 2
                if n == 0:
                    v.wait_ge(k_turned, i + 1)
                elif i >= 1:
                    v.wait_ge(q_turned, i)
                tt(r, b, cos, ALU.mult).then_inc(dve, 1)
                tt(o[:, :, 0:k], b[:, :, k:HD], sin[:, :, 0:k], ALU.mult).then_inc(dve, 1)
                steps[0] += 2
                tt(o[:, :, k:HD], b[:, :, 0:k], sin[:, :, k:HD], ALU.mult).then_inc(V.free, 1)
                V.drained(v, name)
                tt(dst, dst, rt, ALU.add).then_inc(done, 1)

            def front(i):
                split_xt(("x2", i), [XT2[:, 0, a] for a in range(2)])
                rotate(i, 1, kf, k_turned)
                rotate(i, 0, qf, q_turned)
                q = qsp[:, i % 2]
                v.wait_ge(k_high, i + 1)
                tt(ksp[:, :, HD:2 * HD], kf.rearrange("p (h d) -> p h d", d=HD), ksp[:, :, 0:HD], ALU.subtract).then_inc(ksp_ready, 1)
                nc.vector.memset(q[:, :, 3 * HD:3 * HD + 2], 0.0).then_inc(dve, 1)
                steps[0] += 1
                v.wait_ge(q_high, i + 1)
                tt(q[:, :, 2 * HD:3 * HD].bitcast(F32R), qf.rearrange("p (h d) -> p h d", d=HD), q[:, :, 0:HD], ALU.subtract)\
                    .then_inc(qsp_ready, 1)

            def row_maxima(i):
                n = P if i == 0 else 2 * P
                for f in range(H // 2):
                    b = V.take(v, ("rowscores", i, f))[:, :].rearrange("p (a k) -> p a k", a=2)[:, :, 0:n]
                    h = 4 * (f // 2) + f % 2
                    nc.vector.tensor_reduce(hmax[:, h:h + 3:2], b, AX, ALU.max).then_inc(V.free, 1)
                V.drained(v, ("rowscores", i, H // 2 - 1))
                m = hmax[:, :].rearrange("p (h a) -> p h a", a=1)
                q = qsp[:, i % 2]
                own(nc.vector.tensor_copy(q[:, :, 3 * HD:3 * HD + 1].bitcast(F32R), m))
                tt(q[:, :, 3 * HD + 1:3 * HD + 2], m, q[:, :, 3 * HD:3 * HD + 1], ALU.subtract).then_inc(max_ready, 1)

            def shared_low(e):
                v.wait_ge(we_high, e + 1)
                tt(W[:, 2 * e + 1, 0:WCOLS], wblock[e % 2], W[:, 2 * e, 0:WCOLS].bitcast(F32), ALU.subtract).then_inc(we_split, 1)

            front(0)
            row_maxima(0)
            for i in range(T):
                if i + 1 < T:
                    front(i + 1)
                    row_maxima(i + 1)
                else:
                    for e in range(SE - 1):
                        shared_low(e)
                v.wait_ge(weighed, 8 * (i + 1))
                for a in range(2):
                    nc.vector.tensor_copy(cT[:, a * 512:(a + 1) * 512], C.banks[a][:, :]).then_inc(ctx_ready, 1)
                for a in range(2):
                    b = V.take(v, ("context2", i, a))[:, :].rearrange("p (h r) -> p h r", r=32)
                    s = hsum[:, a, :].rearrange("p (h r) -> p h r", r=1)
                    own(nc.vector.reciprocal(s, b[:, :, HD:HD + 1]))
                    tt(co[:, a * 256:(a + 1) * 256].rearrange("p (h d) -> p h d", d=HD), b[:, :, 0:HD], s.broadcast_to([P, 16, HD]),
                       ALU.mult).then_inc(V.free, 1)
                split_xt(("co", i), [XT2[:, 1, a] for a in range(2)])
                b = V.take(v, ("wo", i))
                tt(X[:, i, :], X[:, i, :], b[:, :], ALU.add).then_inc(V.free, 1)
                V.drained(v, ("wo", i))
                ins = stats(i)
                if i < T - 1:
                    ins.then_inc(dve, 1)
                    steps[0] += 1
            ins.then_inc(stats_ready, 1)
            normalise(slice(0, T), 4)

            v.wait_ge(gate_in, 32)
            gv = gates.rearrange("p (c e) -> p c e", c=DC)
            nc.vector.tensor_copy(gr[:, 0], gv).then_inc(gate_ready, 1)
            v.wait_ge(gate_ready, 1)
            tt(gr[:, 1], gv, gr[:, 0].bitcast(F32), ALU.subtract).then_inc(gate_ready, 1)
            nc.vector.memset(picked[:, T, :], 0.0).then_inc(picked_ready, 1)
            for t in range(T):
                split_xt(("x3", t), [XT3[t // G][:, a, :, t % G * P:(t % G + 1) * P] for a in range(2)])

            def spread(vec, axis, shape):
                form = "p (a n) -> p a n" if axis == 1 else "p (n a) -> p n a"
                return vec.rearrange(form, a=1).broadcast_to(shape)

            b = V.take(v, "logits")
            nc.vector.tensor_copy(lg, b[:, 0:T * E].rearrange("p (t e) -> p t e", e=E)).then_inc(V.free, 1)
            V.drained(v, "logits")

            def best(src, one, mx):
                own(nc.vector.tensor_reduce(tiny[:, mx, :], src, AX, ALU.max))
                own(tt(tmp, src, spread(tiny[:, mx, :], 2, [P, T, E]), ALU.is_equal))
                own(tt(tmp, tmp, spread(rank, 1, [P, T, E]), ALU.mult))
                own(nc.vector.tensor_reduce(tiny[:, 2, :], tmp, AX, ALU.max))
                own(tt(one, tmp, spread(tiny[:, 2, :], 2, [P, T, E]), ALU.is_equal))

            best(lg, oh[:, 0], 0)
            own(nc.vector.scalar_tensor_tensor(l2, oh[:, 0], -BIG, lg, ALU.mult, ALU.add))
            best(l2, oh[:, 1], 1)
            tt(picked[:, 0:T, :], oh[:, 0], oh[:, 1], ALU.add).then_inc(picked_ready, 1)
            tt(tiny[:, 3, :], tiny[:, 1, :], tiny[:, 0, :], ALU.subtract).then_inc(logits_shifted, 1)
            def place():
                b = V.take(v, "ranks")
                nc.vector.tensor_copy(ranks, b[:, 0:(T + 1) * E].rearrange("p (t e) -> p t e", e=E)).then_inc(V.free, 1)
                V.drained(v, "ranks")
                own(tt(over, spread(ranks[:, T, :], 2, [P, E, T]), spread(full, 1, [P, E, T]), ALU.is_gt))
                own(nc.vector.tensor_reduce(nblocks, over, AX, ALU.add))
                own(tt(firsts, first.rearrange("p (e f) -> p e f", f=E), spread(nblocks, 1, [P, E, E]), ALU.mult))
                own(nc.vector.tensor_reduce(base, firsts, AX, ALU.add))
                own(nc.vector.scalar_tensor_tensor(ranks[:, 0:T, :], spread(base, 1, [P, T, E]), float(P), ranks[:, 0:T, :], ALU.mult, ALU.add))
                for k in range(TOP):
                    own(tt(oslot[:, k], oh[:, k], ranks[:, 0:T, :], ALU.mult))
                own(nc.vector.tensor_reduce(slotf, oslot, AX, ALU.add))
                nc.vector.tensor_copy(slots[:, :, :], slotf).then_inc(slots_ready, 1)
                own(tt(ends, base, nblocks, ALU.add))
                own(tt(passed, spread(ends[0:1, :], 1, [1, NB, E]), spread(block_no[0:1, :], 2, [1, NB, E]), ALU.is_le))
                own(nc.vector.tensor_reduce(ownf, passed, AX, ALU.add))
                nc.vector.tensor_scalar(owner[0:1, 0:NB], ownf, float(E - 1), None, ALU.min).then_inc(owner_ready, 1)
                v.wait_ge(logits_exp, 1)
                own(nc.vector.tensor_scalar(tiny[:, 4, :], tiny[:, 3, :], 1.0, None, ALU.add))
                own(nc.vector.reciprocal(share[:, 0, :], tiny[:, 4, :]))
                own(tt(share[:, 1, :], tiny[:, 3, :], share[:, 0, :], ALU.mult))

            def collect(g):
                for j in range(G):
                    t = g * G + j
                    tt(X[:, t, :], X[:, t, :], banks[4 + j][:, :], ALU.add).then_inc(acc_done, 1)

            def combine(t):
                v.wait_ge(tile_gathered[t], 16 * TOP)
                for k in range(TOP):
                    nc.vector.scalar_tensor_tensor(X[:, t, :], gathered[:, (TOP * t + k) % YG, :], share[:, k, t:t + 1], X[:, t, :],
                                                   ALU.mult, ALU.add).then_inc(combined, 1)
                    v.wait_ge(combined, TOP * t + k + 1)

            nshared = 0
            for k, item in enumerate(ITEMS):
                if item == ("shared", 0, SE - 1):
                    shared_low(SE - 1)
                if k + 1 < len(ITEMS) and ITEMS[k + 1][0] == "block":
                    b = ITEMS[k + 1][1]
                    bank = XBank.take(v, ("xblock", b))[:, :].rearrange("p (c n) -> p c n", c=DC)
                    if b >= 2:
                        v.wait_ge(down_done, item_of[b - 2] + 1)
                    nc.vector.tensor_copy(xbT[:, b % 2], bank).then_inc(XBank.free, 1)
                v.wait_ge(silu_done, k + 1)
                if item[0] == "shared":
                    bank = A.filled(v, ("up", k, 1))
                    if nshared >= 1:
                        v.wait_ge(act_ready, nshared)
                    nshared += 1
                    tt(ac, sg[:, k % 2, :], bank[:, :], ALU.mult).then_inc(A.free, 2)
                    A.drained(v, ("up", k, 1))
                    if k >= 2:
                        v.wait_ge(down_done, k - 1)
                    own(nc.vector.tensor_copy(ah[:, k % 2, 0, :], ac))
                    tt(ah[:, k % 2, 1, :], ac, ah[:, k % 2, 0, :].bitcast(F32), ALU.subtract).then_inc(act_ready, 1)
                else:
                    bank = A.filled(v, ("up", k, 0))
                    v.wait_ge(down_done, k - 1)
                    tt(ab[:, k % 2, :], sg[:, k % 2, 0:P], bank[:, P:2 * P], ALU.mult).then_inc(A.free, 1)
                if k == 0:
                    place()
                if item == ("block", 3):
                    v.wait_ge(scattered, 16 * TOP * T)
                    v.wait_ge(down_done, SE)
                    collect(0)
            for g in range(2):
                for j in range(G):
                    combine(g * G + j)
                if g == 1:
                    v.wait_ge(down_done, len(ITEMS))
                    collect(1)
                    v.wait_ge(acc_done, T)
                for j in range(G):
                    t = g * G + j
                    ins = stats(t)
                    if j < G - 1:
                        ins.then_inc(dve, 1)
                        steps[0] += 1
                ins.then_inc(stats_ready, 1)
                normalise(slice(g * G, g * G + G), 5 + g)

        @block.scalar
        def _(s):
            steps = [0]

            def act(o, i, func, **kw):
                return nc.scalar.activation(o, i, func, **kw)

            def high_part(n, slot, raw, arrived):
                s.wait_ge(arrived, 16)
                act(W[:, 2 * slot, :], raw, ACT.Copy).then_inc(w_high, 1)

            def roots(tiles, batch):
                s.wait_ge(stats_ready, batch + 1)
                act(std[:, tiles], mv[:, tiles, 1], ACT.Sqrt, bias=epst[:, 0:1]).then_inc(std_ready, 1)

            for n in range(3):
                high_part(n, n, raw_a[n], wa_in[n])
            s.wait_ge(small_ready, 1)
            for g in range(2):
                def rows_out(n):
                    for j in range(G):
                        b = A.take(s, ("rows", g, n, j))
                        if n == 2:
                            act(vrow[:, :, j, :], b[:, :].rearrange("p (h d) -> p d h", d=HD), ACT.Copy).then_inc(A.free, 1)
                        else:
                            act(qkrow[:, :, j, 0:HD], b[:, :].rearrange("p (h d) -> p h d", d=HD), ACT.Copy).then_inc(A.free, 1)

                if g == 0:
                    s.wait_ge(pads_ready, 1)
                rows_out(0)
                if g == 1:
                    V.drained(s, ("context", 0, HD // 4 - 1))
                rows_out(2)
                s.wait_ge(w_split, 3)
                for a in range(H // 4):
                    b = A.take(s, ("heads", g, 0, a))
                    act(qT[:, :, 4 * a:4 * a + 4].rearrange("p s h -> p h s"), b[:, :].rearrange("p (h s) -> p h s", h=4),
                        ACT.Copy).then_inc(A.free, 1)
                rows_out(1)
                for c in range(NCH):
                    C.drained(s, ("scores", g, c))
                    act(sc[:, c % 2], sc[:, c % 2], ACT.Exp, scale=SCALE).then_inc(expd, 1)
                roots(slice(g * G, g * G + G), g)

            for g in range(2):
                if g == 1:
                    for n in range(3):
                        high_part(3 + n, n, raw_c[n], wc_in[n])
                for layer, dst in ((0, h1), (1, h2)):
                    for o in range(DC):
                        n = (2 * g + layer) * DC + o
                        b = A.take(s, ("hidden", g, layer, o))
                        if n >= 2:
                            s.wait_ge(h_ready, n - 1)
                        act(dst[:, 0, o, :], b[:, :], ACT.Relu, scale=scales[:, layer:layer + 1]).then_inc(act_step, 1)
                        act(hf[:, o % 2, :], b[:, :], ACT.Relu, scale=scales[:, layer:layer + 1]).then_inc(A.free, 1)
                roots(slice(g * G, g * G + G), 2 + g)
            high_part(6, 3, raw_c[3], wc_in[3])

            def front(i):
                q = qsp[:, i % 2].rearrange("p h (a r) -> p h a r", r=HD)
                k = ksp.rearrange("p h (a r) -> p h a r", r=HD)
                s.wait_ge(k_turned, i + 1)
                act(k[:, :, 0:3:2, :].bitcast(F32R), kf.rearrange("p (h a r) -> p h a r", a=1, r=HD).broadcast_to([P, H, 2, HD]), ACT.Copy)\
                    .then_inc(k_high, 1)
                s.wait_ge(q_turned, i + 1)
                act(q[:, :, 0:2, :].bitcast(F32R), qf.rearrange("p (h a r) -> p h a r", a=1, r=HD).broadcast_to([P, H, 2, HD]), ACT.Copy)\
                    .then_inc(q_high, 1)
                b = A.take(s, ("qkv", i, 2))
                act(vaug[:, i % 3, :, 0:HD], b[:, :].rearrange("p (h d) -> p h d", d=HD), ACT.Copy).then_inc(A.free, 1)
                for a in range(4):
                    b = A.take(s, ("kstack", i, a))
                    act(kS[:, 4 * a:4 * a + 4, i % 3, :], b[:, :].rearrange("p (m k) -> p m k", m=4), ACT.Copy).then_inc(A.free, 1)
                for a in range(4):
                    b = A.take(s, ("qstack", i, a))
                    act(qS[:, 4 * a:4 * a + 4, :], b[:, :].rearrange("p (m k) -> p m k", m=4), ACT.Copy).then_inc(A.free, 1)

            def shared_high(e):
                s.wait_ge(shared_in[e % 2], 16 * (e // 2 + 1))
                act(W[:, 2 * e, 0:WCOLS], wblock[e % 2], ACT.Copy).then_inc(we_high, 1)

            s.wait_ge(pads_ready, 5)
            s.wait_ge(zeroed, 16 * ((NB + 3) // 4))
            front(0)
            for i in range(T):
                if i + 1 < T:
                    front(i + 1)
                for a in range(4):
                    b = A.take(s, ("qmstack", i, a))
                    act(qM[:, 4 * a:4 * a + 4, :], b[:, :].rearrange("p (m k) -> p m k", m=4), ACT.Copy).then_inc(A.free, 1)
                for hg in range(8):
                    n = 8 * i + hg
                    if n >= 2:
                        s.wait_ge(weighed, n - 1)
                    for w in range(1 if i == 0 else 2):
                        b = S.take(s, ("keyscores", i, hg, w))
                        act(PT[:, hg % 2, w], b[:, :].rearrange("p (m q) -> p m q", m=4), ACT.Exp, scale=SCALE).then_inc(S.free, 1)
                    if i == T - 1 and hg % 2 == 1 and hg // 2 < SE - 1:
                        shared_high(hg // 2)
            roots(slice(0, T), 4)

            V.drained(s, ("wo", T - 1))
            shared_high(SE - 1)
            s.wait_ge(logits_shifted, 1)
            act(tiny[:, 3, :], tiny[:, 3, :], ACT.Exp).then_inc(logits_exp, 1)
            for k, item in enumerate(ITEMS):
                bank = A.filled(s, ("up", k, 0))
                n = D if item[0] == "shared" else P
                if k >= 2:
                    A.drained(s, last_fill(k - 2))
                act(sg[:, k % 2, 0:n], bank[:, 0:n], ACT.Silu).then_inc(silu_done, 1)
                if k >= 1 and ITEMS[k - 1][0] == "block":
                    b = ITEMS[k - 1][1]
                    s.wait_ge(down_done, k)
                    if b >= YB_:
                        s.wait_ge(yblock_out[b % YB_], 16 * (b // YB_))
                    act(yblock[:, b % YB_, :], YBank.banks[0][:, :], ACT.Copy).then_inc(YBank.free, 1)
            for g in range(2):
                roots(slice(g * G, g * G + G), 5 + g)

        @block.gpsimd
        def _(p):
            nc.gpsimd.memset(ident[:, :], 0.0).then_inc(ident_ready, 1)
            p.wait_ge(ident_ready, 1)
            nc.gpsimd.affine_select(out=ident[:, :], in_=ident[:, :], compare_op=ALU.not_equal, fill=1.0, base=0,
                                    pattern=[[-1, P]], channel_multiplier=1).then_inc(ident_ready, 1)
            nc.gpsimd.memset(qkrow[:, :, :, HD:2 * HD], 0.0).then_inc(pads_ready, 1)
            nc.gpsimd.memset(zeros, 0.0).then_inc(zeros_ready, 1)
            nc.gpsimd.memset(maskb[:, :], 0.0).then_inc(masks_ready, 1)
            nc.gpsimd.memset(identb[:, :], 0.0).then_inc(masks_ready, 1)
            p.wait_ge(masks_ready, 2)
            nc.gpsimd.affine_select(out=identb[:, :], in_=identb[:, :], compare_op=ALU.not_equal, fill=1.0, base=0,
                                    pattern=[[-1, P]], channel_multiplier=1).then_inc(masks_ready, 1)
            for k, (base, step) in enumerate(((0, -1), (-1, 1), (0, -1))):
                m = maskb[:, k * P:(k + 1) * P]
                nc.gpsimd.affine_select(out=m, in_=m, compare_op=ALU.is_ge, fill=-BIG, base=base,
                                        pattern=[[step, P]], channel_multiplier=-step).then_inc(masks_ready, 1)
            nc.gpsimd.memset(onesb[:, :], 1.0).then_inc(pool, 1)
            p.wait_ge(pool, 1)
            nc.gpsimd.affine_select(out=before[:, :], in_=onesb[:, :], compare_op=ALU.is_ge, fill=0.0, base=-1,
                                    pattern=[[1, P]], channel_multiplier=-1).then_inc(pool, 1)
            p.wait_ge(w_split, 6)
            nc.gpsimd.memset(qsp[:, :, :, 3 * HD:KS], 0.0).then_inc(pads_ready, 1)
            nc.gpsimd.memset(ksp[:, :, 3 * HD:3 * HD + 2], -1.0).then_inc(pads_ready, 1)
            nc.gpsimd.memset(ksp[:, :, 3 * HD + 2:KS], 0.0).then_inc(pads_ready, 1)
            nc.gpsimd.memset(vaug[:, :, :, HD + 1:32], 0.0).then_inc(pool, 1)
            nc.gpsimd.memset(vaug[:, :, :, HD:HD + 1], 1.0).then_inc(pads_ready, 1)
            for i in range(T):
                for hg in range(8):
                    nw = 1 if i == 0 else 2
                    for w in range(nw):
                        S.drained(p, ("keyscores", i, hg, w))
                        pt = PT[:, hg % 2, w]
                        if w == 0:
                            ins = nc.gpsimd.affine_select(out=pt, in_=pt, compare_op=ALU.is_ge, fill=0.0, base=0,
                                                          pattern=[[0, 4], [1, P]], channel_multiplier=-1)
                        else:
                            ins = nc.gpsimd.affine_select(out=pt, in_=pt, compare_op=ALU.is_ge, fill=0.0, base=-1,
                                                          pattern=[[0, 4], [-1, P]], channel_multiplier=1)
                        ins.then_inc(pt_masked if w == nw - 1 else pool, 1)
            p.wait_ge(zeroed, 16 * ((NB + 3) // 4))
            p.wait_ge(slots_ready, 1)
            for t in range(T):
                for k in range(TOP):
                    nc.gpsimd.indirect_dma_start(xs, bass.IndirectOffsetOnAxis(slots[:, k, t:t + 1], 0), X[:, t, :], None).then_inc(scattered, 16)
            for b in range(NB):
                YBank.drained(p, ("yblock", b))
                nc.gpsimd.dma_start(ys[b * P:(b + 1) * P, :], yblock[:, b % YB_, :]).then_inc(yblock_out[b % YB_], 16)
            for r in range(YB_):
                p.wait_ge(yblock_out[r], 16 * len(range(r, NB, YB_)))
            for t in range(T):
                if TOP * t + TOP > YG:
                    p.wait_ge(combined, TOP * t + TOP - YG)
                for k in range(TOP):
                    nc.gpsimd.indirect_dma_start(gathered[:, (TOP * t + k) % YG, :], None, ys,
                                                 bass.IndirectOffsetOnAxis(slots[:, k, t:t + 1], 0)).then_inc(tile_gathered[t], 16)


def _constants(np):
    inv = (1.0 / np.power(np.float32(10000.0), np.arange(0, HD, 2, dtype=np.float32) / np.float32(HD))).astype(np.float32)
    freqs = np.arange(T * P, dtype=np.float32)[:, None] * inv[None, :]
    cos, sin = np.cos(freqs), np.sin(freqs)
    f = np.where(np.arange(D) < round(D * 0.8), 2.0, 2.0 * -0.8 / (1.0 - 0.8)).astype(np.float32).reshape(DC, P).T
    e = np.arange(E)
    table = np.concatenate([E - e, (e[None, :] < e[:, None]).reshape(-1), P * np.arange(T), np.arange(NB)])
    tables = {
        "rope": np.stack([np.concatenate([cos, cos], 1), np.concatenate([-sin, sin], 1)], 1),
        "factor": np.stack([2 * f, f], 1),
        "table": np.broadcast_to(table, (P, TABLE)),
    }
    return {k: np.ascontiguousarray(t, dtype=np.float32) for k, t in tables.items()}


def kernel(**inputs):
    import numpy as np
    import concourse.bacc as _bacc
    from concourse import mybir as _mybir
    from concourse.bass_utils import run_bass_kernel_spmd as _run

    def by_partition(gate_up, down):
        n = gate_up.shape[0]
        gu = gate_up.reshape(n, 2, P, DC, P).transpose(0, 4, 3, 1, 2).reshape(n, P, DC * 2 * P)
        return np.concatenate([gu, down.transpose(0, 2, 1)], axis=2)

    a = {k: np.asarray(v) for k, v in inputs.items()}
    lay = {
        "x": a["L0_attn_hidden_states"][0],
        "wq": a["L0_attn_wq"].T, "wk": a["L0_attn_wk"].T, "wv": a["L0_attn_wv"].T,
        "bias": np.stack([a["L0_attn_bq"], a["L0_attn_bk"], a["L0_attn_bv"]]),
        "k0": a["L0_ffn_k0"], "k1": a["L0_ffn_k1"], "k2": a["L0_ffn_k2"],
        "s0": a["L0_ffn_s0"].reshape(1, 1), "s1": a["L0_ffn_s1"].reshape(1, 1), "s2": a["L0_ffn_s2"].reshape(1, 1),
        "aq": a["L1_attn_Wq"].T, "ak": a["L1_attn_Wk"].T, "av": a["L1_attn_Wv"].T, "ao": a["L1_attn_Wo"].T,
        "gate": a["L1_ffn_gate_w"].T,
        "experts": by_partition(a["L1_ffn_w_gate_up"].reshape(E, 2, P, D), a["L1_ffn_w_down"]),
        "shared": by_partition(a["L1_ffn_shared_w_gate_up"].reshape(2, SE, P, D).transpose(1, 0, 2, 3),
                               a["L1_ffn_shared_w_down"].reshape(D, SE, P).transpose(1, 0, 2)),
    }
    nc = _bacc.Bacc("TRN2", target_bir_lowering=False, num_devices=1)
    arrays, args = {}, []
    for name, array in [*lay.items(), *_constants(np).items()]:
        array = np.ascontiguousarray(array)
        arrays[f"in_{name}_dram"] = array
        args.append(nc.dram_tensor(f"in_{name}_dram", array.shape, _mybir.dt.from_np(array.dtype), kind="ExternalInput").ap())
    args.append(nc.dram_tensor("out_0_dram", (T * P, D), _mybir.dt.from_np(np.dtype("float32")), kind="ExternalOutput").ap())
    for name in ("slots_in", "slots_out"):
        args.append(nc.dram_tensor(name, (NB * P, D), _mybir.dt.from_np(np.dtype("float32")), kind="Internal").ap())
    build(nc, *args)
    r = _run(nc, [arrays], core_ids=[0])
    return r.results[0]["out_0_dram"].reshape(1, T * P, D)
```

```python
from contextlib import ExitStack

import concourse.bass as bass
from concourse import mybir

F32 = mybir.dt.float32
F32R = mybir.dt.float32r
BF16 = mybir.dt.bfloat16
U8 = mybir.dt.uint8
U32 = mybir.dt.uint32
I32 = mybir.dt.int32
ALU = mybir.AluOpType
ACT = mybir.ActivationFunctionType
AX = mybir.AxisListType.X

P = 128
D = 512
DC = D // P
T = 1024 // P
G = 4
H = 32
HD = D // H
KS = 64
E = 16
SE = 4
TOP = 2
NB = T * TOP + E - 1
WBUFS, XBUFS, YBUFS = 6, 4, 3
GBUFS = 11
EPS = 1e-5
SCALE = HD ** -0.5
CONSTS = 5 * 16
BIG = 1e30
CH = 16
NCH = P // CH
AHEAD = 2
WCOLS = DC * 2 * P + D
TABLE = E + E * E + T + NB

ITEMS = ([("shared", 0, e) for e in range(SE)] + [("shared", 1, 0)] + [("block", b) for b in range(NB - 8)]
         + [("shared", 1, 1)] + [("block", b) for b in range(NB - 8, NB)] + [("shared", 1, e) for e in range(2, SE)])
LAST = ITEMS.index(("block", NB - 1))


class Ring:

    def __init__(self, banks, full, free):
        self.banks, self.full, self.free = banks, full, free
        self.number, self.taken = {}, 0

    def fill(self, pe, name):
        n, size = len(self.number), len(self.banks)
        assert name not in self.number
        self.number[name] = n
        if n >= size:
            pe.wait_ge(self.free, n - size + 1)
        return self.banks[n % size]

    def filled(self, engine, name):
        n = self.number[name]
        engine.wait_ge(self.full, n + 1)
        return self.banks[n % len(self.banks)]

    def take(self, engine, name):
        n = self.number[name]
        assert n == self.taken, (name, n, self.taken)
        self.taken += 1
        return self.filled(engine, name)

    def drained(self, engine, name):
        engine.wait_ge(self.free, self.number[name] + 1)


def build(nc, x, wq, wk, wv, bias, k0, k1, k2, s0, s1, s2, aq, ak, av, ao, gate, experts, shared,
          rope_c, factor_c, table_c, out, xs, ys):
    with ExitStack() as ctx:
        def sb(name, shape, dt):
            return ctx.enter_context(nc.sbuf_tensor(name, shape, dt))

        def sem(name):
            return ctx.enter_context(nc.semaphore(name))

        banks = [ctx.enter_context(nc.psum_tensor(f"bank{i}", [P, 512], F32)) for i in range(8)]

        X = sb("X", [P, T, D], F32)
        W = sb("W", [P, 8, DC * D], F32R)
        XR = sb("XR", [P, 2 * DC * G * P], F32R)
        XT = XR[:, :].rearrange("p (a c n) -> p a c n", a=2, c=DC)
        RP = sb("RP", [P, 8192], F32R)
        FP = sb("FP", [P, 18432], F32)
        ident = sb("ident", [P, P], F32)
        identb = sb("identb", [P, P], BF16)
        maskb = sb("maskb", [P, 3 * P], BF16)
        rope = sb("rope", [P, T, 2, HD], F32)
        factor = sb("factor", [P, 2, DC], F32)
        scales = sb("scales", [P, 3], F32)
        ones = sb("ones", [1, P], F32R)
        kraw = sb("kraw", [P, DC, D], U8)
        epst = sb("epst", [P, 1], F32)
        st6 = sb("st6", [P, T, 6], F32)
        mv = sb("mv", [P, T, 2], F32)
        std = sb("std", [P, T], F32)
        rstd = sb("rstd", [P, T], F32)
        offset = sb("offset", [P, T], F32)
        small = sb("small", [P, 4, CH], F32)
        hmax = sb("hmax", [P, H], F32)
        before = sb("before", [P, P], BF16)
        onesb = sb("onesb", [P, P], BF16)
        picked = sb("picked", [P, T + 1, E], BF16)
        slots = sb("slots", [P, TOP, T], U32)
        owner = sb("owner", [1, NB + 1], I32)
        share = sb("share", [P, TOP, T], F32)
        hsum = sb("hsum", [P, 2, G * G], F32)

        biasf = FP[0:1, 16384:17920].rearrange("p (n d) -> p n d", n=3)
        biasr = RP[0:1, 0:3072].rearrange("p (a n d) -> p a n d", a=2, n=3)
        qkrow = FP[:, 0:4096].rearrange("p (h t r) -> p h t r", h=H, t=G)
        vrow = FP[:, 4096:6144].rearrange("p (d t h) -> p d t h", d=HD, t=G)
        cx = FP[:, 4096:6144].rearrange("p (s d) -> p s d", d=HD)
        qT = FP[:, 6144:10240].rearrange("p (s h) -> p s h", h=H)
        kT = FP[:, 10240:14336].rearrange("p (s h) -> p s h", h=H)
        vT = FP[:, 14336:16384].rearrange("p (s d) -> p s d", d=HD)
        sc = FP[:, 16384:17408].rearrange("p (b s t) -> p b s t", b=2, t=H)
        pT = FP[:, 17408:18432].rearrange("p (b s t) -> p b s t", b=2, t=H)
        raw_a = [FP[:, 6144:8192], FP[:, 10240:12288], FP[:, 14336:16384]]
        pair = [W[:, n:n + 2, :].rearrange("p a (c n) -> p a c n", c=DC) for n in (2, 4)]
        x1T = [XT, pair[1]]
        h1 = [RP[:, 0:4096].rearrange("p (a c n) -> p a c n", a=2, c=DC), pair[0]]
        h2 = x1T
        K = [W[:, 6, :].rearrange("p (c n) -> p c n", c=DC), W[:, 7, :].rearrange("p (c n) -> p c n", c=DC),
             RP[:, 4096:6144].rearrange("p (c n) -> p c n", c=DC)]
        hf = FP[:, 17408:18432].rearrange("p (b n) -> p b n", b=2)
        raw_c = [FP[:, a:a + DC * D] for a in (4096, 10752, 12800, 14848)]
        qsp = FP[:, 0:4096].rearrange("p (b h r) -> p b h r", b=2, r=KS)
        ksp = FP[:, 4096:6144].rearrange("p (h r) -> p h r", r=KS)
        qf = FP[:, 6144:6656]
        kf = FP[:, 6656:7168]
        rt = FP[:, 7168:7680]
        vaug = FP[:, 7680:10752].rearrange("p (s h r) -> p s h r", s=3, r=32)
        PT = FP[:, 10752:12800].rearrange("p (b w h q) -> p b w h q", b=2, w=2, h=G)
        cT = FP[:, 12800:13824]
        co = FP[:, 13824:14336]
        XT2 = XR[:, 0:2048].rearrange("p (b a c n) -> p b a c n", b=2, a=2, c=DC)
        qS = XR[:, 2048:4096].rearrange("p (a q) -> p a q", q=P)
        qM = RP[:, 0:2048].rearrange("p (a q) -> p a q", q=P)
        kS = RP[:, 2048:8192].rearrange("p (a s k) -> p a s k", s=3, k=P)
        wblock = [FP[:, c:c + WCOLS] for c in (14336, 14336 + WCOLS, 0, WCOLS, 8704, 8704 + WCOLS)]
        xblock = FP[:, 3072:5120].rearrange("p (b n) -> p b n", b=XBUFS)
        xbT = FP[:, 5120:6144].rearrange("p (b c n) -> p b c n", b=2, c=DC)
        yblock = FP[:, 6144:7680].rearrange("p (b n) -> p b n", b=YBUFS)
        sg = FP[:, 7680:8704].rearrange("p (b n) -> p b n", b=2)
        gathered = FP[:, 8704:14336].rearrange("p (b n) -> p b n", b=GBUFS)
        ac = FP[:, 17408:17920]
        diagonal = FP[:, WCOLS:WCOLS + TOP * G * P].rearrange("p (n q) -> p n q", q=P)
        ab = FP[:, 17920:18176].rearrange("p (b n) -> p b n", b=2)
        gates = FP[:, 17408:17472]
        table = FP[:, 17920:17920 + TABLE]
        rank, first, full, block_no = (table[:, a:b] for a, b in ((0, E), (E, E + E * E), (E + E * E, E + E * E + T),
                                                                 (E + E * E + T, TABLE)))
        lg, l2, tmp = (FP[:, 8704 + 128 * n:8832 + 128 * n].rearrange("p (t e) -> p t e", e=E) for n in range(3))
        oh, oslot = (FP[:, a:a + 256].rearrange("p (k t e) -> p k t e", k=TOP, e=E) for a in (9088, 9344))
        ranks = FP[:, 9600:9600 + (T + 1) * E].rearrange("p (t e) -> p t e", e=E)
        nblocks, base, ends = (FP[:, 9744 + E * n:9744 + E * (n + 1)] for n in range(3))
        over = FP[:, 9792:9920].rearrange("p (e k) -> p e k", k=T)
        firsts = FP[:, 9920:10176].rearrange("p (e f) -> p e f", f=E)
        passed = FP[0:1, 10176:10176 + NB * E].rearrange("p (b e) -> p b e", e=E)
        ownf = FP[0:1, 10688:10688 + NB]
        held = FP[:, 12288:14336].rearrange("p (j n) -> p j n", j=G)
        lgT = FP[0:E, 10816:10816 + T * P]
        slotf = FP[:, 10752:10768].rearrange("p (k t) -> p k t", k=TOP)
        tiny = FP[:, 18240:18280].rearrange("p (a t) -> p a t", t=T)
        XT3 = [RP[:, a:a + 4096].rearrange("p (a c n) -> p a c n", a=2, c=DC) for a in (4096, 0)]
        ah = XR[:, 0:2048].rearrange("p (b a n) -> p b a n", b=2, a=2)
        gr = XR[:, 2048:2048 + 2 * DC * E].rearrange("p (a c e) -> p a c e", a=2, c=DC)
        zeros = RP[:, 6144:8192].bitcast(F32)

        V = Ring(banks[0:2], sem("vbank_full"), sem("vbank_free"))
        A = Ring(banks[2:4], sem("abank_full"), sem("abank_free"))
        C = Ring(banks[4:6], sem("cbank_full"), sem("cbank_free"))
        S = Ring(banks[6:8], sem("sbank_full"), sem("sbank_free"))
        x_in = [sem(f"x_in{g}") for g in range(2)]
        wa_in = [sem(f"wa_in{n}") for n in range(3)]
        k_in = [sem(f"k_in{n}") for n in range(3)]
        wc_in = [sem(f"wc_in{n}") for n in range(4)]
        shared_in = [sem(f"shared_in{n}") for n in range(2)]
        wblock_in = [sem(f"wblock_in{n}") for n in range(WBUFS)]
        xblock_in = [sem(f"xblock_in{n}") for n in range(XBUFS)]
        yblock_out = [sem(f"yblock_out{n}") for n in range(YBUFS)]
        tile_gathered = [sem(f"tile_gathered{t}") for t in range(T)]
        zeros_ready = sem("zeros_ready")
        zeroed = sem("zeroed")
        picked_ready = sem("picked_ready")
        slots_ready = sem("slots_ready")
        owner_ready = sem("owner_ready")
        scattered = sem("scattered")
        xt_high = sem("xt_high")
        silu_done = sem("silu_done")
        diagonals_ready = sem("diagonals_ready")
        routed_added = sem("routed_added")
        combined = sem("combined")
        XBank = Ring(banks[0:1], sem("xtbank_full"), sem("xtbank_free"))
        YBank = Ring(banks[1:2], sem("ybank_full"), sem("ybank_free"))
        consts_in = sem("consts_in")
        bias_in = sem("bias_in")
        gate_in = sem("gate_in")
        out_done = sem("out_done")
        w_high = sem("w_high")
        w_split = sem("w_split")
        wo_split = sem("wo_split")
        k_ready = sem("k_ready")
        dve = sem("dve_step")
        act_step = sem("act_step")
        pool = sem("pool_step")
        small_ready = sem("small_ready")
        bias_ready = sem("bias_ready")
        ident_ready = sem("ident_ready")
        masks_ready = sem("masks_ready")
        pads_ready = sem("pads_ready")
        x_ready = sem("x_ready")
        stats_ready = sem("stats_ready")
        offset_ready = sem("offset_ready")
        x_out = sem("x_out")
        std_ready = sem("std_ready")
        expd = sem("expd")
        pt_ready = sem("pt_ready")
        h_ready = sem("h_ready")
        k_turned = sem("k_turned")
        q_turned = sem("q_turned")
        k_high = sem("k_high")
        q_high = sem("q_high")
        ksp_ready = sem("ksp_ready")
        qsp_ready = sem("qsp_ready")
        max_ready = sem("max_ready")
        pt_masked = sem("pt_masked")
        weighed = sem("weighed")
        ctx_ready = sem("ctx_ready")
        we_high = sem("we_high")
        we_split = sem("we_split")
        gate_ready = sem("gate_ready")
        logits_shifted = sem("logits_shifted")
        logits_exp = sem("logits_exp")
        act_ready = sem("act_ready")
        down_done = sem("down_done")
        acc_done = sem("acc_done")
        x_summed = sem("x_summed")

        def wsplit(n):
            return (W[:, 2 * n, :].rearrange("p (c n) -> p c n", c=DC), W[:, 2 * n + 1, :].rearrange("p (c n) -> p c n", c=DC))

        def window(i):
            cur, prev = i % 3, (i - 1) % 3
            if i == 0:
                return cur, 0
            if prev < cur:
                return slice(prev, cur + 1, cur - prev), P
            return slice(cur, prev + 1, prev - cur), 0

        def halves(e):
            return [(W[:, 2 * e + a, 0:DC * 2 * P].rearrange("p (c g n) -> p c g n", c=DC, g=2),
                     W[:, 2 * e + a, DC * 2 * P:WCOLS]) for a in range(2)]

        def last_fill(k):
            return ("up", k, 1 if ITEMS[k][0] == "shared" else 0)

        item_of = {item[1]: k for k, item in enumerate(ITEMS) if item[0] == "block"}

        block = ctx.enter_context(nc.Block())

        @block.sync
        def _(sp):
            xin = x.rearrange("(g t p) n -> g p t n", g=2, p=P)
            sp.dma_start(biasf, bias.rearrange("(a b) n -> a b n", a=1)).then_inc(bias_in, 16)
            sp.dma_start(X[:, 0:G, :], xin[0]).then_inc(x_in[0], 16)
            for n, w in ((0, wq), (2, wv), (1, wk)):
                sp.dma_start(raw_a[n].rearrange("p (c n) -> p c n", c=DC), w.rearrange("(c p) n -> p c n", p=P)).then_inc(wa_in[n], 16)
            sp.dma_start(rope[:, :, :, :], rope_c.rearrange("(t p) a d -> p t a d", p=P)).then_inc(consts_in, 16)
            sp.dma_start(factor[:, :, :], factor_c).then_inc(consts_in, 16)
            for n, s in enumerate((s0, s1, s2)):
                sp.dma_start(scales[:, n:n + 1], s.broadcast_to([P, 1])).then_inc(consts_in, 16)
            sp.dma_start(X[:, G:T, :], xin[1]).then_inc(x_in[1], 16)
            for n, k in enumerate((k0, k1, k2)):
                if n >= 1:
                    sp.wait_ge(k_ready, 1 + (n - 1) * DC)
                sp.dma_start(kraw[:, :, :], k.rearrange("(c p) n -> p c n", p=P)).then_inc(k_in[n], 16)
            sp.wait_ge(zeros_ready, 1)
            for b in range(0, NB, 4):
                n = min(4, NB - b)
                sp.dma_start(xs[b * P:(b + n) * P, :].rearrange("(b p) n -> p b n", p=P),
                             zeros.rearrange("p (b n) -> p b n", b=4)[:, 0:n, :]).then_inc(zeroed, 16)
            sp.wait_ge(x_ready, T)
            for n, w in enumerate((ak, av, aq, ao)):
                sp.dma_start(raw_c[n].rearrange("p (c n) -> p c n", c=DC), w.rearrange("(c p) n -> p c n", p=P)).then_inc(wc_in[n], 16)
            sp.wait_ge(w_split, 6)
            sp.wait_ge(wo_split, 1)
            for e in range(SE):
                if e >= 2:
                    sp.wait_ge(we_split, e - 1)
                sp.dma_start(wblock[e % 2], shared[e]).then_inc(shared_in[e % 2], 16)
                if e == 1:
                    sp.dma_start(gates.rearrange("p (c e) -> p c e", c=DC), gate.rearrange("(c p) e -> p c e", p=P)).then_inc(gate_in, 16)
                    sp.dma_start(table, table_c).then_inc(gate_in, 16)

            def load_weights(b):
                if b < 2:
                    sp.wait_ge(we_split, b + 3)
                if b >= WBUFS:
                    sp.wait_ge(down_done, item_of[b - WBUFS] + 1)
                e = nc.sync.value_load(owner[0:1, b:b + 1], min_val=0, max_val=E - 1)
                sp.dma_start(wblock[b % WBUFS], experts[bass.ds(e, 1), :, :].rearrange("a p n -> (a p) n")).then_inc(wblock_in[b % WBUFS], 16)

            def load_tokens(b):
                if b >= XBUFS:
                    sp.wait_ge(XBank.full, b - XBUFS + 1)
                sp.dma_start(xblock[:, b % XBUFS, :], xs[b * P:(b + 1) * P, :]).then_inc(xblock_in[b % XBUFS], 16)

            sp.wait_ge(owner_ready, 1)
            for b in range(WBUFS - 1):
                load_weights(b)
            sp.wait_ge(scattered, 16 * TOP * T)
            load_tokens(0)
            load_tokens(1)
            load_tokens(2)
            for b in range(NB):
                if b + 3 < NB:
                    load_tokens(b + 3)
                if b + WBUFS - 1 < NB:
                    load_weights(b + WBUFS - 1)
            for t in range(T):
                sp.wait_ge(x_out, t + 1)
                sp.dma_start(out[t * P:(t + 1) * P, :], X[:, t, :]).then_inc(out_done, 16)
            sp.wait_ge(out_done, 16 * T)

        @block.tensor
        def _(pe):
            def product(bank, terms):
                for n, (lhs, rhs) in enumerate(terms):
                    mm = nc.tensor.matmul(bank, lhs, rhs, start=(n == 0), stop=(n == len(terms) - 1))
                return mm

            def split_terms(lhs, rhs):
                return [t for lh, ll, rh, rl in zip(*lhs, *rhs) for t in ((lh, rh), (lh, rl), (ll, rh))]

            def transpose_row(name, src):
                b = V.fill(pe, name)
                for c in range(DC):
                    mm = nc.tensor.transpose(b[:, c * P:(c + 1) * P], src[:, c * P:(c + 1) * P], ident[:, :])
                mm.then_inc(V.full, 1)

            def tokens(j):
                return [[XT[:, a, c, j * P:(j + 1) * P] for c in range(DC)] for a in range(2)]

            def tokens2(b):
                return [[XT2[:, b, a, c, :] for c in range(DC)] for a in range(2)]

            def chunks(w):
                return [[m[:, c, :] for c in range(DC)] for m in w]

            pe.wait_ge(ident_ready, 2)
            for g in range(2):
                if g == 0:
                    pe.wait_ge(x_in[0], 16)
                    for j in range(G):
                        transpose_row(("x", j), X[:, j, :])
                    pe.wait_ge(bias_ready, 3)

                def project(n):
                    pe.wait_ge(w_split, 1 + (0, 2, 1).index(n))
                    for j in range(G):
                        V.drained(pe, ("x", g * G + j))
                        b = A.fill(pe, ("rows", g, n, j))
                        terms = [(ones[:, :], biasr[:, a, n, :]) for a in range(2)]
                        product(b[:, :], terms + split_terms(tokens(j), chunks(wsplit(n)))).then_inc(A.full, 1)

                def to_heads(ring, n, src, count):
                    A.drained(pe, ("rows", g, n, G - 1))
                    for a in range(count // 4):
                        b = ring.fill(pe, ("heads", g, n, a))
                        for m in range(4):
                            mm = nc.tensor.transpose(b[:, m * P:(m + 1) * P], src[:, 4 * a + m, :, :], ident[:, :])
                        mm.then_inc(ring.full, 1)

                project(0)
                project(2)
                to_heads(A, 0, qkrow, H)
                project(1)
                to_heads(V, 2, vrow, HD)
                to_heads(V, 1, qkrow, H)

                def scores(c):
                    b = C.fill(pe, ("scores", g, c))
                    for s in range(CH):
                        for j in range(G):
                            q = slice(32 * j, 32 * j + HD)
                            mm = nc.tensor.matmul(b[32 * j:32 * j + 32, s * H:(s + 1) * H], qT[q, c * CH + s, :],
                                                  kT[q, c * CH + s, :], start=True, stop=True)
                    mm.then_inc(C.full, 1)

                def values(c):
                    pe.wait_ge(pt_ready, g * NCH + c + 1)
                    b = S.fill(pe, ("values", g, c))
                    for s in range(CH):
                        for j in range(G):
                            q = slice(32 * j, 32 * j + 32)
                            mm = nc.tensor.matmul(b[q, s * HD:(s + 1) * HD], pT[q, c % 2, s, :],
                                                  vT[q, c * CH + s, :], start=True, stop=True)
                    mm.then_inc(S.full, 1)

                A.drained(pe, ("heads", g, 0, H // 4 - 1))
                V.drained(pe, ("heads", g, 1, H // 4 - 1))
                scores(0)
                scores(1)
                for c in range(NCH):
                    if c + 2 < NCH:
                        scores(c + 2)
                    if AHEAD <= c < AHEAD + G:
                        j = c - AHEAD
                        if g == 0:
                            pe.wait_ge(x_in[1], 16)
                            transpose_row(("x", G + j), X[:, G + j, :])
                        else:
                            pe.wait_ge(x_ready, j + 1)
                            transpose_row(("x1", j), X[:, j, :])
                    values(c)
                S.drained(pe, ("values", g, NCH - 1))
                for a in range(HD // 4):
                    b = V.fill(pe, ("context", g, a))
                    for m in range(4):
                        mm = nc.tensor.transpose(b[:, m * P:(m + 1) * P], cx[:, :, 4 * a + m], ident[:, :])
                    mm.then_inc(V.full, 1)

            def turn_x1(t):
                pe.wait_ge(x_ready, t + 1)
                transpose_row(("x1", t), X[:, t, :])

            def hidden(g, layer):
                src = (x1T, h1)[layer][g]
                pe.wait_ge(k_ready, 1 if layer == 0 else 1 + DC)
                if layer == 0:
                    V.drained(pe, ("x1", g * G + G - 1))
                else:
                    pe.wait_ge(h_ready, (2 * g + 1) * DC)
                for o in range(DC):
                    if (g, layer, o) == (0, 1, 2):
                        turn_x1(G + 2)
                        turn_x1(G + 3)
                    b = A.fill(pe, ("hidden", g, layer, o))
                    product(b[:, :], [(K[layer][:, c, o * P:(o + 1) * P], src[:, a, c, :]) for c in range(DC) for a in range(2)])\
                        .then_inc(A.full, 1)

            def last_layer(g):
                pe.wait_ge(h_ready, (2 * g + 2) * DC)
                pe.wait_ge(k_ready, 1 + 2 * DC)
                for j in range(G):
                    b = V.fill(pe, ("ffn", g * G + j))
                    product(b[:, :], [(h2[g][:, a, c, j * P:(j + 1) * P], K[2][:, c, :]) for c in range(DC) for a in range(2)])\
                        .then_inc(V.full, 1)

            hidden(0, 0)
            turn_x1(G)
            turn_x1(G + 1)
            hidden(0, 1)
            hidden(1, 0)
            last_layer(0)
            hidden(1, 1)
            pe.wait_ge(x_ready, T + 1)
            transpose_row(("x2", 0), X[:, 0, :])
            last_layer(1)

            def stack(name, src, which=range(4)):
                for a in which:
                    b = A.fill(pe, name + (a,))
                    for m in range(4):
                        pr = 2 * (4 * a + m)
                        mm = nc.tensor.transpose(b[:, m * P:(m + 1) * P], src[:, pr:pr + 2, :], ident[:, :])
                    mm.then_inc(A.full, 1)

            def half(hh):
                return slice(KS * hh, KS * hh + KS)

            def turn_x(i):
                pe.wait_ge(x_ready, T + i + 1)
                transpose_row(("x2", i), X[:, i, :])

            def project2(i, n, ring):
                V.drained(pe, ("x2", i))
                place = (1, 2, 0).index(n)
                pe.wait_ge(w_split, 4 + place)
                b = ring.fill(pe, ("qkv", i, n))
                product(b[:, :], split_terms(tokens2(0), chunks(wsplit(place)))).then_inc(ring.full, 1)

            def stack_keys(i, which):
                pe.wait_ge(ksp_ready, i + 1)
                stack(("kstack", i), ksp, which)

            def stack_queries(i, which):
                pe.wait_ge(qsp_ready, i + 1)
                stack(("qstack", i), qsp[:, i % 2], which)

            def context_rows(i, parts=(0, 1)):
                for a in parts:
                    pe.wait_ge(ctx_ready, 2 * i + a + 1)
                    b = V.fill(pe, ("context2", i, a))
                    for m in range(4):
                        mm = nc.tensor.transpose(b[:, m * P:(m + 1) * P], cT[:, (4 * a + m) * P:(4 * a + m + 1) * P], ident[:, :])
                    mm.then_inc(V.full, 1)

            def turn_context(i):
                V.drained(pe, ("context2", i, 1))
                transpose_row(("co", i), co)

            def output(i):
                V.drained(pe, ("co", i))
                pe.wait_ge(wo_split, 1)
                b = V.fill(pe, ("wo", i))
                product(b[:, :], split_terms(tokens2(1), chunks(wsplit(3)))).then_inc(V.full, 1)

            def row_scores(i, f):
                slots, m0 = window(i)
                n = P if i == 0 else 2 * P
                r = half(f % 2)
                b = V.fill(pe, ("rowscores", i, f))[:, :].rearrange("p (a k) -> p a k", a=2)[:, :, 0:n]
                nc.tensor.matmul(b, identb[:, :], maskb[:, m0:m0 + n].rearrange("p (a k) -> p a k", a=1).broadcast_to([P, 2, n]),
                                 start=True, stop=False)
                for m in range(2):
                    pr = 2 * (f // 2) + m
                    mm = nc.tensor.matmul(b[:, m, :], qS[r, pr, :], kS[r, pr, slots, :], start=False, stop=(m == 1))
                mm.then_inc(V.full, 1)

            def key_scores(i, hg):
                r = half(hg % 2)
                for w in range(1 if i == 0 else 2):
                    b = S.fill(pe, ("keyscores", i, hg, w))
                    for m in range(4):
                        pr = 4 * (hg // 2) + m
                        mm = nc.tensor.matmul(b[:, m * P:(m + 1) * P], kS[r, pr, (i - w) % 3, :], qM[r, pr, :],
                                              start=True, stop=True)
                    mm.then_inc(S.full, 1)

            def weigh(i, hg):
                pe.wait_ge(pt_masked, 8 * i + hg + 1)
                if hg == 0 and i >= 1:
                    pe.wait_ge(ctx_ready, 2 * i)
                nw = 1 if i == 0 else 2
                for m in range(4):
                    h = 8 * (hg // 2) + 2 * m + hg % 2
                    for w in range(nw):
                        mm = nc.tensor.matmul(C.banks[h // 16][32 * (h % 4):32 * (h % 4) + 32, (h // 4 % 4) * P:(h // 4 % 4 + 1) * P],
                                              vaug[:, (i - w) % 3, h, :], PT[:, hg % 2, w, m, :],
                                              start=(w == 0), stop=(w == nw - 1))
                mm.then_inc(weighed, 1)

            pe.wait_ge(pads_ready, 5)
            pe.wait_ge(masks_ready, 6)
            def between(i):
                last, following = i >= 1, i + 1 < T
                if 0 <= i and following:
                    turn_x(i + 1)
                if i >= 0:
                    pe.wait_ge(max_ready, i + 1)
                    stack(("qmstack", i), qsp[:, i % 2], (0, 1))
                for a in range(2):
                    if last:
                        context_rows(i - 1, (a,))
                    if i >= 0:
                        stack(("qmstack", i), qsp[:, i % 2], (2 + a,))
                if following:
                    project2(i + 1, 1, V)
                    project2(i + 1, 2, A)
                if last:
                    turn_context(i - 1)
                if following:
                    project2(i + 1, 0, V)
                    stack_keys(i + 1, (0, 1))
                if last:
                    output(i - 1)
                if following:
                    stack_keys(i + 1, (2, 3))
                    stack_queries(i + 1, (0, 1) if i >= 0 else range(4))

            between(-1)
            A.drained(pe, ("qstack", 0, 3))
            for f in range(H // 2):
                row_scores(0, f)
            for i in range(T):
                between(i)
                A.drained(pe, ("qmstack", i, 3))
                for hg in range(8):
                    key_scores(i, hg)
                    if i + 1 < T:
                        if hg == 0:
                            stack_queries(i + 1, (2, 3))
                        if hg in (0, 2):
                            A.drained(pe, ("qstack", i + 1, 1 + hg))
                        row_scores(i + 1, 2 * hg)
                        row_scores(i + 1, 2 * hg + 1)
                    if hg >= 1:
                        weigh(i, hg - 1)
                weigh(i, 7)
            def turn_x3(*tiles):
                for t in tiles:
                    pe.wait_ge(x_ready, 2 * T + t + 1)
                    transpose_row(("x3", t), X[:, t, :])

            context_rows(T - 1)
            turn_x3(0, 1)
            turn_context(T - 1)
            turn_x3(2, 3)
            output(T - 1)
            turn_x3(4, 5, 6)

            acc = banks[4:8]

            pe.wait_ge(gate_ready, 2)
            for g in range(2):
                if g == 1:
                    turn_x3(T - 1)
                V.drained(pe, ("x3", g * G + G - 1))
                x3 = [[XT3[g][:, a, c, :] for c in range(DC)] for a in range(2)]
                b = V.fill(pe, ("logitsT", g))
                product(b[0:E, :], split_terms([[gr[:, a, c, :] for c in range(DC)] for a in range(2)], x3)).then_inc(V.full, 1)
            V.drained(pe, ("logitsT", 1))
            b = V.fill(pe, "logits")
            for t in range(T):
                mm = nc.tensor.transpose(b[:, t * E:(t + 1) * E], lgT[:, t * P:(t + 1) * P], ident[0:E, 0:E])
            mm.then_inc(V.full, 1)

            def turn(b):
                pe.wait_ge(xblock_in[b % XBUFS], 16 * (b // XBUFS + 1))
                if b == 0:
                    V.drained(pe, "ranks")
                bank = XBank.fill(pe, ("xblock", b))
                for c in range(DC):
                    mm = nc.tensor.transpose(bank[:, c * P:(c + 1) * P], xblock[:, b % XBUFS, c * P:(c + 1) * P], ident[:, :])
                mm.then_inc(XBank.full, 1)

            def up(k):
                if ITEMS[k][0] == "shared":
                    _, g, e = ITEMS[k]
                    if g == 0:
                        pe.wait_ge(we_split, e + 1)
                    x3 = [[XT3[g][:, a, c, :] for c in range(DC)] for a in range(2)]
                    for part in range(2):
                        bank = A.fill(pe, ("up", k, part))
                        w = [[m[:, c, part, :] for c in range(DC)] for m, _ in halves(e)]
                        product(bank[:, :], split_terms(w, x3)).then_inc(A.full, 1)
                else:
                    b = ITEMS[k][1]
                    pe.wait_ge(wblock_in[b % WBUFS], 16 * (b // WBUFS + 1))
                    XBank.drained(pe, ("xblock", b))
                    bank = A.fill(pe, ("up", k, 0))
                    w = wblock[b % WBUFS][:, 0:DC * 2 * P].rearrange("p (c g n) -> p c g n", c=DC, g=2)
                    for part in range(2):
                        mm = product(bank[:, part * P:(part + 1) * P], [(w[:, c, part, :], xbT[:, b % 2, c, :]) for c in range(DC)])
                    mm.then_inc(A.full, 1)

            def down(k):
                if ITEMS[k][0] == "shared":
                    _, g, e = ITEMS[k]
                    pe.wait_ge(act_ready, g * SE + e + 1)
                    if g == 1 and e == 0:
                        pe.wait_ge(acc_done, G)
                    (_, dh), (_, dl) = halves(e)
                    hi, lo = (ah[:, k % 2, a, :] for a in range(2))
                    for j in range(G):
                        for n, (l, r) in enumerate(((hi, dh), (hi, dl), (lo, dh))):
                            mm = nc.tensor.matmul(acc[j][:, :], l[:, j * P:(j + 1) * P], r,
                                                  start=(e == 0 and n == 0), stop=(g == 0 and e == SE - 1 and n == 2))
                    mm.then_inc(down_done, 1)
                else:
                    b = ITEMS[k][1]
                    A.drained(pe, ("up", k, 0))
                    bank = YBank.fill(pe, ("yblock", b))
                    product(bank[:, :], [(ab[:, k % 2, :], wblock[b % WBUFS][:, DC * 2 * P:WCOLS])]).then_inc(down_done, 1)

            for k in range(len(ITEMS)):
                following = ITEMS[k + 1] if k + 1 < len(ITEMS) else None
                if following and following[0] == "block" and following[1] > 0:
                    turn(following[1])
                if k == LAST + 1:
                    down(k - 1)
                up(k)
                if k == 0:
                    pe.wait_ge(picked_ready, 2)
                    b = V.fill(pe, "ranks")[:, 0:(T + 1) * E]
                    nc.tensor.matmul(b, before[:, :], picked[:, :, :], start=True, stop=False)
                    for t in range(T):
                        nc.tensor.matmul(b[:, (t + 1) * E:(T + 1) * E], onesb[:, :], picked[:, t:t + 1, :].broadcast_to([P, T - t, E]),
                                         start=False, stop=False)
                    nc.tensor.matmul(b, onesb[:, :], picked[:, T:T + 1, :].broadcast_to([P, T + 1, E]), start=False, stop=True)\
                        .then_inc(V.full, 1)
                if k >= 1 and k != LAST + 1:
                    down(k - 1)
                if following == ("block", 0):
                    turn(0)
            down(len(ITEMS) - 1)
            for t in range(G, T):
                pe.wait_ge(tile_gathered[t], 16 * TOP)
                pe.wait_ge(diagonals_ready, TOP * G)
                for k in range(TOP):
                    mm = nc.tensor.matmul(acc[t - G][:, :], diagonal[:, TOP * (t - G) + k, :], gathered[:, (TOP * t + k) % GBUFS, :],
                                          start=False, stop=(k == TOP - 1))
                mm.then_inc(routed_added, 1)

        @block.vector
        def _(v):
            steps = [0]

            def own(ins):
                ins.then_inc(dve, 1)
                steps[0] += 1
                v.wait_ge(dve, steps[0])

            def tt(o, a, b, op):
                return nc.vector.tensor_tensor(o, a, b, op)

            def tile_parts(j):
                return [XT[:, a, :, j * P:(j + 1) * P] for a in range(2)]

            def split_xt(name, parts):
                b = V.take(v, name)[:, :].rearrange("p (c n) -> p c n", c=DC)
                hi, lo = parts
                own(nc.vector.tensor_copy(hi, b))
                tt(lo, b, hi.bitcast(F32), ALU.subtract).then_inc(V.free, 1)

            highs = [0]

            def low_xt(name, parts):
                b = V.take(v, name)[:, :].rearrange("p (c n) -> p c n", c=DC)
                hi, lo = parts
                highs[0] += 1
                v.wait_ge(xt_high, highs[0])
                tt(lo, b, hi.bitcast(F32), ALU.subtract).then_inc(V.free, 1)

            def stats(t):
                own(nc.vector.bn_stats(st6[:, t, :], X[:, t, :]))
                return nc.vector.bn_aggr(mv[:, t, :], st6[:, t, :])

            def normalise(tiles, batch):
                v.wait_ge(std_ready, batch + 1)
                own(nc.vector.reciprocal(rstd[:, tiles], std[:, tiles]))
                for t in range(tiles.start, tiles.stop):
                    nc.vector.tensor_scalar(X[:, t, :], X[:, t, :], mv[:, t, 0:1], rstd[:, t:t + 1],
                                            ALU.subtract, ALU.mult).then_inc(x_ready, 1)

            def low_part(n, slot, raw):
                v.wait_ge(w_high, n + 1)
                tt(W[:, 2 * slot + 1, :], raw, W[:, 2 * slot, :].bitcast(F32), ALU.subtract).then_inc(w_split, 1)

            nc.vector.memset(epst[:, :], EPS).then_inc(small_ready, 1)
            v.wait_ge(bias_ready, 1)
            tt(biasr[:, 1, :, :], biasf, biasr[:, 0, :, :].bitcast(F32), ALU.subtract).then_inc(bias_ready, 1)
            nc.vector.memset(ones[:, :].bitcast(F32), 1.0).then_inc(bias_ready, 1)

            for g in range(2):
                if g == 0:
                    for j in range(G):
                        low_xt(("x", j), tile_parts(j))
                    for n, m in enumerate((0, 2, 1)):
                        low_part(n, m, raw_a[m])
                    v.wait_ge(k_in[0], 16)
                    nc.vector.tensor_scalar(K[0][:, :, :], kraw[:, :, :], 2.0, -1.0, ALU.mult, ALU.add).then_inc(k_ready, 1)
                    v.wait_ge(consts_in, CONSTS)
                    for n in (1, 2):
                        v.wait_ge(k_in[n], 16)
                        for c in range(DC):
                            nc.vector.tensor_scalar(K[n][:, c, :], kraw[:, c, :], factor[:, 0, c:c + 1], factor[:, 1, c:c + 1],
                                                    ALU.mult, ALU.subtract).then_inc(k_ready, 1)
                for n, dst, count in ((2, vT, HD), (1, kT, H)):
                    for a in range(count // 4):
                        b = V.take(v, ("heads", g, n, a))
                        nc.vector.tensor_copy(dst[:, :, 4 * a:4 * a + 4].rearrange("p s h -> p h s"),
                                              b[:, :].rearrange("p (h s) -> p h s", h=4)).then_inc(V.free, 1)

                def shift(c):
                    if c >= 1:
                        C.drained(v, ("scores", g, c - 1))
                    b = C.take(v, ("scores", g, c))[:, :].rearrange("p (s t) -> p s t", t=H)
                    own(nc.vector.tensor_reduce(small[:, 0, :], b, AX, ALU.max))
                    tt(sc[:, c % 2], b, small[:, 0, :].rearrange("p (s a) -> p s a", a=1).broadcast_to([P, CH, H]), ALU.subtract)\
                        .then_inc(C.free, 1)

                def weights(c):
                    v.wait_ge(expd, g * NCH + c + 1)
                    own(nc.vector.tensor_reduce(small[:, 1, :], sc[:, c % 2], AX, ALU.add))
                    if c >= 2:
                        S.drained(v, ("values", g, c - 2))
                    own(nc.vector.reciprocal(small[:, 2 + c % 2, :], small[:, 1, :]))
                    nc.vector.transpose(pT[:, c % 2], sc[:, c % 2]).then_inc(pt_ready, 1)

                def contexts(c):
                    b = S.take(v, ("values", g, c))[:, 0:CH * HD].rearrange("p (s d) -> p s d", d=HD)
                    tt(cx[:, c * CH:(c + 1) * CH, :], b,
                       small[:, 2 + c % 2, :].rearrange("p (s a) -> p s a", a=1).broadcast_to([P, CH, HD]), ALU.mult).then_inc(S.free, 1)

                shift(0)
                for c in range(NCH):
                    if c + 1 < NCH:
                        shift(c + 1)
                    weights(c)
                    if c >= 1:
                        contexts(c - 1)
                    if AHEAD <= c < AHEAD + G:
                        j = c - AHEAD
                        split_xt(("x", G + j) if g == 0 else ("x1", j), tile_parts(j))
                contexts(NCH - 1)
                tiles = slice(g * G, g * G + G)
                for a in range(HD // 4):
                    b = V.take(v, ("context", g, a))[:, :].rearrange("p (m j h) -> p j h m", m=4, j=G)
                    for j in range(G):
                        xv = X[:, g * G + j, :].rearrange("p (h d) -> p h d", d=HD)[:, :, 4 * a:4 * a + 4]
                        ins = tt(xv, xv, b[:, j], ALU.add)
                        if j < G - 1:
                            ins.then_inc(dve, 1)
                            steps[0] += 1
                    ins.then_inc(V.free, 1)
                V.drained(v, ("context", g, HD // 4 - 1))
                for t in range(tiles.start, tiles.stop):
                    ins = stats(t)
                    if t < tiles.stop - 1:
                        ins.then_inc(dve, 1)
                        steps[0] += 1
                ins.then_inc(stats_ready, 1)
                normalise(tiles, g)

            def hidden_low(g, layer):
                dst = (h1, h2)[layer][g]
                for o in range(DC):
                    if (g, layer, o) == (0, 1, 2):
                        split_x1(2)
                        split_x1(3)
                    A.drained(v, ("hidden", g, layer, o))
                    tt(dst[:, 1, o, :], hf[:, o % 2, :], dst[:, 0, o, :].bitcast(F32), ALU.subtract).then_inc(h_ready, 1)

            def split_x1(j):
                split_xt(("x1", G + j), [x1T[1][:, a, :, j * P:(j + 1) * P] for a in range(2)])

            def ffn_out(g):
                for j in range(G):
                    t = g * G + j
                    b = V.take(v, ("ffn", t))
                    nc.vector.scalar_tensor_tensor(X[:, t, :], b[:, :], scales[:, 2:3], X[:, t, :], ALU.mult, ALU.add)\
                        .then_inc(V.free, 1)
                    V.drained(v, ("ffn", t))
                    ins = stats(t)
                    if j < G - 1:
                        ins.then_inc(dve, 1)
                        steps[0] += 1
                ins.then_inc(stats_ready, 1)
                normalise(slice(g * G, g * G + G), 2 + g)

            hidden_low(0, 0)
            split_x1(0)
            split_x1(1)
            hidden_low(0, 1)
            low_part(3, 0, raw_c[0])
            hidden_low(1, 0)
            ffn_out(0)
            hidden_low(1, 1)
            split_xt(("x2", 0), [XT2[:, 0, a] for a in range(2)])
            low_part(4, 1, raw_c[1])
            ffn_out(1)
            low_part(5, 2, raw_c[2])

            def rotate(i, n, dst, done):
                name = ("qkv", i, n)
                b = V.take(v, name)[:, :].rearrange("p (h d) -> p h d", d=HD)
                o = dst.rearrange("p (h d) -> p h d", d=HD)
                r = rt.rearrange("p (h d) -> p h d", d=HD)
                cos, sin = (rope[:, i, a:a + 1, :].broadcast_to([P, H, HD]) for a in range(2))
                k = HD // 2
                if n == 0:
                    v.wait_ge(k_turned, i + 1)
                elif i >= 1:
                    v.wait_ge(q_turned, i)
                tt(r, b, cos, ALU.mult).then_inc(dve, 1)
                tt(o[:, :, 0:k], b[:, :, k:HD], sin[:, :, 0:k], ALU.mult).then_inc(dve, 1)
                steps[0] += 2
                tt(o[:, :, k:HD], b[:, :, 0:k], sin[:, :, k:HD], ALU.mult).then_inc(V.free, 1)
                V.drained(v, name)
                tt(dst, dst, rt, ALU.add).then_inc(done, 1)

            def keys_low(i):
                v.wait_ge(k_high, i + 1)
                tt(ksp[:, :, HD:2 * HD], kf.rearrange("p (h d) -> p h d", d=HD), ksp[:, :, 0:HD], ALU.subtract).then_inc(ksp_ready, 1)

            def queries_low(i):
                q = qsp[:, i % 2]
                nc.vector.memset(q[:, :, 3 * HD:3 * HD + 2], 0.0).then_inc(dve, 1)
                steps[0] += 1
                v.wait_ge(q_high, i + 1)
                tt(q[:, :, 2 * HD:3 * HD].bitcast(F32R), qf.rearrange("p (h d) -> p h d", d=HD), q[:, :, 0:HD], ALU.subtract)\
                    .then_inc(qsp_ready, 1)

            def context_out(i):
                v.wait_ge(weighed, 8 * (i + 1))
                for a in range(2):
                    nc.vector.tensor_copy(cT[:, a * 512:(a + 1) * 512], C.banks[a][:, :]).then_inc(ctx_ready, 1)

            def context_divided(i):
                for a in range(2):
                    b = V.take(v, ("context2", i, a))[:, :].rearrange("p (h r) -> p h r", r=32)
                    r = hsum[:, a, :].rearrange("p (h r) -> p h r", r=1)
                    own(nc.vector.reciprocal(r, b[:, :, HD:HD + 1]))
                    tt(co[:, a * 256:(a + 1) * 256].rearrange("p (h d) -> p h d", d=HD), b[:, :, 0:HD], r.broadcast_to([P, 16, HD]),
                       ALU.mult).then_inc(V.free, 1)

            def add_output(i):
                b = V.take(v, ("wo", i))
                tt(X[:, i, :], X[:, i, :], b[:, :], ALU.add).then_inc(V.free, 1)
                V.drained(v, ("wo", i))
                ins = stats(i)
                if i < T - 2:
                    ins.then_inc(dve, 1)
                    steps[0] += 1
                else:
                    ins.then_inc(stats_ready, 1)

            def between(i):
                last, following = i >= 1, i + 1 < T
                if last:
                    context_out(i - 1)
                if 0 <= i and following:
                    split_xt(("x2", i + 1), [XT2[:, 0, a] for a in range(2)])
                if last:
                    context_divided(i - 1)
                if following:
                    rotate(i + 1, 1, kf, k_turned)
                    keys_low(i + 1)
                if last:
                    split_xt(("co", i - 1), [XT2[:, 1, a] for a in range(2)])
                if following:
                    rotate(i + 1, 0, qf, q_turned)
                    queries_low(i + 1)
                if last:
                    add_output(i - 1)

            def row_maxima(i):
                n = P if i == 0 else 2 * P
                for f in range(H // 2):
                    b = V.take(v, ("rowscores", i, f))[:, :].rearrange("p (a k) -> p a k", a=2)[:, :, 0:n]
                    h = 4 * (f // 2) + f % 2
                    nc.vector.tensor_reduce(hmax[:, h:h + 3:2], b, AX, ALU.max).then_inc(V.free, 1)
                V.drained(v, ("rowscores", i, H // 2 - 1))
                m = hmax[:, :].rearrange("p (h a) -> p h a", a=1)
                q = qsp[:, i % 2]
                own(nc.vector.tensor_copy(q[:, :, 3 * HD:3 * HD + 1].bitcast(F32R), m))
                tt(q[:, :, 3 * HD + 1:3 * HD + 2], m, q[:, :, 3 * HD:3 * HD + 1], ALU.subtract).then_inc(max_ready, 1)

            def shared_low(e):
                v.wait_ge(we_high, e + 1)
                tt(W[:, 2 * e + 1, 0:WCOLS], wblock[e % 2], W[:, 2 * e, 0:WCOLS].bitcast(F32), ALU.subtract).then_inc(we_split, 1)

            between(-1)
            row_maxima(0)
            for i in range(T):
                between(i)
                if i + 1 < T:
                    row_maxima(i + 1)
            normalise(slice(0, T - 1), 4)
            for e in range(SE - 1):
                shared_low(e)

            def low_x3(*tiles):
                for t in tiles:
                    low_xt(("x3", t), [XT3[t // G][:, a, :, t % G * P:(t % G + 1) * P] for a in range(2)])

            v.wait_ge(gate_in, 32)
            gv = gates.rearrange("p (c e) -> p c e", c=DC)
            nc.vector.tensor_copy(gr[:, 0], gv).then_inc(gate_ready, 1)
            v.wait_ge(gate_ready, 1)
            tt(gr[:, 1], gv, gr[:, 0].bitcast(F32), ALU.subtract).then_inc(gate_ready, 1)
            nc.vector.memset(picked[:, T, :], 0.0).then_inc(picked_ready, 1)
            context_out(T - 1)
            context_divided(T - 1)
            low_x3(0, 1)
            split_xt(("co", T - 1), [XT2[:, 1, a] for a in range(2)])
            low_x3(2, 3)
            add_output(T - 1)
            low_x3(4, 5, 6)
            normalise(slice(T - 1, T), 5)

            for g in range(2):
                if g == 1:
                    low_x3(T - 1)
                b = V.take(v, ("logitsT", g))
                nc.vector.tensor_copy(lgT[:, g * D:(g + 1) * D], b[0:E, :]).then_inc(V.free, 1)

            def spread(vec, axis, shape):
                form = "p (a n) -> p a n" if axis == 1 else "p (n a) -> p n a"
                return vec.rearrange(form, a=1).broadcast_to(shape)

            b = V.take(v, "logits")
            nc.vector.tensor_copy(lg, b[:, 0:T * E].rearrange("p (t e) -> p t e", e=E)).then_inc(V.free, 1)
            V.drained(v, "logits")

            def best(src, one, mx):
                own(nc.vector.tensor_reduce(tiny[:, mx, :], src, AX, ALU.max))
                own(tt(tmp, src, spread(tiny[:, mx, :], 2, [P, T, E]), ALU.is_equal))
                own(tt(tmp, tmp, spread(rank, 1, [P, T, E]), ALU.mult))
                own(nc.vector.tensor_reduce(tiny[:, 2, :], tmp, AX, ALU.max))
                own(tt(one, tmp, spread(tiny[:, 2, :], 2, [P, T, E]), ALU.is_equal))

            best(lg, oh[:, 0], 0)
            own(nc.vector.scalar_tensor_tensor(l2, oh[:, 0], -BIG, lg, ALU.mult, ALU.add))
            best(l2, oh[:, 1], 1)
            tt(picked[:, 0:T, :], oh[:, 0], oh[:, 1], ALU.add).then_inc(picked_ready, 1)
            tt(tiny[:, 3, :], tiny[:, 1, :], tiny[:, 0, :], ALU.subtract).then_inc(logits_shifted, 1)
            def place():
                b = V.take(v, "ranks")
                nc.vector.tensor_copy(ranks, b[:, 0:(T + 1) * E].rearrange("p (t e) -> p t e", e=E)).then_inc(V.free, 1)
                V.drained(v, "ranks")
                own(tt(over, spread(ranks[:, T, :], 2, [P, E, T]), spread(full, 1, [P, E, T]), ALU.is_gt))
                own(nc.vector.tensor_reduce(nblocks, over, AX, ALU.add))
                own(tt(firsts, first.rearrange("p (e f) -> p e f", f=E), spread(nblocks, 1, [P, E, E]), ALU.mult))
                own(nc.vector.tensor_reduce(base, firsts, AX, ALU.add))
                own(nc.vector.scalar_tensor_tensor(ranks[:, 0:T, :], spread(base, 1, [P, T, E]), float(P), ranks[:, 0:T, :], ALU.mult, ALU.add))
                for k in range(TOP):
                    own(tt(oslot[:, k], oh[:, k], ranks[:, 0:T, :], ALU.mult))
                own(nc.vector.tensor_reduce(slotf, oslot, AX, ALU.add))
                nc.vector.tensor_copy(slots[:, :, :], slotf).then_inc(slots_ready, 1)
                own(tt(ends, base, nblocks, ALU.add))
                own(tt(passed, spread(ends[0:1, :], 1, [1, NB, E]), spread(block_no[0:1, :], 2, [1, NB, E]), ALU.is_le))
                own(nc.vector.tensor_reduce(ownf, passed, AX, ALU.add))
                nc.vector.tensor_scalar(owner[0:1, 0:NB], ownf, float(E - 1), None, ALU.min).then_inc(owner_ready, 1)
                v.wait_ge(logits_exp, 1)
                own(nc.vector.tensor_scalar(tiny[:, 4, :], tiny[:, 3, :], 1.0, None, ALU.add))
                own(nc.vector.reciprocal(share[:, 0, :], tiny[:, 4, :]))
                own(tt(share[:, 1, :], tiny[:, 3, :], share[:, 0, :], ALU.mult))

            def collect(tiles, sums):
                for t, total in zip(tiles, sums):
                    tt(X[:, t, :], X[:, t, :], total[:, :], ALU.add).then_inc(x_summed, 1)

            def combine(t):
                v.wait_ge(tile_gathered[t], 16 * TOP)
                for k in range(TOP):
                    nc.vector.scalar_tensor_tensor(X[:, t, :], gathered[:, (TOP * t + k) % GBUFS, :], share[:, k, t:t + 1], X[:, t, :],
                                                   ALU.mult, ALU.add).then_inc(combined, 1)
                    v.wait_ge(combined, TOP * t + k + 1)

            nshared = 0
            for k, item in enumerate(ITEMS):
                if item == ("shared", 0, SE - 2):
                    shared_low(SE - 1)
                if k + 1 < len(ITEMS) and ITEMS[k + 1][0] == "block":
                    b = ITEMS[k + 1][1]
                    bank = XBank.take(v, ("xblock", b))[:, :].rearrange("p (c n) -> p c n", c=DC)
                    if b >= 2:
                        A.filled(v, ("up", item_of[b - 2], 0))
                    nc.vector.tensor_copy(xbT[:, b % 2], bank).then_inc(XBank.free, 1)
                v.wait_ge(silu_done, k + 1)
                if item[0] == "shared":
                    bank = A.filled(v, ("up", k, 1))
                    if nshared >= 1:
                        v.wait_ge(act_ready, nshared)
                    nshared += 1
                    tt(ac, sg[:, k % 2, :], bank[:, :], ALU.mult).then_inc(A.free, 2)
                    A.drained(v, ("up", k, 1))
                    if k >= 2:
                        v.wait_ge(down_done, k - 1)
                    own(nc.vector.tensor_copy(ah[:, k % 2, 0, :], ac))
                    tt(ah[:, k % 2, 1, :], ac, ah[:, k % 2, 0, :].bitcast(F32), ALU.subtract).then_inc(act_ready, 1)
                else:
                    bank = A.filled(v, ("up", k, 0))
                    v.wait_ge(down_done, k - 1)
                    tt(ab[:, k % 2, :], sg[:, k % 2, 0:P], bank[:, P:2 * P], ALU.mult).then_inc(A.free, 1)
                if k == 0:
                    place()
                if item == ("block", 3):
                    v.wait_ge(scattered, 16 * TOP * T)
                    v.wait_ge(acc_done, G)
                    collect(range(G), [held[:, j, :] for j in range(G)])
                    v.wait_ge(x_summed, G)
                if k == LAST:
                    v.wait_ge(down_done, item_of[NB - 4] + 1)
                    for n in range(TOP * G):
                        t = G + n // TOP
                        nc.vector.tensor_scalar(diagonal[:, n, :], ident[:, :], share[:, n % TOP, t:t + 1], None, ALU.mult)\
                            .then_inc(diagonals_ready, 1)
                if k == len(ITEMS) - 2:
                    combine(0)
                    combine(1)
                    combine(2)
                elif k == len(ITEMS) - 1:
                    combine(3)

            def last_stats(tiles, batch):
                for t in tiles:
                    ins = stats(t)
                    if t < tiles[-1]:
                        ins.then_inc(dve, 1)
                        steps[0] += 1
                ins.then_inc(stats_ready, 1)
                v.wait_ge(std_ready, batch + 1)
                q = slice(tiles[0], tiles[-1] + 1)
                own(nc.vector.reciprocal(rstd[:, q], std[:, q]))
                nc.vector.scalar_tensor_tensor(offset[:, q], mv[:, q, 0], -1.0, rstd[:, q], ALU.mult, ALU.mult).then_inc(offset_ready, 1)

            last_stats(range(0, G), 6)
            for a in range(G, T, 2):
                for t in (a, a + 1):
                    v.wait_ge(routed_added, t - G + 1)
                    collect([t], [banks[4 + t - G]])
                v.wait_ge(x_summed, a + 2)
                last_stats(range(a, a + 2), 7 + (a - G) // 2)

        @block.scalar
        def _(s):
            steps = [0]

            def act(o, i, func, **kw):
                return nc.scalar.activation(o, i, func, **kw)

            def high_part(n, slot, raw, arrived):
                s.wait_ge(arrived, 16)
                act(W[:, 2 * slot, :], raw, ACT.Copy).then_inc(w_high, 1)

            def roots(tiles, batch):
                s.wait_ge(stats_ready, batch + 1)
                act(std[:, tiles], mv[:, tiles, 1], ACT.Sqrt, bias=epst[:, 0:1]).then_inc(std_ready, 1)

            def high_xt(name, hi):
                b = V.filled(s, name)[:, :].rearrange("p (c n) -> p c n", c=DC)
                act(hi, b, ACT.Copy).then_inc(xt_high, 1)

            s.wait_ge(bias_in, 16)
            act(biasr[:, 0, :, :], biasf, ACT.Copy).then_inc(bias_ready, 1)
            for j in range(G):
                high_xt(("x", j), XT[:, 0, :, j * P:(j + 1) * P])
            for n, m in enumerate((0, 2, 1)):
                high_part(n, m, raw_a[m], wa_in[m])
            s.wait_ge(small_ready, 1)
            for g in range(2):
                def rows_out(n):
                    for j in range(G):
                        b = A.take(s, ("rows", g, n, j))
                        if n == 2:
                            act(vrow[:, :, j, :], b[:, :].rearrange("p (h d) -> p d h", d=HD), ACT.Copy).then_inc(A.free, 1)
                        else:
                            act(qkrow[:, :, j, 0:HD], b[:, :].rearrange("p (h d) -> p h d", d=HD), ACT.Copy).then_inc(A.free, 1)

                if g == 0:
                    s.wait_ge(pads_ready, 1)
                rows_out(0)
                if g == 1:
                    V.drained(s, ("context", 0, HD // 4 - 1))
                rows_out(2)
                s.wait_ge(w_split, 3)
                for a in range(H // 4):
                    b = A.take(s, ("heads", g, 0, a))
                    act(qT[:, :, 4 * a:4 * a + 4].rearrange("p s h -> p h s"), b[:, :].rearrange("p (h s) -> p h s", h=4),
                        ACT.Copy).then_inc(A.free, 1)
                rows_out(1)
                for c in range(NCH):
                    C.drained(s, ("scores", g, c))
                    act(sc[:, c % 2], sc[:, c % 2], ACT.Exp, scale=SCALE).then_inc(expd, 1)
                roots(slice(g * G, g * G + G), g)

            def hidden_out(g, layer):
                dst = (h1, h2)[layer][g]
                for o in range(DC):
                    n = (2 * g + layer) * DC + o
                    b = A.take(s, ("hidden", g, layer, o))
                    if n >= 2:
                        s.wait_ge(h_ready, n - 1)
                    act(dst[:, 0, o, :], b[:, :], ACT.Relu, scale=scales[:, layer:layer + 1]).then_inc(act_step, 1)
                    act(hf[:, o % 2, :], b[:, :], ACT.Relu, scale=scales[:, layer:layer + 1]).then_inc(A.free, 1)

            hidden_out(0, 0)
            hidden_out(0, 1)
            high_part(3, 0, raw_c[0], wc_in[0])
            hidden_out(1, 0)
            roots(slice(0, G), 2)
            hidden_out(1, 1)
            high_part(4, 1, raw_c[1], wc_in[1])
            roots(slice(G, T), 3)
            V.drained(s, ("ffn", T - 1))
            high_part(5, 2, raw_c[2], wc_in[2])
            high_part(6, 3, raw_c[3], wc_in[3])

            def queries_out(i, a):
                b = A.take(s, ("qstack", i, a))
                act(qS[:, 4 * a:4 * a + 4, :], b[:, :].rearrange("p (m k) -> p m k", m=4), ACT.Copy).then_inc(A.free, 1)

            def between(i):
                if i >= 0:
                    for a in range(4):
                        b = A.take(s, ("qmstack", i, a))
                        act(qM[:, 4 * a:4 * a + 4, :], b[:, :].rearrange("p (m k) -> p m k", m=4), ACT.Copy).then_inc(A.free, 1)
                if i + 1 == T:
                    return
                n = i + 1
                q = qsp[:, n % 2].rearrange("p h (a r) -> p h a r", r=HD)
                k = ksp.rearrange("p h (a r) -> p h a r", r=HD)
                s.wait_ge(k_turned, n + 1)
                act(k[:, :, 0:3:2, :].bitcast(F32R), kf.rearrange("p (h a r) -> p h a r", a=1, r=HD).broadcast_to([P, H, 2, HD]), ACT.Copy)\
                    .then_inc(k_high, 1)
                b = A.take(s, ("qkv", n, 2))
                act(vaug[:, n % 3, :, 0:HD], b[:, :].rearrange("p (h d) -> p h d", d=HD), ACT.Copy).then_inc(A.free, 1)
                for a in range(4):
                    if a == 2:
                        s.wait_ge(q_turned, n + 1)
                        act(q[:, :, 0:2, :].bitcast(F32R), qf.rearrange("p (h a r) -> p h a r", a=1, r=HD).broadcast_to([P, H, 2, HD]),
                            ACT.Copy).then_inc(q_high, 1)
                    b = A.take(s, ("kstack", n, a))
                    act(kS[:, 4 * a:4 * a + 4, n % 3, :], b[:, :].rearrange("p (m k) -> p m k", m=4), ACT.Copy).then_inc(A.free, 1)
                for a in range(4):
                    queries_out(n, a)

            def shared_high(e):
                s.wait_ge(shared_in[e % 2], 16 * (e // 2 + 1))
                act(W[:, 2 * e, 0:WCOLS], wblock[e % 2], ACT.Copy).then_inc(we_high, 1)

            s.wait_ge(pads_ready, 5)
            s.wait_ge(zeroed, 16 * ((NB + 3) // 4))
            between(-1)
            for i in range(T):
                between(i)
                if i == T - 1:
                    roots(slice(0, T - 1), 4)
                for hg in range(8):
                    n = 8 * i + hg
                    if n >= 2:
                        s.wait_ge(weighed, n - 1)
                    for w in range(1 if i == 0 else 2):
                        b = S.take(s, ("keyscores", i, hg, w))
                        act(PT[:, hg % 2, w], b[:, :].rearrange("p (m q) -> p m q", m=4), ACT.Exp, scale=SCALE).then_inc(S.free, 1)
                    if i == T - 1 and hg % 2 == 1 and hg // 2 < SE - 1:
                        shared_high(hg // 2)
            for t in range(G):
                high_xt(("x3", t), XT3[0][:, 0, :, t * P:(t + 1) * P])
            roots(slice(T - 1, T), 5)
            for t in range(G, T):
                high_xt(("x3", t), XT3[1][:, 0, :, t % G * P:(t % G + 1) * P])

            V.drained(s, ("wo", T - 1))
            shared_high(SE - 1)
            s.wait_ge(logits_shifted, 1)
            act(tiny[:, 3, :], tiny[:, 3, :], ACT.Exp).then_inc(logits_exp, 1)
            def block_out(k):
                b = ITEMS[k][1]
                s.wait_ge(down_done, k + 1)
                if b >= YBUFS:
                    s.wait_ge(yblock_out[b % YBUFS], 16 * (b // YBUFS))
                act(yblock[:, b % YBUFS, :], YBank.banks[0][:, :], ACT.Copy).then_inc(YBank.free, 1)

            for k, item in enumerate(ITEMS):
                if k == LAST + 1:
                    block_out(LAST)
                bank = A.filled(s, ("up", k, 0))
                n = D if item[0] == "shared" else P
                if k >= 2:
                    A.drained(s, last_fill(k - 2))
                act(sg[:, k % 2, 0:n], bank[:, 0:n], ACT.Silu).then_inc(silu_done, 1)
                if k == SE:
                    s.wait_ge(down_done, SE)
                    for j in range(G):
                        act(held[:, j, :], banks[4 + j][:, :], ACT.Copy).then_inc(acc_done, 1)
                if k >= 1 and k != LAST + 1 and ITEMS[k - 1][0] == "block":
                    block_out(k - 1)
            for n, (a, b) in enumerate(((0, G), (G, G + 2), (G + 2, T))):
                roots(slice(a, b), 6 + n)
                s.wait_ge(offset_ready, n + 1)
                for t in range(a, b):
                    act(X[:, t, :], X[:, t, :], ACT.Identity, scale=rstd[:, t:t + 1], bias=offset[:, t:t + 1]).then_inc(x_out, 1)

        @block.gpsimd
        def _(p):
            nc.gpsimd.memset(ident[:, :], 0.0).then_inc(ident_ready, 1)
            p.wait_ge(ident_ready, 1)
            nc.gpsimd.affine_select(out=ident[:, :], in_=ident[:, :], compare_op=ALU.not_equal, fill=1.0, base=0,
                                    pattern=[[-1, P]], channel_multiplier=1).then_inc(ident_ready, 1)
            nc.gpsimd.memset(qkrow[:, :, :, HD:2 * HD], 0.0).then_inc(pads_ready, 1)
            nc.gpsimd.memset(zeros, 0.0).then_inc(zeros_ready, 1)
            nc.gpsimd.memset(maskb[:, :], 0.0).then_inc(masks_ready, 1)
            nc.gpsimd.memset(identb[:, :], 0.0).then_inc(masks_ready, 1)
            p.wait_ge(masks_ready, 2)
            nc.gpsimd.affine_select(out=identb[:, :], in_=identb[:, :], compare_op=ALU.not_equal, fill=1.0, base=0,
                                    pattern=[[-1, P]], channel_multiplier=1).then_inc(masks_ready, 1)
            for k, (base, step) in enumerate(((0, -1), (-1, 1), (0, -1))):
                m = maskb[:, k * P:(k + 1) * P]
                nc.gpsimd.affine_select(out=m, in_=m, compare_op=ALU.is_ge, fill=-BIG, base=base,
                                        pattern=[[step, P]], channel_multiplier=-step).then_inc(masks_ready, 1)
            nc.gpsimd.memset(onesb[:, :], 1.0).then_inc(pool, 1)
            p.wait_ge(pool, 1)
            nc.gpsimd.affine_select(out=before[:, :], in_=onesb[:, :], compare_op=ALU.is_ge, fill=0.0, base=-1,
                                    pattern=[[1, P]], channel_multiplier=-1).then_inc(pool, 1)
            p.wait_ge(w_split, 4)
            nc.gpsimd.memset(qsp[:, :, :, 3 * HD:KS], 0.0).then_inc(pads_ready, 1)
            nc.gpsimd.memset(ksp[:, :, 3 * HD:3 * HD + 2], -1.0).then_inc(pads_ready, 1)
            nc.gpsimd.memset(ksp[:, :, 3 * HD + 2:KS], 0.0).then_inc(pads_ready, 1)
            nc.gpsimd.memset(vaug[:, :, :, HD + 1:32], 0.0).then_inc(pool, 1)
            nc.gpsimd.memset(vaug[:, :, :, HD:HD + 1], 1.0).then_inc(pads_ready, 1)
            p.wait_ge(w_high, 7)
            nc.gpsimd.tensor_tensor(W[:, 7, :], raw_c[3], W[:, 6, :].bitcast(F32), ALU.subtract).then_inc(wo_split, 1)
            for i in range(T):
                for hg in range(8):
                    nw = 1 if i == 0 else 2
                    for w in range(nw):
                        S.drained(p, ("keyscores", i, hg, w))
                        pt = PT[:, hg % 2, w]
                        if w == 0:
                            ins = nc.gpsimd.affine_select(out=pt, in_=pt, compare_op=ALU.is_ge, fill=0.0, base=0,
                                                          pattern=[[0, 4], [1, P]], channel_multiplier=-1)
                        else:
                            ins = nc.gpsimd.affine_select(out=pt, in_=pt, compare_op=ALU.is_ge, fill=0.0, base=-1,
                                                          pattern=[[0, 4], [-1, P]], channel_multiplier=1)
                        ins.then_inc(pt_masked if w == nw - 1 else pool, 1)
            p.wait_ge(zeroed, 16 * ((NB + 3) // 4))
            p.wait_ge(slots_ready, 1)
            for t in range(T):
                for k in range(TOP):
                    nc.gpsimd.indirect_dma_start(xs, bass.IndirectOffsetOnAxis(slots[:, k, t:t + 1], 0), X[:, t, :], None).then_inc(scattered, 16)
            for b in range(NB):
                YBank.drained(p, ("yblock", b))
                nc.gpsimd.dma_start(ys[b * P:(b + 1) * P, :], yblock[:, b % YBUFS, :]).then_inc(yblock_out[b % YBUFS], 16)
            for r in range(YBUFS):
                p.wait_ge(yblock_out[r], 16 * len(range(r, NB, YBUFS)))
            for t in range(T):
                if TOP * t + TOP > GBUFS:
                    p.wait_ge(combined, TOP * t + TOP - GBUFS)
                for k in range(TOP):
                    nc.gpsimd.indirect_dma_start(gathered[:, (TOP * t + k) % GBUFS, :], None, ys,
                                                 bass.IndirectOffsetOnAxis(slots[:, k, t:t + 1], 0)).then_inc(tile_gathered[t], 16)


def _constants(np):
    inv = (1.0 / np.power(np.float32(10000.0), np.arange(0, HD, 2, dtype=np.float32) / np.float32(HD))).astype(np.float32)
    freqs = np.arange(T * P, dtype=np.float32)[:, None] * inv[None, :]
    cos, sin = np.cos(freqs), np.sin(freqs)
    f = np.where(np.arange(D) < round(D * 0.8), 2.0, 2.0 * -0.8 / (1.0 - 0.8)).astype(np.float32).reshape(DC, P).T
    e = np.arange(E)
    table = np.concatenate([E - e, (e[None, :] < e[:, None]).reshape(-1), P * np.arange(T), np.arange(NB)])
    tables = {
        "rope": np.stack([np.concatenate([cos, cos], 1), np.concatenate([-sin, sin], 1)], 1),
        "factor": np.stack([2 * f, f], 1),
        "table": np.broadcast_to(table, (P, TABLE)),
    }
    return {k: np.ascontiguousarray(t, dtype=np.float32) for k, t in tables.items()}


def kernel(**inputs):
    import numpy as np
    import concourse.bacc as _bacc
    from concourse import mybir as _mybir
    from concourse.bass_utils import run_bass_kernel_spmd as _run

    def by_partition(gate_up, down):
        n = gate_up.shape[0]
        gu = gate_up.reshape(n, 2, P, DC, P).transpose(0, 4, 3, 1, 2).reshape(n, P, DC * 2 * P)
        return np.concatenate([gu, down.transpose(0, 2, 1)], axis=2)

    a = {k: np.asarray(v) for k, v in inputs.items()}
    lay = {
        "x": a["L0_attn_hidden_states"][0],
        "wq": a["L0_attn_wq"].T, "wk": a["L0_attn_wk"].T, "wv": a["L0_attn_wv"].T,
        "bias": np.stack([a["L0_attn_bq"], a["L0_attn_bk"], a["L0_attn_bv"]]),
        "k0": a["L0_ffn_k0"], "k1": a["L0_ffn_k1"], "k2": a["L0_ffn_k2"],
        "s0": a["L0_ffn_s0"].reshape(1, 1), "s1": a["L0_ffn_s1"].reshape(1, 1), "s2": a["L0_ffn_s2"].reshape(1, 1),
        "aq": a["L1_attn_Wq"].T, "ak": a["L1_attn_Wk"].T, "av": a["L1_attn_Wv"].T, "ao": a["L1_attn_Wo"].T,
        "gate": a["L1_ffn_gate_w"].T,
        "experts": by_partition(a["L1_ffn_w_gate_up"].reshape(E, 2, P, D), a["L1_ffn_w_down"]),
        "shared": by_partition(a["L1_ffn_shared_w_gate_up"].reshape(2, SE, P, D).transpose(1, 0, 2, 3),
                               a["L1_ffn_shared_w_down"].reshape(D, SE, P).transpose(1, 0, 2)),
    }
    nc = _bacc.Bacc("TRN2", target_bir_lowering=False, num_devices=1)
    arrays, args = {}, []
    for name, array in [*lay.items(), *_constants(np).items()]:
        array = np.ascontiguousarray(array)
        arrays[f"in_{name}_dram"] = array
        args.append(nc.dram_tensor(f"in_{name}_dram", array.shape, _mybir.dt.from_np(array.dtype), kind="ExternalInput").ap())
    args.append(nc.dram_tensor("out_0_dram", (T * P, D), _mybir.dt.from_np(np.dtype("float32")), kind="ExternalOutput").ap())
    for name in ("slots_in", "slots_out"):
        args.append(nc.dram_tensor(name, (NB * P, D), _mybir.dt.from_np(np.dtype("float32")), kind="Internal").ap())
    build(nc, *args)
    r = _run(nc, [arrays], core_ids=[0])
    return r.results[0]["out_0_dram"].reshape(1, T * P, D)
```
